# Optimizing a Trainium2 kernel written in Bass

```python
import numpy as np
import jax
import jax.numpy as jnp

def _softmax(x, axis=-1):
    return jax.nn.softmax(x, axis=axis)

def _gelu(x):
    return jax.nn.gelu(x, approximate=True)

def _silu(x):
    return jax.nn.silu(x)

def _sigmoid(x):
    return jax.nn.sigmoid(x)

def _layernorm(x, axis=-1, eps=1e-05):
    m = jnp.mean(x, axis=axis, keepdims=True)
    v = jnp.var(x, axis=axis, keepdims=True)
    return (x - m) / jnp.sqrt(v + eps)

def _scatter_add(tgt, idx, src, axis=0):
    return tgt.at[idx].add(src)

def _segment_sum(src, seg, n):
    return jax.ops.segment_sum(src, seg, n)
kernel_name = 'mk_gnn_ffn_d1_gnn_r8_331f6f'

def setup_inputs(seed: int=0):
    np.random.seed(seed)
    _w = jnp.asarray

    def _rec_inputs():
        import jax
        import jax.numpy as jnp
        _gk = jax.random.key(seed)
        x = -8.776e-05 + 1 * jax.random.normal(jax.random.fold_in(_gk, 1), (1250, 512), jnp.float32)
        _s = jax.random.randint(jax.random.fold_in(_gk, 2), (10000,), 0, 1250, jnp.int32)
        _d = jax.random.randint(jax.random.fold_in(_gk, 3), (10000,), 0, 1250, jnp.int32)
        _loop = jnp.arange(1250, dtype=jnp.int32)
        src = jnp.concatenate([_s, _d, _loop])
        dst = jnp.concatenate([_d, _s, _loop])
        _o = jnp.argsort(dst, stable=True)
        src = src[_o]
        dst = dst[_o]
        return (x, src, dst)
    x, src, dst = _rec_inputs()

    def _L0_gnn_setup():
        import jax, jax.numpy as jnp
        import numpy as np
        N = 1250
        D = 512
        H = 4 * D
        E = 20000
        K = 8
        DELTA = D // K

        def _gcn_conv(x, W, b, src, dst, norm, n):
            msgs = x[src] * norm[:, None]
            agg = jax.ops.segment_sum(msgs, dst, num_segments=n)
            return agg @ W + b
        key = jax.random.key(seed)
        k0, k1, k2, k3, k4, k5 = jax.random.split(key, 6)
        x_all = jax.random.normal(k0, (N, D), dtype=jnp.float32)
        edge_index = jax.random.randint(k1, (2, E), 0, N, dtype=jnp.int64)
        s1 = 1.0 / np.sqrt(D)
        s2 = 1.0 / np.sqrt(H)
        W1 = jax.random.uniform(k2, (D, H), jnp.float32, -s1, s1)
        b1 = jnp.zeros((H,), jnp.float32)
        W2 = jax.random.uniform(k3, (H, D), jnp.float32, -s2, s2)
        b2 = jnp.zeros((D,), jnp.float32)
        return {'x_all': x_all, 'max_iter': 10, 'ix': 0, 'edge_index': edge_index, 'aug_loss': 0, 'W1': W1, 'b1': b1, 'W2': W2, 'b2': b2}
    _L0_gnn_all = _L0_gnn_setup()
    _L0_gnn_in = {k: v for k, v in _L0_gnn_all.items() if k in ('W1', 'b1', 'W2', 'b2')}
    del _L0_gnn_all

    def _L0_ffn_setup():
        import jax, jax.numpy as jnp
        import numpy as np
        B, S, D = (8, 512, 512)
        E, K, M = (16, 2, 1024)
        key = jax.random.key(seed)
        ks = jax.random.split(key, 5)
        return {'x': jax.random.normal(ks[0], (B, S, D), dtype=jnp.float32), 'wg': jax.random.normal(ks[1], (D, E), dtype=jnp.float32) * D ** (-0.5), 'w0': jax.random.normal(ks[2], (E, D, M), dtype=jnp.float32) * D ** (-0.5), 'w1': jax.random.normal(ks[3], (E, D, M), dtype=jnp.float32) * D ** (-0.5), 'wo': jax.random.normal(ks[4], (E, M, D), dtype=jnp.float32) * M ** (-0.5)}
    _L0_ffn_all = _L0_ffn_setup()
    _L0_ffn_in = {k: v for k, v in _L0_ffn_all.items() if k in ('wg', 'w0', 'w1', 'wo')}
    del _L0_ffn_all
    return {'x': x, 'src': src, 'dst': dst, 'L0_gnn_W1': _L0_gnn_in['W1'], 'L0_gnn_b1': _L0_gnn_in['b1'], 'L0_gnn_W2': _L0_gnn_in['W2'], 'L0_gnn_b2': _L0_gnn_in['b2'], 'L0_ffn_wg': _L0_ffn_in['wg'], 'L0_ffn_w0': _L0_ffn_in['w0'], 'L0_ffn_w1': _L0_ffn_in['w1'], 'L0_ffn_wo': _L0_ffn_in['wo']}

def reference(x, src, dst, L0_gnn_W1, L0_gnn_b1, L0_gnn_W2, L0_gnn_b2, L0_ffn_wg, L0_ffn_w0, L0_ffn_w1, L0_ffn_wo):
    import jax
    import jax.numpy as jnp

    def _L0_gnn_ref(x_all, max_iter, ix, edge_index, aug_loss, W1, b1, W2, b2):
        import jax, jax.numpy as jnp
        import numpy as np
        N = 1250
        D = 512
        H = 4 * D
        E = 20000
        K = 8
        DELTA = D // K

        def _gcn_conv(x, W, b, src, dst, norm, n):
            msgs = x[src] * norm[:, None]
            agg = jax.ops.segment_sum(msgs, dst, num_segments=n)
            return agg @ W + b
        n = x_all.shape[0]
        loop = jnp.arange(n, dtype=edge_index.dtype)
        src = jnp.concatenate([edge_index[0], loop])
        dst = jnp.concatenate([edge_index[1], loop])
        deg = jax.ops.segment_sum(jnp.ones_like(src, dtype=x_all.dtype), dst, num_segments=n)
        dinv = jnp.where(deg > 0, jax.lax.rsqrt(deg), 0.0)
        norm = dinv[src] * dinv[dst]
        x = _gcn_conv(x_all, W1, b1, src, dst, norm, n)
        z = jax.nn.relu(x)
        z = _gcn_conv(z, W2, b2, src, dst, norm, n)
        zk = z.reshape(n, K, DELTA)
        nrm = jnp.sqrt(jnp.sum(zk * zk, axis=2, keepdims=True))
        zk = zk / jnp.maximum(nrm, 1e-12)
        return zk.reshape(n, D)

    def _L0_ffn_ref(x, wg, w0, w1, wo):
        import jax, jax.numpy as jnp
        import numpy as np
        B, S, D = (8, 512, 512)
        E, K, M = (16, 2, 1024)
        gate_logits = jnp.einsum('bsd,de->bse', x, wg)
        top_vals, top_idx = jax.lax.top_k(gate_logits, K)
        top_w = jax.nn.softmax(top_vals.astype(jnp.float32), axis=-1).astype(x.dtype)
        dense_w = jnp.sum(jax.nn.one_hot(top_idx, E, dtype=x.dtype) * top_w[..., None], axis=-2)
        out = jnp.zeros_like(x)
        for e in range(E):
            h = jax.nn.silu(x @ w0[e]) * (x @ w1[e])
            out = out + dense_w[..., e:e + 1] * (h @ wo[e])
        return out
    edge_index = jnp.stack([src, dst])
    x = x + _L0_gnn_ref(_layernorm(x, axis=-1), 10, 0, edge_index, 0, L0_gnn_W1, L0_gnn_b1, L0_gnn_W2, L0_gnn_b2)
    x = x + _L0_ffn_ref(_layernorm(x, axis=-1)[None], L0_ffn_wg, L0_ffn_w0, L0_ffn_w1, L0_ffn_wo)[0]
    return x

_drawn_inputs = setup_inputs


def setup_inputs(seed=0):
    import zlib

    import numpy as np

    out = dict(_drawn_inputs(seed))
    spreads = {'L0_gnn_b1': (0.0, 0.1), 'L0_gnn_b2': (0.0, 0.1)}
    factors = {}
    for name, (base, spread) in spreads.items():
        noise = np.random.default_rng([zlib.crc32(name.encode()), seed]).standard_normal(out[name].shape)
        drawn = base * np.exp(spread * noise) if base else spread * noise
        out[name] = jnp.asarray(drawn.astype(out[name].dtype))
    for name, factor in factors.items():
        out[name] = (out[name] * factor).astype(out[name].dtype)
    return out
```

```python
from contextlib import ExitStack

import concourse.bass as bass
from concourse import mybir

F32 = mybir.dt.float32
F16 = mybir.dt.float16
I32 = mybir.dt.int32
ALU = mybir.AluOpType
ACT = mybir.ActivationFunctionType
AX_X = mybir.AxisListType.X

P = 128
GROUP = 64
LN_EPS = 1e-5
NORM_EPS = 1e-12
SLOTS = 224
SB = SLOTS - P
NO_NODE = 1300
RING = 4
Y_RING = 3


def gnn_moe_kernel(nc, x, src, dst, W1, b1, W2, b2, wg, w0, w1, wo, out):
    N, D = x.shape
    H = W1.shape[1]
    NE = src.shape[0]
    X, _, M = w0.shape
    NT = -(-N // P)
    NP = NT * P
    LAST = N - (NT - 1) * P
    KT, HT, MT = D // P, H // P, M // P
    G = D // GROUP
    ET = -(-NE // P)
    EB = ET - P
    EFULL = NE // P - P
    EREST = NE - (NE // P) * P
    EC = ET + NT
    BMAX = (2 * N + X * SLOTS) // SLOTS
    NIDX = BMAX + 1
    BPE = -(-N // SLOTS)
    NCH = [(0, 512), (512, 512), (1024, NP - 1024)]
    CCH = [(0, 512), (512, 512), (1024, N - 1024)]
    ZC = 256
    assert NT == 10 and KT == 4 and MT == 8 and 0 < EB <= P and NE > 3 * P

    xn_rows = nc.dram_tensor("xn_rows", [N, D], F32).ap()
    slot_token = nc.dram_tensor("slot_token", [NIDX * SLOTS, 1], I32).ap()
    y_rows = nc.dram_tensor("y_rows", [BMAX * SLOTS, D], F32).ap()

    with ExitStack() as ctx:
        def sb(name, shape, dt=F32):
            return ctx.enter_context(nc.sbuf_tensor(name, shape, dt))

        def sem(name):
            return ctx.enter_context(nc.semaphore(name))

        xt = sb("xt", [P, NT, D])
        xs = sb("xs", [P, NT, D])
        CT = sb("CT", [P, NT, NP])
        aggn = sb("aggn", [P, KT, NP])
        w1big = sb("w1big", [P, KT, H])
        w2big = sb("w2big", [P, HT, D])
        zbig = sb("zbig", [P, HT, ZC])
        xn2 = aggn[:, :, :].rearrange("p k n -> p (k n)").rearrange("p (t d) -> p t d", d=D)
        onehot = zbig[:, :, :].rearrange("p h z -> p (h z)").bitcast(F16)
        OHW = 1408
        assert RING * OHW <= HT * ZC * 2 and N + P <= OHW
        w0s = w1big[:, :, 0:M]
        w1s = w1big[:, :, M:2 * M]
        wos = zbig[:, :, :].rearrange("p h z -> p (h z)").rearrange("p (j d) -> p j d", d=D)
        w2flat = w2big[:, :, :].rearrange("p h d -> p (h d)")
        crow = aggn[:, 0:2, :]
        xT = w2flat[:, 0:KT * SLOTS].rearrange("p (k s) -> p k s", k=KT)
        hT = w2flat[:, 1024:1024 + MT * SLOTS].rearrange("p (m s) -> p m s", m=MT)
        sil = w2flat[:, 3072:3072 + 2 * SLOTS].rearrange("p (m s) -> p m s", m=2)
        grow = w2flat[:, 4096:5120].rearrange("p (a d) -> p a d", a=2)
        ysb = w2flat[:, 5120:6144].rearrange("p (a d) -> p a d", a=2)
        ctflat = CT[:, :, :].rearrange("p k n -> p (k n)")
        zflat = zbig[:, :, :].rearrange("p h z -> p (h z)")
        erow = ctflat[:, 0:4 * P].bitcast(I32).rearrange("p (q e) -> p q e", q=4)
        erowf = ctflat[:, 4 * P:8 * P].rearrange("p (q e) -> p q e", q=4)
        jidx = ctflat[:, 1024:1536].rearrange("p (q j) -> p q j", q=2)
        jval = ctflat[:, 1536:2048].rearrange("p (q j) -> p q j", q=2)
        diag = zflat[:, 0:NP]
        zero_row = zflat[:, 3072:3072 + D]
        assert RING * OHW <= 2 * 3072
        scratch = w2flat[:, 0:5 * D].rearrange("p (a d) -> p a d", a=5)
        xnT = scratch[:, 4, :]
        LW = NT * X
        gate = ctflat[:, 4096:4096 + 12 * LW].rearrange("p (j l) -> p j l", j=12)
        btab = ctflat[0:1, 6144:6144 + 32 * X].rearrange("p (b e) -> p b e", b=32)
        ygath = CT[:, 0:Y_RING, 0:2 * D].rearrange("p r (k d) -> p r k d", k=2)
        iota_n = sb("iota_n", [P, NP], F16)
        ident = sb("ident", [P, P])
        ones = sb("ones", [P, P])
        upper = sb("upper", [P, P])
        ecol = sb("ecol", [P, 2, EC])
        spans = sb("spans", [P, 2, 2])
        rel = sb("rel", [P, 4, NT])
        tlo = sb("tlo", [P, 2, NT])
        span_c = sb("span_c", [P, 4])
        run_table = sb("run_table", [1, 3, 16], I32)
        mv = sb("mv", [P, NT, 2])
        st6 = sb("st6", [P, NT, 6])
        deg = sb("deg", [P, NT])
        small = sb("small", [P, 12, NT])
        dinv = sb("dinv", [P, NT])
        scl = sb("scl", [P, NT])
        dinv_row = sb("dinv_row", [P, NP])
        b1c = sb("b1c", [P, HT])
        b2b = sb("b2b", [P, D])
        wgs = sb("wgs", [P, KT, X])
        nsm = sb("nsm", [P, 8, G])
        c16 = sb("c16", [P, LW])
        valid = sb("valid", [P, NT])
        tok = sb("tok", [P, NT], I32)
        rt = sb("rt", [P, 10, X])
        slotf = sb("slotf", [P, 2, NT])
        sloti = sb("sloti", [P, 2, NT], I32)
        tops = sb("tops", [P, 8, NT])
        bidx = sb("bidx", [1, 32])
        block_expert = sb("block_expert", [1, 34], I32)
        bef = sb("bef", [1, 34])
        zeros_i = sb("zeros_i", [P, 64], I32)
        idx_all = sb("idx_all", [P, 2, NIDX], I32)
        held = sb("held", [P, 2])
        idx_now = sb("idx_now", [P, 2], I32)
        ps = ctx.enter_context(nc.psum_tensor("ps", [P, 8, 512], F32))

        consts = sem("consts")
        zero_set = sem("zero_set")
        y_zeroed = sem("y_zeroed")
        edge_pad, x_pad, crow_pad = sem("edge_pad"), sem("x_pad"), sem("crow_pad")
        ld_edge, ld_x, ld_w1, ld_w2, ld_small = (sem(n) for n in ("ld_edge", "ld_x", "ld_w1", "ld_w2", "ld_small"))
        dve = sem("dve")
        edge_rows = sem("edge_rows")
        edge_cols_t = sem("edge_cols_t")
        rel_ready = sem("rel_ready")
        rel_t = sem("rel_t")
        span_ready = sem("span_ready")
        table_t = sem("table_t")
        table_ready = sem("table_ready")
        oh_ready = sem("oh_ready")
        oh_free = sem("oh_free")
        c_built = sem("c_built")
        c_row = sem("c_row")
        c_trans = sem("c_trans")
        ct_done = sem("ct_done")
        root_in = sem("root_in")
        root_out = sem("root_out")
        diag_ready = sem("diag_ready")
        bcast_ready = sem("bcast_ready")
        xs_ready = sem("xs_ready")
        agg_ps = sem("agg_ps")
        agg_done = sem("agg_done")
        z_ps = sem("z_ps")
        z_done = sem("z_done")
        y_ps = sem("y_ps")
        y_done = sem("y_done")
        o_ps = sem("o_ps")
        o_read = sem("o_read")
        sq_out = sem("sq_out")
        xn_done = sem("xn_done")
        xnT_ps = sem("xnT_ps")
        xnT_done = sem("xnT_done")
        gate_ps = sem("gate_ps")
        st_xn = sem("st_xn")
        exp_in = sem("exp_in")
        exp_out = sem("exp_out")
        routes = sem("routes")
        rank_ps = sem("rank_ps")
        slots_ready = sem("slots_ready")
        blocks_ready = sem("blocks_ready")
        list_zero = sem("list_zero")
        list_done = sem("list_done")
        idx_loaded = sem("idx_loaded")
        idx_ready = sem("idx_ready")
        gath_a, gath_b = sem("gath_a"), sem("gath_b")
        g_trans = sem("g_trans")
        xT_done = sem("xT_done")
        ld_w = [sem(f"ld_wp{i}") for i in range(6)]
        wo_used = sem("wo_used")
        gu_ps = sem("gu_ps")
        silu_done = sem("silu_done")
        h_done = sem("h_done")
        yb_ps = sem("yb_ps")
        yb_done = sem("yb_done")
        st_ya, st_yb = sem("st_ya"), sem("st_yb")
        ygat = [sem(f"ygat{i}") for i in range(Y_RING)]
        comb = sem("comb")
        st_out = sem("st_out")

        w_pieces = [
            (w0s[:, :, 0:M // 2], lambda e: w0[bass.ds(e, 1), :, 0:M // 2].rearrange("o (k p) m -> p (o k) m", p=P)),
            (w1s[:, :, 0:M // 2], lambda e: w1[bass.ds(e, 1), :, 0:M // 2].rearrange("o (k p) m -> p (o k) m", p=P)),
            (w0s[:, :, M // 2:M], lambda e: w0[bass.ds(e, 1), :, M // 2:M].rearrange("o (k p) m -> p (o k) m", p=P)),
            (w1s[:, :, M // 2:M], lambda e: w1[bass.ds(e, 1), :, M // 2:M].rearrange("o (k p) m -> p (o k) m", p=P)),
            (wos[:, 0:MT // 2, :], lambda e: wo[bass.ds(e, 1), 0:M // 2, :].rearrange("o (j p) d -> p (o j) d", p=P)),
            (wos[:, MT // 2:MT, :], lambda e: wo[bass.ds(e, 1), M // 2:M, :].rearrange("o (j p) d -> p (o j) d", p=P)),
        ]

        block = ctx.enter_context(nc.Block())

        @block.sync
        def _(sp):
            sp.wait_ge(edge_pad, 1)
            for q, e in ((2, dst), (0, src)):
                sp.dma_start(erow[:, q, :], e[0:P * P].rearrange("(j p) -> j p", p=P)).then_inc(ld_edge, 16)
                sp.dma_start(erow[0:EFULL, q + 1, :],
                             e[P * P:(P + EFULL) * P].rearrange("(j p) -> j p", p=P)).then_inc(ld_edge, 16)
                if EREST:
                    sp.dma_start(erow[EFULL:EFULL + 1, q + 1, 0:EREST],
                                 e[(P + EFULL) * P:NE].rearrange("(a p) -> a p", a=1)).then_inc(ld_edge, 16)
            sp.wait_ge(x_pad, 1)
            sp.dma_start(xt[:, 0:NT - 1, :], x[0:(NT - 1) * P, :].rearrange("(t p) d -> p t d", p=P)).then_inc(ld_x, 16)
            sp.dma_start(xt[0:LAST, NT - 1, :], x[(NT - 1) * P:N, :]).then_inc(ld_x, 16)
            sp.dma_start(b1c[:, :], b1.rearrange("(h p) -> p h", p=P), allow_slow_non_contiguous=True).then_inc(ld_small, 16)
            sp.dma_start(b2b[:, :], b2.rearrange("(a d) -> a d", a=1).broadcast_to([P, D])).then_inc(ld_small, 16)
            sp.dma_start(wgs[:, :, :], wg.rearrange("(k p) e -> p k e", p=P)).then_inc(ld_small, 16)
            sp.dma_start(w1big[:, :, :], W1.rearrange("(k p) h -> p k h", p=P)).then_inc(ld_w1, 16)
            sp.dma_start(w2big[:, :, :], W2.rearrange("(h p) d -> p h d", p=P)).then_inc(ld_w2, 16)
            sp.wait_ge(zero_set, 1)
            sp.dma_start(y_rows[X * SLOTS:BMAX * SLOTS, :].rearrange("(p j) d -> p j d", p=SLOTS // 2),
                         zero_row[0:SLOTS // 2, :].unsqueeze(1).broadcast_to([SLOTS // 2, 2 * (BMAX - X), D])).then_inc(y_zeroed, 16)
            sp.wait_ge(y_ps, NT)
            for i, (where, what) in enumerate(w_pieces):
                sp.dma_start(where, what(0)).then_inc(ld_w[i], 16)
            for t in range(NT):
                sp.wait_ge(xn_done, t + 1)
                n = P if t < NT - 1 else LAST
                sp.dma_start(xn_rows[t * P:t * P + n, :], xn2[0:n, t, :]).then_inc(st_xn, 16)
            sp.wait_ge(blocks_ready, 1)
            n_blocks = sp.value_load(block_expert[0:1, 33:34], min_val=2, max_val=BMAX)
            with sp.Fori(0, n_blocks - 1) as b:
                e = sp.value_load(block_expert[0:1, bass.ds(b + 1, 1)], min_val=0, max_val=X - 1)
                for i, (where, what) in enumerate(w_pieces):
                    if i == 0:
                        sp.wait_ge(gu_ps, b * MT + MT // 2)
                    if i == 2:
                        sp.wait_ge(gu_ps, b * MT + MT)
                    if i == 4:
                        sp.wait_ge(wo_used, b + 1)
                    if i == 5:
                        sp.wait_ge(yb_ps, b + 1)
                    sp.dma_start(where, what(e)).then_inc(ld_w[i], 16)
            for t in range(NT):
                sp.wait_ge(comb, t + 1)
                n = P if t < NT - 1 else LAST
                sp.dma_start(out[t * P:t * P + n, :], xt[0:n, t, :]).then_inc(st_out, 16)
            sp.wait_ge(st_out, 16 * NT)

        @block.gpsimd
        def _(pool):
            g = nc.gpsimd
            g.memset(erow[:, :, :], NO_NODE).then_inc(edge_pad, 1)
            g.iota(iota_n[:, :], pattern=[[1, NP]], base=0, channel_multiplier=0,
                   allow_small_or_imprecise_dtypes=True).then_inc(consts, 1)
            g.memset(ident[:, :], 0.0).then_inc(consts, 1)
            g.memset(ones[:, :], 1.0).then_inc(consts, 1)
            g.memset(upper[:, :], 1.0).then_inc(consts, 1)
            g.memset(valid[:, :], 1.0).then_inc(consts, 1)
            pool.wait_ge(consts, 5)
            g.affine_select(out=ident[:, :], in_=ident[:, :], compare_op=ALU.not_equal, fill=1.0, base=0,
                            pattern=[[-1, P]], channel_multiplier=1).then_inc(consts, 1)
            g.affine_select(out=upper[:, :], in_=upper[:, :], compare_op=ALU.is_ge, fill=0.0, base=-1,
                            pattern=[[1, P]], channel_multiplier=-1).then_inc(consts, 1)
            g.affine_select(out=valid[:, :], in_=valid[:, :], compare_op=ALU.is_ge, fill=0.0, base=N - 1,
                            pattern=[[-P, NT]], channel_multiplier=-1).then_inc(consts, 1)
            for q in range(2):
                g.iota(ecol[:, q, ET:EC], pattern=[[P, NT]], base=0, channel_multiplier=1,
                       allow_small_or_imprecise_dtypes=True).then_inc(consts, 1)
                g.iota(tlo[:, q, :], pattern=[[P, NT]], base=q * (P - 1), channel_multiplier=0,
                       allow_small_or_imprecise_dtypes=True).then_inc(consts, 1)
                g.iota(jidx[:, q, :], pattern=[[1 - 2 * q, 256]], base=1 if q == 0 else 256, channel_multiplier=0,
                       allow_small_or_imprecise_dtypes=True).then_inc(consts, 1)
            pool.wait_ge(consts, 14)
            for q in range(2):
                g.affine_select(out=ecol[:, q, ET:EC], in_=ecol[:, q, ET:EC], compare_op=ALU.is_ge,
                                fill=float(NO_NODE), base=N - 1, pattern=[[-P, NT]],
                                channel_multiplier=-1).then_inc(consts, 1)
            g.iota(tok[:, :], pattern=[[P, NT]], base=0, channel_multiplier=1).then_inc(consts, 1)
            g.iota(c16[:, :], pattern=[[0, NT], [-1, X]], base=X, channel_multiplier=0,
                   allow_small_or_imprecise_dtypes=True).then_inc(consts, 1)
            g.iota(bidx[:, :], pattern=[[1, 32]], base=0, channel_multiplier=0,
                   allow_small_or_imprecise_dtypes=True).then_inc(consts, 1)
            g.memset(zeros_i[:, :], 0).then_inc(consts, 1)
            pool.wait_ge(consts, 20)

            def hold(c):
                g.tensor_tensor(held[:, c:c + 1], ones[:, 0:1], ones[:, 0:1], ALU.mult)

            g.dma_start(slot_token.rearrange("(p j) a -> p (j a)", p=SLOTS // 2), zeros_i[0:SLOTS // 2, 0:2 * NIDX]).then_inc(list_zero, 16)
            pool.wait_ge(list_zero, 16)
            pool.wait_ge(slots_ready, 1)
            for t in range(NT):
                n = P if t < NT - 1 else LAST
                for k in range(2):
                    g.indirect_dma_start(out=slot_token, out_offset=bass.IndirectOffsetOnAxis(ap=sloti[0:n, k, t:t + 1], axis=0),
                                         in_=tok[0:n, t:t + 1], in_offset=None).then_inc(list_done, 16)
            pool.wait_ge(list_done, 16 * 2 * NT)
            by_slot = slot_token.rearrange("(b s) a -> s (b a)", s=SLOTS)
            g.dma_start(idx_all[:, 0, :], by_slot[0:P, :], allow_slow_non_contiguous=True).then_inc(idx_loaded, 16)
            g.dma_start(idx_all[0:SB, 1, :], by_slot[P:SLOTS, :], allow_slow_non_contiguous=True).then_inc(idx_loaded, 16)
            pool.wait_ge(idx_loaded, 32)
            pool.wait_ge(st_xn, 16 * NT)
            pool.wait_ge(blocks_ready, 1)
            n_blocks = pool.value_load(block_expert[0:1, 33:34], min_val=2, max_val=BMAX)
            with pool.Fori(0, n_blocks + 1) as b:
                pool.wait_ge(g_trans, b + 1)
                g.tensor_copy(idx_now[:, 0:1], idx_all[:, 0, bass.ds(b, 1)]).then_inc(idx_ready, 1)
                g.tensor_copy(idx_now[0:SB, 1:2], idx_all[0:SB, 1, bass.ds(b, 1)]).then_inc(idx_ready, 1)
                pool.wait_ge(idx_ready, b * 2 + 2)
                hold(0)
                g.indirect_dma_start(out=grow[:, 0, :], out_offset=None, in_=xn_rows,
                                     in_offset=bass.IndirectOffsetOnAxis(ap=idx_now[:, 0:1], axis=0)).then_inc(gath_a, 16)
                g.indirect_dma_start(out=grow[0:SB, 1, :], out_offset=None, in_=xn_rows,
                                     in_offset=bass.IndirectOffsetOnAxis(ap=idx_now[0:SB, 1:2], axis=0)).then_inc(gath_b, 16)
            pool.wait_ge(st_ya, n_blocks * 16 + 16)
            pool.wait_ge(st_yb, n_blocks * 16 + 16)
            hold(1)
            for t in range(NT):
                n = P if t < NT - 1 else LAST
                if t >= Y_RING:
                    pool.wait_ge(comb, t - Y_RING + 1)
                for k in range(2):
                    g.indirect_dma_start(out=ygath[0:n, t % Y_RING, k, :], out_offset=None, in_=y_rows,
                                         in_offset=bass.IndirectOffsetOnAxis(ap=sloti[0:n, k, t:t + 1], axis=0)
                                         ).then_inc(ygat[t % Y_RING], 16)

        @block.scalar
        def _(act):
            s = nc.scalar

            def root(n, where):
                act.wait_ge(root_in, n)
                s.activation(where, where, ACT.Sqrt).then_inc(root_out, 1)

            def c_tile(t, par):
                act.wait_ge(c_built, t + 1)
                if not isinstance(t, int) or t >= 2:
                    act.wait_ge(c_trans, t * 3 - 3)
                s.activation(crow[:, par, 0:N], ps[:, 3 * par:3 * par + 3, :].rearrange("p a n -> p (a n)")[:, 0:N],
                             ACT.Copy, accum_out=deg[:, bass.ds(t, 1)]).then_inc(c_row, 1)

            def c_cols(t):
                for q, n in enumerate((4, 4, 2)):
                    act.wait_ge(c_trans, t * 3 + q + 1)
                    s.activation(CT[:, 4 * q:4 * q + n, bass.ds(t * P, P)],
                                 ps[:, 6 + q % 2, 0:n * P].rearrange("p (a n) -> p a n", a=n), ACT.Copy).then_inc(ct_done, 1)

            act.wait_ge(crow_pad, 1)
            c_tile(0, 0)
            c_tile(1, 1)
            c_cols(0)
            with act.Fori(0, NT // 2 - 1) as i:
                c_tile(i * 2 + 2, 0)
                c_cols(i * 2 + 1)
                c_tile(i * 2 + 3, 1)
                c_cols(i * 2 + 2)
            c_cols(NT - 1)
            root(1, small[:, 0, :])
            root(2, small[:, 4, :])
            act.wait_ge(ld_small, 48)
            act.wait_ge(y_zeroed, 16)
            n = 0
            for c in range(NP // ZC):
                for h in range(HT):
                    act.wait_ge(z_ps, n + 1)
                    s.activation(zbig[:, h, :], ps[:, n % 4, 0:ZC], ACT.Relu, bias=b1c[:, h:h + 1]).then_inc(z_done, 1)
                    n += 1
            for t in range(NT):
                act.wait_ge(o_read, t + 1)
                s.activation(scratch[:, 2 + t % 2, :], scratch[:, t % 2, :], ACT.Square).then_inc(sq_out, 1)
                root(3 + 2 * t, nsm[:, 1, :])
                root(4 + 2 * t, small[:, 8, t:t + 1])
            act.wait_ge(exp_in, 1)
            s.activation(tops[:, 3, :], tops[:, 2, :], ACT.Exp).then_inc(exp_out, 1)

            act.wait_ge(blocks_ready, 1)
            n_blocks = act.value_load(block_expert[0:1, 33:34], min_val=2, max_val=BMAX)

            def take_xT(b):
                act.wait_ge(g_trans, b + 2)
                s.activation(xT[:, :, 0:P], ps[:, 0, :].rearrange("p (k n) -> p k n", k=KT), ACT.Copy).then_inc(xT_done, 1)

            take_xT(0)
            with act.Fori(0, n_blocks) as b:
                for m in range(MT):
                    act.wait_ge(gu_ps, b * MT + m + 1)
                    s.activation(sil[:, m % 2, :], ps[:, 2 + m % 2, 0:SLOTS], ACT.Silu).then_inc(silu_done, 1)
                take_xT(b + 1)
                act.wait_ge(yb_ps, b + 1)
                act.wait_ge(st_ya, b * 16 + 16)
                s.activation(ysb[:, 0, :], ps[:, 6, :], ACT.Copy).then_inc(yb_done, 1)
                act.wait_ge(yb_done, b * 2 + 4)
                act.dma_start(y_rows[bass.ds(b * SLOTS, P), :], ysb[:, 0, :]).then_inc(st_ya, 16)
                act.dma_start(y_rows[bass.ds(b * SLOTS + P, SB), :], ysb[0:SB, 1, :]).then_inc(st_yb, 16)

        @block.vector
        def _(v):
            V = nc.vector
            steps = [0]

            def then(ins):
                steps[0] += 1
                ins.then_inc(dve, 1)
                v.wait_ge(dve, steps[0])

            roots = [0]

            def rsqrt(rows, value):
                V.tensor_copy(rows[0], value).then_inc(root_in, 1)
                roots[0] += 1
                v.wait_ge(root_out, roots[0])
                then(V.reciprocal(rows[2], rows[0]))
                newton(rows, value)

            def newton(rows, value):
                then(V.tensor_tensor(rows[1], rows[2], rows[2], ALU.mult))
                then(V.tensor_tensor(rows[3], rows[1], value, ALU.mult))
                then(V.tensor_scalar(rows[1], rows[3], -0.5, 1.5, ALU.mult, ALU.add))
                then(V.tensor_tensor(rows[0], rows[2], rows[1], ALU.mult))

            V.memset(xt[:, NT - 1, :], 0.0).then_inc(x_pad, 1)
            V.memset(crow[:, 0, N:NP], 0.0)
            V.memset(crow[:, 1, N:NP], 0.0).then_inc(crow_pad, 1)
            V.memset(zero_row, 0.0).then_inc(zero_set, 1)
            V.memset(st6[:, :, :], 0.0).then_inc(h_done, 2)
            V.memset(run_table[0:1, :, :], 0).then_inc(oh_free, RING - 1)
            for j, (free, n) in enumerate(((c_row, 2), (ct_done, 1), (g_trans, 1), (yb_done, 2), (st_ya, 16), (st_yb, 16))):
                V.memset(slotf[:, 0, j:j + 1], 0.0).then_inc(free, n)
            v.wait_ge(ld_edge, 16 * (6 if EREST else 4))
            V.tensor_copy(erowf, erow[:, :, :]).then_inc(edge_rows, 1)
            v.wait_ge(edge_rows, 1)
            for q in range(2):
                V.tensor_reduce(spans[:, 0, q:q + 1], erowf[:, 2 + q, :], AX_X, ALU.min)
                then(V.tensor_reduce(spans[:, 1, q:q + 1], erowf[:, 2 + q, :], AX_X, ALU.max))
            v.wait_ge(consts, 20)
            for q in range(2):
                V.tensor_scalar(rel[:, q, :], tlo[:, 1, :], spans[:, 0, q:q + 1], None, ALU.is_ge)
                then(V.tensor_scalar(rel[:, 2 + q, :], tlo[:, 0, :], spans[:, 1, q:q + 1], None, ALU.is_le))
            V.tensor_tensor(rel[:, 0:2, :], rel[:, 0:2, :], rel[:, 2:4, :], ALU.mult).then_inc(rel_ready, 1)
            v.wait_ge(edge_cols_t, 1)
            V.tensor_copy(ecol[:, 0, 0:ET], ps[:, 0, 0:ET])
            then(V.tensor_copy(ecol[:, 1, 0:ET], ps[:, 0, 2 * P:2 * P + ET]))
            v.wait_ge(rel_t, 1)
            for q in range(2):
                then(V.tensor_tensor(jval[0:NT, q, 0:ET], ps[0:NT, 1, 0:ET], jidx[0:NT, q, 0:ET], ALU.mult))
                then(V.tensor_reduce(span_c[0:NT, q:q + 1], jval[0:NT, q, 0:ET], AX_X, ALU.max))
            then(V.tensor_scalar(span_c[0:NT, 1:2], span_c[0:NT, 1:2], -1.0, 256.0, ALU.mult, ALU.add))
            then(V.tensor_scalar(span_c[0:NT, 1:2], span_c[0:NT, 1:2], float(ET - 2), None, ALU.min))
            then(V.tensor_scalar(span_c[0:NT, 2:3], span_c[0:NT, 1:2], 2.0, None, ALU.add))
            then(V.tensor_tensor(span_c[0:NT, 0:1], span_c[0:NT, 0:1], span_c[0:NT, 2:3], ALU.max))
            V.tensor_tensor(span_c[0:NT, 2:3], span_c[0:NT, 0:1], span_c[0:NT, 1:2], ALU.subtract).then_inc(span_ready, 1)
            v.wait_ge(table_t, 1)
            V.tensor_copy(run_table[0:1, :, 0:NT], ps[0:1, 1, 0:48].rearrange("p (a n) -> p a n", a=3)[:, :, 0:NT]).then_inc(table_ready, 1)
            v.wait_ge(table_ready, 1)

            def one_hots(col, n, t):
                v.wait_ge(oh_free, n + 1)
                g = n + t
                dst_lo = t * P
                o = g % RING * OHW
                V.tensor_scalar(onehot[:, bass.ds(o, N)], iota_n[:, 0:N], ecol[:, 0, bass.ds(col, 1)], None, ALU.is_equal)
                V.tensor_scalar(onehot[:, bass.ds(o + N, P)], iota_n[:, bass.ds(dst_lo, P)],
                                ecol[:, 1, bass.ds(col, 1)], None, ALU.is_equal).then_inc(oh_ready, 1)

            with v.Fori(0, NT) as t:
                first = v.value_load(run_table[0:1, 0, bass.ds(t, 1)], min_val=0, max_val=ET - 2)
                count = v.value_load(run_table[0:1, 1, bass.ds(t, 1)], min_val=2, max_val=ET)
                base = v.value_load(run_table[0:1, 2, bass.ds(t, 1)], min_val=0, max_val=(NT - 1) * ET)
                with v.Fori(0, count) as i:
                    one_hots(nc.s_assert_within(first + i, 0, ET - 1, skip_runtime_bounds_check_because="a run ends at ET or before"), base + i, t)
                one_hots(t + ET, base + count, t)
            v.wait_ge(ld_x, 32)
            for t in range(NT):
                last = V.bn_stats(st6[:, t, :], xt[:, t, :])
            then(last)
            for t in range(NT):
                last = V.bn_aggr(mv[:, t, :], st6[:, t, :])
            then(last)
            then(V.tensor_scalar(small[:, 10, :], mv[:, :, 1], LN_EPS, None, ALU.add))
            rsqrt([small[:, j, :] for j in range(4)], small[:, 10, :])
            v.wait_ge(c_row, NT + 2)
            then(V.tensor_scalar(small[:, 9, :], deg[:, :], 1.0, None, ALU.max))
            rsqrt([small[:, j, :] for j in range(4, 8)], small[:, 9, :])
            then(V.tensor_copy(dinv[:, :], small[:, 4, :]))
            then(V.tensor_tensor(scl[:, :], dinv[:, :], small[:, 0, :], ALU.mult))
            for t in range(NT):
                V.tensor_scalar(xs[:, t, :], xt[:, t, :], mv[:, t, 0:1], scl[:, t:t + 1], ALU.subtract,
                                ALU.mult).then_inc(xs_ready, 1)
            for t in range(NT):
                V.tensor_scalar(diag[:, t * P:(t + 1) * P], ident[:, :], dinv[:, t:t + 1], None,
                                ALU.mult).then_inc(diag_ready, 1)
            v.wait_ge(bcast_ready, 1)
            then(V.tensor_copy(dinv_row[:, :], ps[:, 0:3, :].rearrange("p a n -> p (a n)")[:, 0:NP]))
            n = 0
            for m in range(KT):
                for lo, w in NCH:
                    v.wait_ge(agg_ps, n + 1)
                    V.tensor_tensor(aggn[:, m, lo:lo + w], ps[:, 3 + n % 4, 0:w], dinv_row[:, lo:lo + w],
                                    ALU.mult).then_inc(agg_done, 1)
                    n += 1
            for t in range(NT):
                v.wait_ge(y_ps, t + 1)
                V.tensor_scalar(xs[:, t, :], ps[:, 4 + t % 2, :], dinv[:, t:t + 1], None, ALU.mult).then_inc(y_done, 1)
            v.wait_ge(ld_small, 48)
            for t in range(NT):
                z, sq = scratch[:, t % 2, :], scratch[:, 2 + t % 2, :]
                v.wait_ge(o_ps, t + 1)
                V.scalar_tensor_tensor(z, ps[:, t % 3, :], dinv[:, t:t + 1], b2b[:, :], ALU.mult, ALU.add).then_inc(o_read, 1)
                v.wait_ge(sq_out, t + 1)
                then(V.tensor_reduce(nsm[:, 0, :], sq.rearrange("p (g f) -> p g f", g=G), AX_X, ALU.add))
                V.tensor_copy(nsm[:, 1, :], nsm[:, 0, :]).then_inc(root_in, 1)
                roots[0] += 1
                v.wait_ge(root_out, roots[0])
                then(V.tensor_scalar(nsm[:, 1, :], nsm[:, 1, :], NORM_EPS, None, ALU.max))
                then(V.reciprocal(nsm[:, 3, :], nsm[:, 1, :]))
                newton([nsm[:, 5, :], nsm[:, 2, :], nsm[:, 3, :], nsm[:, 4, :]], nsm[:, 0, :])
                then(V.tensor_scalar(nsm[:, 5, :], nsm[:, 5, :], 1.0 / NORM_EPS, None, ALU.min))
                then(V.tensor_tensor(z.rearrange("p (g f) -> p g f", g=G), z.rearrange("p (g f) -> p g f", g=G),
                                     nsm[:, 5, :].unsqueeze(2).broadcast_to([P, G, GROUP]), ALU.mult))
                then(V.tensor_tensor(xt[:, t, :], xt[:, t, :], z, ALU.add))
                then(V.bn_stats(st6[:, t, :], xt[:, t, :]))
                then(V.bn_aggr(mv[:, t, :], st6[:, t, :]))
                then(V.tensor_scalar(small[:, 10, t:t + 1], mv[:, t, 1:2], LN_EPS, None, ALU.add))
                rsqrt([small[:, j, t:t + 1] for j in (8, 1, 2, 3)], small[:, 10, t:t + 1])
                V.tensor_scalar(xn2[:, t, :], xt[:, t, :], mv[:, t, 0:1], small[:, 8, t:t + 1], ALU.subtract,
                                ALU.mult).then_inc(xn_done, 1)
                v.wait_ge(xnT_ps, t + 1)
                V.tensor_copy(xnT, ps[:, 3 + t % 2, :]).then_inc(xnT_done, 1)

            v.wait_ge(gate_ps, NT)
            g3 = lambda j: gate[:, j, :].rearrange("p (t e) -> p t e", e=X)
            c3 = c16[:, :].rearrange("p (t e) -> p t e", e=X)
            over = lambda ap: ap.unsqueeze(2).broadcast_to([P, NT, X])
            then(V.tensor_copy(gate[:, 0, :], ps[:, 5, 0:LW]))
            for k in range(2):
                then(V.tensor_reduce(tops[:, k, :], g3(k), AX_X, ALU.max))
                then(V.tensor_tensor(g3(2), g3(k), over(tops[:, k, :]), ALU.is_equal))
                then(V.tensor_tensor(g3(3), g3(2), c3, ALU.mult))
                then(V.tensor_reduce(tops[:, 7, :], g3(3), AX_X, ALU.max))
                then(V.tensor_tensor(g3(4 + k), c3, over(tops[:, 7, :]), ALU.is_equal))
                if k == 0:
                    then(V.scalar_tensor_tensor(gate[:, 1, :], gate[:, 4, :], -3.0e38, gate[:, 0, :], ALU.mult, ALU.add))
            V.tensor_tensor(tops[:, 2, :], tops[:, 1, :], tops[:, 0, :], ALU.subtract).then_inc(exp_in, 1)
            then(V.tensor_tensor(gate[:, 6, :], gate[:, 4, :], gate[:, 5, :], ALU.add))
            V.tensor_tensor(g3(7), g3(6), over(valid[:, :]), ALU.mult).then_inc(routes, 1)
            v.wait_ge(exp_out, 1)
            then(V.tensor_scalar(tops[:, 4, :], tops[:, 3, :], 1.0, None, ALU.add))
            then(V.reciprocal(tops[:, 5, :], tops[:, 4, :]))
            then(V.tensor_tensor(tops[:, 6, :], tops[:, 5, :], tops[:, 3, :], ALU.mult))
            v.wait_ge(rank_ps, 1)
            then(V.tensor_copy(gate[:, 8, :], ps[:, 7, 0:LW]))
            then(V.memset(rt[:, 0, :], 0.0))
            for t in range(NT):
                then(V.tensor_tensor(gate[:, 9, t * X:(t + 1) * X], ps[:, 6, t * X:(t + 1) * X], rt[:, t % 2, :], ALU.add))
                then(V.tensor_tensor(rt[:, (t + 1) % 2, :], ps[:, 7, t * X:(t + 1) * X], rt[:, t % 2, :], ALU.add))
            tot = rt[:, NT % 2, :]
            then(V.memset(rt[:, 2, :], 1.0))
            for m in range(1, BPE):
                then(V.tensor_scalar(rt[:, 3, :], tot, float(m * SLOTS), None, ALU.is_gt))
                then(V.tensor_tensor(rt[:, 2, :], rt[:, 2, :], rt[:, 3, :], ALU.add))
            cur, nxt, sh = 4, 5, 1
            then(V.tensor_copy(rt[:, cur, :], rt[:, 2, :]))
            while sh < X:
                V.tensor_copy(rt[:, nxt, 0:sh], rt[:, cur, 0:sh])
                then(V.tensor_tensor(rt[:, nxt, sh:X], rt[:, cur, sh:X], rt[:, cur, 0:X - sh], ALU.add))
                cur, nxt, sh = nxt, cur, 2 * sh
            ends = rt[:, cur, :]
            then(V.tensor_tensor(rt[:, 6, :], ends, rt[:, 2, :], ALU.subtract))
            then(V.tensor_scalar(rt[:, 7, :], rt[:, 6, :], float(SLOTS), None, ALU.mult))
            then(V.tensor_tensor(g3(10), g3(9), rt[:, 7, :].unsqueeze(1).broadcast_to([P, NT, X]), ALU.add))
            for k in range(2):
                then(V.tensor_tensor(g3(11), g3(10), g3(4 + k), ALU.mult))
                then(V.tensor_reduce(slotf[:, k, :], g3(11), AX_X, ALU.add))
            V.tensor_copy(sloti[:, :, :], slotf[:, :, :]).then_inc(slots_ready, 1)
            bt = btab
            then(V.tensor_tensor(bt, bidx[0:1, :].unsqueeze(2).broadcast_to([1, 32, X]),
                                 ends[0:1, :].unsqueeze(1).broadcast_to([1, 32, X]), ALU.is_ge))
            then(V.tensor_reduce(bef[0:1, 0:32], bt, AX_X, ALU.add))
            then(V.tensor_scalar(bef[0:1, 0:32], bef[0:1, 0:32], float(X - 1), None, ALU.min))
            then(V.tensor_copy(bef[0:1, 32:33], ends[0:1, X - 1:X]))
            then(V.tensor_copy(bef[0:1, 33:34], ends[0:1, X - 1:X]))
            V.tensor_copy(block_expert[0:1, :], bef[0:1, :]).then_inc(blocks_ready, 1)
            v.wait_ge(blocks_ready, 1)
            n_blocks = v.value_load(block_expert[0:1, 33:34], min_val=2, max_val=BMAX)

            def take_xT(b):
                v.wait_ge(g_trans, b + 2)
                V.tensor_copy(xT[:, :, P:SLOTS], ps[:, 1, 0:KT * SB].rearrange("p (k n) -> p k n", k=KT)).then_inc(xT_done, 1)

            take_xT(0)
            with v.Fori(0, n_blocks) as b:
                for m in range(MT):
                    v.wait_ge(silu_done, b * MT + m + 1)
                    V.tensor_tensor(hT[:, m, :], ps[:, 4 + m % 2, 0:SLOTS], sil[:, m % 2, :], ALU.mult).then_inc(h_done, 1)
                take_xT(b + 1)
                v.wait_ge(yb_ps, b + 1)
                v.wait_ge(st_yb, b * 16 + 16)
                V.tensor_copy(ysb[0:SB, 1, :], ps[0:SB, 7, :]).then_inc(yb_done, 1)
            for t in range(NT):
                n = P if t < NT - 1 else LAST
                v.wait_ge(ygat[t % Y_RING], 32 * (t // Y_RING + 1))
                then(V.scalar_tensor_tensor(xt[0:n, t, :], ygath[0:n, t % Y_RING, 0, :], tops[0:n, 5, t:t + 1],
                                            xt[0:n, t, :], ALU.mult, ALU.add))
                V.scalar_tensor_tensor(xt[0:n, t, :], ygath[0:n, t % Y_RING, 1, :], tops[0:n, 6, t:t + 1],
                                       xt[0:n, t, :], ALU.mult, ALU.add).then_inc(comb, 1)

        @block.tensor
        def _(pe):
            T = nc.tensor
            pe.wait_ge(consts, 20)
            pe.wait_ge(edge_rows, 1)
            for q in range(4):
                last = T.transpose(ps[:, 0, q * P:(q + 1) * P], erowf[:, q, :], ident[:, :])
            last.then_inc(edge_cols_t, 1)
            pe.wait_ge(rel_ready, 1)
            T.transpose(ps[0:NT, 1, 0:P], rel[:, 0, :], ident[:, :])
            T.transpose(ps[0:NT, 1, P:P + EB], rel[0:EB, 1, :], ident[0:EB, 0:EB]).then_inc(rel_t, 1)
            pe.wait_ge(span_ready, 1)
            for j, (c, rhs) in enumerate(((1, ident), (2, ident), (2, upper))):
                last = T.matmul(ps[0:1, 1, 16 * j:16 * j + NT], span_c[0:NT, c:c + 1], rhs[0:NT, 0:NT],
                                start=True, stop=True)
            last.then_inc(table_t, 1)
            pe.wait_ge(table_ready, 1)

            def count_edges(par, g, start, stop):
                pe.wait_ge(oh_ready, g + 1)
                o = g % RING * OHW
                for q, (lo, w) in enumerate(CCH):
                    last = T.matmul(ps[:, 3 * par + q, 0:w], onehot[:, bass.ds(o + N, P)],
                                    onehot[:, bass.ds(o + lo, w)], start=start, stop=stop)
                last.then_inc(c_built if stop else oh_free, 1)

            def build(t, par):
                count = pe.value_load(run_table[0:1, 1, bass.ds(t, 1)], min_val=2, max_val=ET)
                base = pe.value_load(run_table[0:1, 2, bass.ds(t, 1)], min_val=0, max_val=(NT - 1) * ET)
                pe.wait_ge(c_row, t + 1)
                count_edges(par, base + t, True, False)
                with pe.Fori(1, count) as i:
                    count_edges(par, base + t + i, False, False)
                count_edges(par, base + t + count, False, True)

            def turn(t, par):
                pe.wait_ge(c_row, t + 3)
                for q, n in enumerate((4, 4, 2)):
                    pe.wait_ge(ct_done, t * 3 + max(q, 1))
                    for a in range(n):
                        k = 4 * q + a
                        last = T.transpose(ps[:, 6 + q % 2, a * P:(a + 1) * P], crow[:, par, k * P:(k + 1) * P], ident[:, :])
                    last.then_inc(c_trans, 1)

            build(0, 0)
            with pe.Fori(0, NT // 2 - 1) as i:
                build(i * 2 + 1, 1)
                turn(i * 2, 0)
                build(i * 2 + 2, 0)
                turn(i * 2 + 1, 1)
            build(NT - 1, 1)
            turn(NT - 2, 0)
            turn(NT - 1, 1)

            pe.wait_ge(diag_ready, NT)
            for q, (lo, w) in enumerate(NCH):
                last = T.matmul(ps[:, q, 0:w], ones[:, :], diag[:, lo:lo + w], start=True, stop=True)
            last.then_inc(bcast_ready, 1)
            pe.wait_ge(ct_done, 3 * NT + 1)
            pe.wait_ge(xs_ready, NT)
            n = 0
            for m in range(KT):
                for lo, w in NCH:
                    if n >= 4:
                        pe.wait_ge(agg_done, n - 3)
                    for k in range(NT):
                        last = T.matmul(ps[:, 3 + n % 4, 0:w], xs[:, k, m * P:(m + 1) * P], CT[:, k, lo:lo + w],
                                        start=k == 0, stop=k == NT - 1)
                    last.then_inc(agg_ps, 1)
                    n += 1
            pe.wait_ge(ld_w1, 16)
            pe.wait_ge(ld_w2, 16)
            pe.wait_ge(agg_done, n)
            n = 0
            for c in range(NP // ZC):
                for h in range(HT):
                    if n >= 4:
                        pe.wait_ge(z_done, n - 3)
                    for k in range(KT):
                        last = T.matmul(ps[:, n % 4, 0:ZC], w1big[:, k, h * P:(h + 1) * P],
                                        aggn[:, k, c * ZC:(c + 1) * ZC], start=k == 0, stop=k == KT - 1)
                    last.then_inc(z_ps, 1)
                    n += 1
                pe.wait_ge(z_done, n)
                for a in range(ZC // P):
                    t = c * (ZC // P) + a
                    if t >= 2:
                        pe.wait_ge(y_done, t - 1)
                    for h in range(HT):
                        last = T.matmul(ps[:, 4 + t % 2, :], zbig[:, h, a * P:(a + 1) * P], w2big[:, h, :],
                                        start=h == 0, stop=h == HT - 1)
                    last.then_inc(y_ps, 1)

            def gate_tile(t):
                pe.wait_ge(xn_done, t + 1)
                if t >= 1:
                    pe.wait_ge(xnT_done, t)
                for k in range(KT):
                    last = T.transpose(ps[:, 3 + t % 2, k * P:(k + 1) * P], xn2[:, t, k * P:(k + 1) * P], ident[:, :])
                last.then_inc(xnT_ps, 1)
                pe.wait_ge(xnT_done, t + 1)
                for k in range(KT):
                    last = T.matmul(ps[:, 5, t * X:(t + 1) * X], xnT[:, k * P:(k + 1) * P], wgs[:, k, :],
                                    start=k == 0, stop=k == KT - 1)
                last.then_inc(gate_ps, 1)

            pe.wait_ge(y_done, NT)
            pe.wait_ge(ld_small, 48)
            for t in range(NT):
                if t >= 3:
                    pe.wait_ge(o_read, t - 2)
                for k in range(NT):
                    last = T.matmul(ps[:, t % 3, :], CT[:, k, t * P:(t + 1) * P], xs[:, k, :],
                                    start=k == 0, stop=k == NT - 1)
                last.then_inc(o_ps, 1)
                if t >= 1:
                    gate_tile(t - 1)
            gate_tile(NT - 1)
            pe.wait_ge(routes, 1)
            T.matmul(ps[:, 6, 0:LW], upper[:, :], gate[:, 7, :], start=True, stop=True)
            T.matmul(ps[:, 7, 0:LW], ones[:, :], gate[:, 7, :], start=True, stop=True).then_inc(rank_ps, 1)

            def turn_rows(b):
                pe.wait_ge(gath_a, b * 16 + 16)
                pe.wait_ge(gath_b, b * 16 + 16)
                for k in range(KT):
                    T.transpose(ps[:, 0, k * P:(k + 1) * P], grow[:, 0, k * P:(k + 1) * P], ident[:, :])
                for k in range(KT):
                    last = T.transpose(ps[:, 1, k * SB:(k + 1) * SB], grow[0:SB, 1, k * P:(k + 1) * P], ident[0:SB, 0:SB])
                last.then_inc(g_trans, 1)

            pe.wait_ge(blocks_ready, 1)
            n_blocks = pe.value_load(block_expert[0:1, 33:34], min_val=2, max_val=BMAX)
            turn_rows(0)
            with pe.Fori(0, n_blocks) as b:
                pe.wait_ge(xT_done, b * 2 + 2)
                for m in range(MT):
                    if m % (MT // 2) == 0:
                        for i in range(2):
                            pe.wait_ge(ld_w[2 * (m // (MT // 2)) + i], b * 16 + 16)
                    pe.wait_ge(h_done, b * MT + m + 1)
                    for ws, bank in ((w0s, 2), (w1s, 4)):
                        for k in range(KT):
                            last = T.matmul(ps[:, bank + m % 2, 0:SLOTS], ws[:, k, m * P:(m + 1) * P], xT[:, k, :],
                                            start=k == 0, stop=k == KT - 1)
                    last.then_inc(gu_ps, 1)
                turn_rows(b + 1)
                pe.wait_ge(h_done, b * MT + MT + 2)
                pe.wait_ge(yb_done, b * 2 + 2)
                for m in range(MT):
                    if m % (MT // 2) == 0:
                        pe.wait_ge(ld_w[4 + m // (MT // 2)], b * 16 + 16)
                    T.matmul(ps[:, 6, :], hT[:, m, 0:P], wos[:, m, :], start=m == 0, stop=m == MT - 1)
                    last = T.matmul(ps[0:SB, 7, :], hT[:, m, P:SLOTS], wos[:, m, :], start=m == 0, stop=m == MT - 1)
                    if m == MT // 2 - 1:
                        last.then_inc(wo_used, 1)
                last.then_inc(yb_ps, 1)


INPUTS = ["x", "src", "dst", "L0_gnn_W1", "L0_gnn_b1", "L0_gnn_W2", "L0_gnn_b2",
          "L0_ffn_wg", "L0_ffn_w0", "L0_ffn_w1", "L0_ffn_wo"]


def kernel(**inputs):
    import numpy as np
    import concourse.bacc as bacc
    from concourse.bass_utils import run_bass_kernel_spmd

    nc = bacc.Bacc("TRN2", target_bir_lowering=False, num_devices=1)
    arrays, args = {}, []
    for name in INPUTS:
        a = np.ascontiguousarray(inputs[name])
        arrays[f"in_{name}"] = a
        args.append(nc.dram_tensor(f"in_{name}", a.shape, mybir.dt.from_np(a.dtype), kind="ExternalInput").ap())
    out = nc.dram_tensor("out", arrays["in_x"].shape, F32, kind="ExternalOutput").ap()
    gnn_moe_kernel(nc, *args, out)
    result = run_bass_kernel_spmd(nc, [arrays], core_ids=[0])
    return result.results[0]["out"]
```

```python
from contextlib import ExitStack

import concourse.bass as bass
from concourse import mybir

F32 = mybir.dt.float32
F32R = mybir.dt.float32r
F16 = mybir.dt.float16
BF16 = mybir.dt.bfloat16
I32 = mybir.dt.int32
ALU = mybir.AluOpType
ACT = mybir.ActivationFunctionType
AX_X = mybir.AxisListType.X

P = 128
GROUP = 64
LN_EPS = 1e-5
NORM_EPS = 1e-12
SLOTS = 224
SB = SLOTS - P
NO_NODE = 1300
Y_RING = 3


def gnn_moe_kernel(nc, x, src, dst, W1, b1, W2, b2, wg, w0, w1, wo, out):
    N, D = x.shape
    H = W1.shape[1]
    NE = src.shape[0]
    X, _, M = w0.shape
    NT = -(-N // P)
    NP = NT * P
    LAST = N - (NT - 1) * P
    KT, HT, MT = D // P, H // P, M // P
    G = D // GROUP
    ET = -(-NE // P)
    EB = ET - P
    EFULL = NE // P - P
    EREST = NE - (NE // P) * P
    U = 4
    EC = ET + 2 * U
    BMAX = (2 * N + X * SLOTS) // SLOTS
    NIDX = BMAX + 1
    BPE = -(-N // SLOTS)
    NCH = [(0, 512), (512, 512), (1024, NP - 1024)]
    CCH = [(0, 512), (512, 512), (1024, N - 1024)]
    ZC = 256
    NZ = NP // ZC
    HQ = 2
    HG = HT // HQ
    ROUND = 1.5 * 2 ** 23
    COUNT_MAX = 4095
    assert NT == 10 and KT == 4 and MT == 8 and 0 < EB <= P and NE > 3 * P

    xn_rows = nc.dram_tensor("xn_rows", [N, D], F32).ap()
    y_rows = nc.dram_tensor("y_rows", [BMAX * SLOTS, D], F32).ap()

    with ExitStack() as ctx:
        def sb(name, shape, dt=F32):
            return ctx.enter_context(nc.sbuf_tensor(name, shape, dt))

        def sem(name):
            return ctx.enter_context(nc.semaphore(name))

        ARENA = 192512
        arena = ctx.enter_context(nc.sbuf_tensor("arena", [P, ARENA], mybir.dt.uint8))
        arena_base = nc.sbuf_base - ARENA

        def at(name, offset, shape, dt=F32):
            return nc.alloc_sbuf_tensor_at(name, shape, dt, offset=arena_base + offset)

        CT = at("CT", 0, [P, NT, NP])
        CTr = at("CTr", 0, [P, NT, NP], F32R)
        erow = at("erow", 0, [P, 4, P], I32)
        erowf = at("erowf", 2048, [P, 4, P])
        jidx = at("jidx", 4096, [P, 2, 256])
        jval = at("jval", 6144, [P, 2, 256])
        crow = at("crow", 51200, [P, 2, NP])
        oh_src = at("oh_src", 171008, [P, 2 * U * NP], F16)
        oh_dst = at("oh_dst", 61440, [P, 2 * U * P], F16)
        iota_n = at("iota_n", 72704, [P, NP], F16)
        ecol = at("ecol", 75264, [P, 2, EC])
        loops = at("loops", 146432, [P, 2 * NP - P], F16)
        ident_h = loops[:, NP - P:NP]
        dst_h = at("dst_h", 77824, [P, EC], F16)
        x_in = at("x_in", 84992, [P, NT, D])
        xs_r = at("xs_r", 105472, [P, NT, D], F32R)
        xs_l = at("xs_l", 125952, [P, NT, D], F32R)
        xs_f = at("xs_f", 146432, [P, 3, D])
        ln_rest = at("ln_rest", 105472, [P, 2, NT, D])
        zero_row = at("zero_row", 158720, [P, D])
        agg_r = at("agg_r", 51200, [P, KT, NP], F32R)
        agg_b = at("agg_b", 71680, [P, KT, NP], BF16)
        agg_l = at("agg_l", 81920, [P, KT, NP], BF16)
        dinv_row = at("dinv_row", 176128, [P, NP])
        diag = at("diag", 171008, [P, NP])
        agg_f = at("agg_f", 162816, [P, 2, 512])
        yacc = at("yacc", 105472, [P, NT, D])
        raw1 = at("raw1", 97280, [P, KT, HQ * P])
        raw2 = at("raw2", 101376, [P, HQ, D])
        y_l = at("y_l", 125952, [P, NT, D], F32R)
        W1_r = at("W1_r", 146432, [P, KT, HQ * P], F32R)
        W1_b = at("W1_b", 150528, [P, KT, HQ * P], BF16)
        W1_l = at("W1_l", 152576, [P, KT, HQ * P], BF16)
        W2_r = at("W2_r", 154624, [P, HQ, D], F32R)
        W2_l = at("W2_l", 158720, [P, HQ, D], BF16)
        z_r = at("z_r", 162816, [P, 2, HQ, ZC], F32R)
        z_l = at("z_l", 166912, [P, 2, HQ, ZC], F32R)
        y_r = at("y_r", 171008, [P, NT, D], F32R)
        xt = at("xt", 51200, [P, NT, D])
        zn = at("zn", 71680, [P, 2, D])
        sq = at("sq", 75776, [P, 2, D])
        x_re = at("x_re", 90112, [P, 4, D])
        xn2 = at("xn2", 83968, [P, 2, D])
        xnT = at("xnT", 88064, [P, D])
        LW = NT * X
        gate = at("gate", 71680, [P, 12, LW])
        btab = at("btab", 79360, [1, 32, X])
        etab = at("etab", 81408, [P, X, X])
        oh_place = at("oh_place", 90112, [P, 2 * NT, SLOTS], F16)
        oh_block = at("oh_block", 99072, [P, 2 * NT, 32], F16)
        w_r = at("w_r", 0, [P, 3, 2, KT * 512], F32R)
        w_l = at("w_l", 105472, [P, 3, 2, KT * 512], BF16)
        w_b = at("w_b", 130048, [P, 2, 2, KT * 512], BF16)
        raw = at("raw", 146432, [P, 3, KT * 512])
        xT_r = at("xT_r", 171008, [P, KT, SLOTS], F32R)
        hT_r = at("hT_r", 174592, [P, MT, SLOTS], F32R)
        hT_l = at("hT_l", 181760, [P, MT, SLOTS], F32R)
        hT_b = at("hT_b", 188928, [P, MT, SLOTS], BF16)
        sil = at("sil", 92160, [P, 2, SLOTS])
        h_f = at("h_f", 93952, [P, 2, SLOTS])
        grow = at("grow", 95744, [P, 2, D])
        ysb = at("ysb", 99840, [P, 2, D])
        xT_b = at("xT_b", 83968, [P, KT, SLOTS], BF16)
        xT_l = at("xT_l", 85760, [P, KT, SLOTS], BF16)
        ygath = at("ygath", 0, [P, Y_RING, 2, D])
        z_b = sb("z_b", [P, 2, HQ, ZC], BF16)
        z_f = sb("z_f", [P, 2, ZC])
        assert NZ * ZC == NP and MT * P == 2 * 512 and KT * 512 == (MT // 2) * D

        ident = sb("ident", [P, P])
        minus_half = sb("minus_half", [P, 16])
        ln_sum = sb("ln_sum", [P, NT])
        ln_neg = sb("ln_neg", [P, NT])
        ln_sq = sb("ln_sq", [P, NT])
        ones = sb("ones", [P, P])
        upper = sb("upper", [P, P])
        spans = sb("spans", [P, 2, 2])
        rel = sb("rel", [P, 4, NT])
        tlo = sb("tlo", [P, 2, NT])
        span_c = sb("span_c", [P, 4])
        run_table = sb("run_table", [1, 3, 16], I32)
        mv = sb("mv", [P, NT, 2])
        st6 = sb("st6", [P, NT, 6])
        deg = sb("deg", [P, NT])
        most = sb("most", [P, 4])
        crowded = sb("crowded", [1, 2], I32)
        small = sb("small", [P, 12, NT])
        dinv = sb("dinv", [P, NT])
        scl = sb("scl", [P, NT])
        b1c = sb("b1c", [P, HT])
        b1_now = sb("b1_now", [P, HQ])
        b2b = sb("b2b", [P, D])
        wgs = sb("wgs", [P, KT, X])
        pow_in = sb("pow_in", [P, 2, G + 1])
        pow_out = sb("pow_out", [P, 2, G + 1])
        c16 = sb("c16", [P, LW])
        valid = sb("valid", [P, NT])
        tok = sb("tok", [P, NT])
        routed = sb("routed", [P, (NT + 1) * X], F16)
        upper_h = sb("upper_h", [P, P], F16)
        ones_h = sb("ones_h", [P, P], F16)
        before = sb("before", [P, X, X])
        place = sb("place", [P, SLOTS], F16)
        rank = sb("rank", [P, 2, NT])
        first_block = sb("first_block", [P, 2, NT])
        part = sb("part", [P, 3, 2, NT])
        rt = sb("rt", [P, 10, X])
        slotf = sb("slotf", [P, 2, NT])
        sloti = sb("sloti", [P, 2, NT], I32)
        tops = sb("tops", [P, 8, NT])
        bidx = sb("bidx", [P, 32])
        block_expert = sb("block_expert", [1, 34], I32)
        bef = sb("bef", [1, 34])
        idx_all = sb("idx_all", [P, 2, NIDX], I32)
        credit = sb("credit", [P, 16])
        held = sb("held", [P, 2])
        idx_now = sb("idx_now", [P, 2], I32)
        ps = ctx.enter_context(nc.psum_tensor("ps", [P, 8, 512], F32))

        consts = sem("consts")
        zero_set = sem("zero_set")
        y_zeroed = sem("y_zeroed")
        edge_pad, x_pad, crow_pad = sem("edge_pad"), sem("x_pad"), sem("crow_pad")
        ld_edge, ld_x, ld_w1, ld_w2, ld_small = (sem(n) for n in ("ld_edge", "ld_x", "ld_w1", "ld_w2", "ld_small"))
        ld_xre = [sem(f"ld_xre{i}") for i in range(4)]
        dve = sem("dve")
        edge_rows = sem("edge_rows")
        edge_cols_t = sem("edge_cols_t")
        rel_ready = sem("rel_ready")
        rel_t = sem("rel_t")
        span_ready = sem("span_ready")
        table_t = sem("table_t")
        table_ready = sem("table_ready")
        oh_ready = sem("oh_ready")
        oh_free = sem("oh_free")
        ln_summed, ln_centred, ln_squared = sem("ln_summed"), sem("ln_centred"), sem("ln_squared")
        c_built = sem("c_built")
        c_row = sem("c_row")
        c_trans = sem("c_trans")
        ct_done = sem("ct_done")
        rsqrt_in, rsqrt_out = sem("rsqrt_in"), sem("rsqrt_out")
        scl_ready = sem("scl_ready")
        diag_ready = sem("diag_ready")
        bcast_ready, bcast_read = sem("bcast_ready"), sem("bcast_read")
        xs_made = sem("xs_made")
        xs_round = sem("xs_round")
        xs_ready = sem("xs_ready")
        agg_ps = sem("agg_ps")
        agg_done = sem("agg_done")
        agg_scaled = sem("agg_scaled")
        agg_round = sem("agg_round")
        crowd_ready = sem("crowd_ready")
        crowd_ps = sem("crowd_ps")
        crowd_in = sem("crowd_in")
        ct_round = [sem("ct_round0"), sem("ct_round1")]
        yacc_zero = sem("yacc_zero")
        w1_round, w1_rest = sem("w1_round"), sem("w1_rest")
        w2_round, w2_rest = sem("w2_round"), sem("w2_rest")
        b1_taken = sem("b1_taken")
        z_ps = sem("z_ps")
        z_relu = sem("z_relu")
        z_round = sem("z_round")
        z_done = sem("z_done")
        y_ps = sem("y_ps")
        y_done = sem("y_done")
        y_round = sem("y_round")
        y_split = sem("y_split")
        o_ps = sem("o_ps")
        o_read = sem("o_read")
        sq_out = sem("sq_out")
        xn_done = sem("xn_done")
        xnT_ps = sem("xnT_ps")
        xnT_done = sem("xnT_done")
        gate_ps = sem("gate_ps")
        st_xn = [sem("st_xn0"), sem("st_xn1")]
        exp_in = sem("exp_in")
        exp_out = sem("exp_out")
        routes = sem("routes")
        rank_ps = sem("rank_ps")
        slots_ready = sem("slots_ready")
        blocks_ready = sem("blocks_ready")
        place_ready, slots_ps, rows_known = sem("place_ready"), sem("slots_ps"), sem("rows_known")
        idx_ready = sem("idx_ready")
        gath_a, gath_b = sem("gath_a"), sem("gath_b")
        g_trans = sem("g_trans")
        xT_done = sem("xT_done")
        ld_raw = [sem(f"ld_raw{i}") for i in range(3)]
        prep_act, prep_dve, prep_pool = sem("prep_act"), sem("prep_dve"), sem("prep_pool")
        xT_round = sem("xT_round")
        wo_used = sem("wo_used")
        gu_ps = sem("gu_ps")
        silu_done = sem("silu_done")
        h_done = sem("h_done")
        h_round = sem("h_round")
        h_split = sem("h_split")
        yb_ps = sem("yb_ps")
        yb_done = sem("yb_done")
        st_ya, st_yb = sem("st_ya"), sem("st_yb")
        ygat = [sem(f"ygat{i}") for i in range(Y_RING)]
        comb = sem("comb")
        st_out = sem("st_out")

        HM = M // 2

        def columns(w, half):
            return lambda e: w[bass.ds(e, 1), :, half * HM:(half + 1) * HM].rearrange("o (k p) m -> p (o k) m", p=P)

        def rows(w, half):
            return lambda e: w[bass.ds(e, 1), half * HM:(half + 1) * HM, :].rearrange("o (j p) d -> p (o j) d", p=P)

        W0A, W1A, W0B, W1B = ((m, half, columns(w, half)) for half in (0, 1) for m, w in ((0, w0), (1, w1)))
        WOA, WOB = ((2, half, rows(wo, half)) for half in (0, 1))
        FIRST = [W0A, W1A, W0B, W1B]
        EACH = [WOA, WOB, W0A, W1A, W0B, W1B]
        RAW_SLOTS = 3
        BY_POOL = (WOA, WOB, W1B)
        BY_DVE = (W0A, W1A, W0B, W1B)

        def count(pieces, kinds):
            return sum(p in kinds for p in pieces)

        FREE = [
            lambda b: lambda e: e.wait_ge(wo_used, b + 1),
            lambda b: lambda e: e.wait_ge(yb_ps, b + 1),
            lambda b: lambda e: e.wait_ge(gu_ps, b * MT + MT // 2),
            lambda b: lambda e: e.wait_ge(gu_ps, b * MT + MT // 2),
            lambda b: lambda e: e.wait_ge(gu_ps, b * MT + MT),
            lambda b: lambda e: e.wait_ge(gu_ps, b * MT + MT),
        ]

        CONSTS = 18

        def read_run(engine, t):
            return (engine.value_load(run_table[0:1, 0, bass.ds(t, 1)], min_val=0, max_val=ET - 1),
                    engine.value_load(run_table[0:1, 1, bass.ds(t, 1)], min_val=2, max_val=-(-ET // U)),
                    engine.value_load(run_table[0:1, 2, bass.ds(t, 1)], min_val=0, max_val=(NT - 1) * -(-ET // U)))

        def edge_column(first, i, j):
            return nc.s_assert_within(first + i * U + j, 0, EC - 2, skip_runtime_bounds_check_because="the last group ends at EC or before")

        block = ctx.enter_context(nc.Block())

        @block.sync
        def _(sp):
            sp.wait_ge(edge_pad, 1)
            for q, e in ((2, dst), (0, src)):
                sp.dma_start(erow[:, q, :], e[0:P * P].rearrange("(j p) -> j p", p=P)).then_inc(ld_edge, 16)
                sp.dma_start(erow[0:EFULL, q + 1, :],
                             e[P * P:(P + EFULL) * P].rearrange("(j p) -> j p", p=P)).then_inc(ld_edge, 16)
                if EREST:
                    sp.dma_start(erow[EFULL:EFULL + 1, q + 1, 0:EREST],
                                 e[(P + EFULL) * P:NE].rearrange("(a p) -> a p", a=1)).then_inc(ld_edge, 16)
            sp.wait_ge(x_pad, 1)
            sp.dma_start(x_in[:, 0:NT - 1, :], x[0:(NT - 1) * P, :].rearrange("(t p) d -> p t d", p=P)).then_inc(ld_x, 16)
            sp.dma_start(x_in[0:LAST, NT - 1, :], x[(NT - 1) * P:N, :]).then_inc(ld_x, 16)
            sp.dma_start(b1c[:, :], b1.rearrange("(h p) -> p h", p=P), allow_slow_non_contiguous=True).then_inc(ld_small, 16)
            sp.dma_start(b2b[:, :], b2.rearrange("(a d) -> a d", a=1).broadcast_to([P, D])).then_inc(ld_small, 16)
            sp.dma_start(wgs[:, :, :], wg.rearrange("(k p) e -> p k e", p=P)).then_inc(ld_small, 16)
            sp.wait_ge(zero_set, 1)
            sp.dma_start(y_rows[X * SLOTS:BMAX * SLOTS, :].rearrange("(p j) d -> p j d", p=SLOTS // 2),
                         zero_row[0:SLOTS // 2, :].unsqueeze(1).broadcast_to([SLOTS // 2, 2 * (BMAX - X), D])).then_inc(y_zeroed, 16)
            def load_group(g):
                sp.dma_start(raw1[:, :, :], W1[:, bass.ds(g * (HQ * P), HQ * P)].rearrange("(k p) h -> p k h", p=P)).then_inc(ld_w1, 16)
                sp.dma_start(raw2[:, :, :], W2[bass.ds(g * (HQ * P), HQ * P), :].rearrange("(h p) d -> p h d", p=P)).then_inc(ld_w2, 16)

            sp.wait_ge(xs_made, NT)
            load_group(0)
            with sp.Fori(0, HG - 1) as g:
                sp.wait_ge(w1_rest, g + 1)
                sp.wait_ge(w2_rest, g + 1)
                load_group(g + 1)

            def reload(t):
                n = P if t < NT - 1 else LAST
                sp.dma_start(x_re[0:n, t % 4, :], x[t * P:t * P + n, :]).then_inc(ld_xre[t % 4], 16)

            sp.wait_ge(y_split, NT)
            for t in range(4):
                reload(t)
            sp.wait_ge(y_ps, HG * NT + 1)
            for i in range(RAW_SLOTS):
                sp.dma_start(raw[:, i, :].rearrange("p (k m) -> p k m", m=512), FIRST[i][2](0)).then_inc(ld_raw[i], 16)
            for t in range(NT):
                sp.wait_ge(xn_done, t + 1)
                n = P if t < NT - 1 else LAST
                sp.dma_start(xn_rows[t * P:t * P + n, :], xn2[0:n, t % 2, :]).then_inc(st_xn[t % 2], 16)
                if t + 4 < NT:
                    reload(t + 4)
            for i in range(RAW_SLOTS, len(FIRST)):
                sp.wait_ge(prep_act, i - RAW_SLOTS + 1)
                sp.wait_ge(prep_dve, i - RAW_SLOTS + 1)
                sp.dma_start(raw[:, i % RAW_SLOTS, :].rearrange("p (k m) -> p k m", m=512),
                             FIRST[i][2](0)).then_inc(ld_raw[i % RAW_SLOTS], 16)
            sp.wait_ge(blocks_ready, 1)
            n_blocks = sp.value_load(block_expert[0:1, 33:34], min_val=2, max_val=BMAX)
            with sp.Fori(0, n_blocks) as b:
                own = sp.value_load(block_expert[0:1, bass.ds(b, 1)], min_val=0, max_val=X - 1)
                nxt = sp.value_load(block_expert[0:1, bass.ds(b + 1, 1)], min_val=0, max_val=X - 1)
                for i, piece in enumerate(EACH):
                    slot = (len(FIRST) + i) % RAW_SLOTS
                    before = (FIRST + EACH)[:len(FIRST) + i - RAW_SLOTS + 1]
                    if before[-1] in BY_DVE:
                        sp.wait_ge(prep_dve, b * count(EACH, BY_DVE) + count(before, BY_DVE))
                    if before[-1] in BY_POOL:
                        sp.wait_ge(prep_pool, b * count(EACH, BY_POOL) + count(before, BY_POOL) + 1)
                    sp.dma_start(raw[:, slot, :].rearrange("p (k m) -> p k m", m=512),
                                 piece[2](own if i < 2 else nxt)).then_inc(ld_raw[slot], 16)
            for t in range(NT):
                sp.wait_ge(comb, t + 1)
                n = P if t < NT - 1 else LAST
                sp.dma_start(out[t * P:t * P + n, :], xt[0:n, t, :]).then_inc(st_out, 16)
            sp.wait_ge(st_out, 16 * NT)

        @block.gpsimd
        def _(pool):
            g = nc.gpsimd
            g.memset(erow[:, :, :], NO_NODE).then_inc(edge_pad, 1)
            g.iota(iota_n[:, :], pattern=[[1, NP]], base=0, channel_multiplier=0,
                   allow_small_or_imprecise_dtypes=True).then_inc(consts, 1)
            g.memset(ident[:, :], 0.0).then_inc(consts, 1)
            g.memset(ones[:, :], 1.0).then_inc(consts, 1)
            g.memset(upper[:, :], 1.0).then_inc(consts, 1)
            g.memset(valid[:, :], 1.0).then_inc(consts, 1)
            g.memset(loops[:, :], 0.0).then_inc(consts, 1)
            g.memset(minus_half[:, :], -0.5).then_inc(consts, 1)
            pool.wait_ge(consts, 7)
            g.affine_select(out=ident[:, :], in_=ident[:, :], compare_op=ALU.not_equal, fill=1.0, base=0,
                            pattern=[[-1, P]], channel_multiplier=1).then_inc(consts, 1)
            g.affine_select(out=upper[:, :], in_=upper[:, :], compare_op=ALU.is_ge, fill=0.0, base=-1,
                            pattern=[[1, P]], channel_multiplier=-1).then_inc(consts, 1)
            g.affine_select(out=valid[:, :], in_=valid[:, :], compare_op=ALU.is_ge, fill=0.0, base=N - 1,
                            pattern=[[-P, NT]], channel_multiplier=-1).then_inc(consts, 1)
            pool.wait_ge(consts, 10)
            g.tensor_copy(ident_h, ident[:, :]).then_inc(consts, 1)
            g.memset(ecol[:, :, ET:EC], NO_NODE).then_inc(consts, 1)
            for q in range(2):
                g.iota(tlo[:, q, :], pattern=[[P, NT]], base=q * (P - 1), channel_multiplier=0,
                       allow_small_or_imprecise_dtypes=True).then_inc(consts, 1)
                g.iota(jidx[:, q, :], pattern=[[1 - 2 * q, 256]], base=1 if q == 0 else 256, channel_multiplier=0,
                       allow_small_or_imprecise_dtypes=True).then_inc(consts, 1)
            g.iota(c16[:, :], pattern=[[0, NT], [-1, X]], base=X, channel_multiplier=0,
                   allow_small_or_imprecise_dtypes=True).then_inc(consts, 1)
            g.iota(bidx[:, :], pattern=[[1, 32]], base=0, channel_multiplier=0,
                   allow_small_or_imprecise_dtypes=True).then_inc(consts, 1)
            pool.wait_ge(consts, CONSTS)

            def rsqrt(n, where, value, width):
                pool.wait_ge(rsqrt_in, n)
                g.tensor_tensor(where, value, minus_half[:, 0:width], ALU.pow).then_inc(rsqrt_out, 1)

            g.iota(tok[:, :], pattern=[[P, NT]], base=0, channel_multiplier=1,
                   allow_small_or_imprecise_dtypes=True).then_inc(consts, 1)
            g.iota(place[:, :], pattern=[[1, SLOTS]], base=0, channel_multiplier=0,
                   allow_small_or_imprecise_dtypes=True).then_inc(consts, 1)
            g.memset(before[:, :, :], 1.0).then_inc(consts, 1)
            g.memset(routed[:, :], 0.0).then_inc(consts, 1)
            g.tensor_copy(upper_h[:, :], upper[:, :]).then_inc(consts, 1)
            g.tensor_copy(ones_h[:, :], ones[:, :]).then_inc(consts, 1)
            pool.wait_ge(consts, CONSTS + 6)
            g.tensor_tensor(tok[:, :], tok[:, :], valid[:, :], ALU.mult).then_inc(consts, 1)
            g.affine_select(out=before[:, :, :], in_=before[:, :, :], compare_op=ALU.is_ge, fill=0.0, base=-1,
                            pattern=[[1, X], [-1, X]], channel_multiplier=0).then_inc(consts, 1)

            rsqrt(1, small[:, 0, :], small[:, 1, :], NT)
            rsqrt(2, dinv[:, :], small[:, 2, :], NT)
            pool.wait_ge(agg_ps, KT * len(NCH))
            g.memset(yacc[:, :, :], 0.0).then_inc(yacc_zero, 1)

            for t in range(NT):
                rsqrt(t + 3, pow_out[:, t % 2, :], pow_in[:, t % 2, :], G + 1)
            rsqrt(NT + 3, pow_out[:, :, G], pow_in[:, :, G], 2)

            def hold(c):
                g.tensor_tensor(held[:, c:c + 1], ones[:, 0:1], ones[:, 0:1], ALU.mult)

            pool.wait_ge(slots_ready, 1)
            pool.wait_ge(st_xn[0], 16 * (NT // 2))
            pool.wait_ge(st_xn[1], 16 * (NT // 2))
            pool.wait_ge(blocks_ready, 1)
            n_blocks = pool.value_load(block_expert[0:1, 33:34], min_val=2, max_val=BMAX)

            def fetch(b):
                pool.wait_ge(g_trans, b + 1)
                g.tensor_copy(idx_now[:, 0:1], idx_all[:, 0, bass.ds(b, 1)]).then_inc(idx_ready, 1)
                g.tensor_copy(idx_now[0:SB, 1:2], idx_all[0:SB, 1, bass.ds(b, 1)]).then_inc(idx_ready, 1)
                pool.wait_ge(idx_ready, b * 2 + 2)
                hold(0)
                g.indirect_dma_start(out=grow[:, 0, :], out_offset=None, in_=xn_rows,
                                     in_offset=bass.IndirectOffsetOnAxis(ap=idx_now[:, 0:1], axis=0)).then_inc(gath_a, 16)
                g.indirect_dma_start(out=grow[0:SB, 1, :], out_offset=None, in_=xn_rows,
                                     in_offset=bass.IndirectOffsetOnAxis(ap=idx_now[0:SB, 1:2], axis=0)).then_inc(gath_b, 16)

            def rest(piece, stream, b):
                m, half, _ = piece
                pool.wait_ge(prep_act, b * len(EACH) + stream + 1)
                g.tensor_tensor(w_l[:, m, half, :], raw[:, stream % RAW_SLOTS, :],
                                w_r[:, m, half, :].bitcast(F32), ALU.subtract).then_inc(prep_pool, 1)

            fetch(0)
            rest(W1B, 3, 0)
            with pool.Fori(0, n_blocks) as b:
                fetch(b + 1)
                for i, piece in enumerate(EACH):
                    if piece in BY_POOL:
                        rest(piece, len(FIRST) + i, b)
            pool.wait_ge(rows_known, 1)
            pool.wait_ge(st_ya, n_blocks * 16 + 16)
            pool.wait_ge(st_yb, n_blocks * 16 + 16)
            hold(1)
            for t in range(NT):
                n = P if t < NT - 1 else LAST
                if t >= Y_RING:
                    pool.wait_ge(comb, t - Y_RING + 1)
                for k in range(2):
                    g.indirect_dma_start(out=ygath[0:n, t % Y_RING, k, :], out_offset=None, in_=y_rows,
                                         in_offset=bass.IndirectOffsetOnAxis(ap=sloti[0:n, k, t:t + 1], axis=0)
                                         ).then_inc(ygat[t % Y_RING], 16)

        @block.scalar
        def _(act):
            s = nc.scalar

            def c_tile(t, par):
                act.wait_ge(c_built, t + 1)
                if not isinstance(t, int) or t >= 2:
                    act.wait_ge(c_trans, t * 3 - 3)
                s.activation(crow[:, par, 0:N], ps[:, 3 * par:3 * par + 3, :].rearrange("p a n -> p (a n)")[:, 0:N],
                             ACT.Copy, accum_out=deg[:, bass.ds(t, 1)]).then_inc(c_row, 1)

            def c_cols(t):
                for q, n in enumerate((4, 4, 2)):
                    act.wait_ge(c_trans, t * 3 + q + 1)
                    s.activation(CT[:, 4 * q:4 * q + n, bass.ds(t * P, P)],
                                 ps[:, 6 + q % 2, 0:n * P].rearrange("p (a n) -> p a n", a=n), ACT.Copy).then_inc(ct_done, 1)

            act.wait_ge(crow_pad, 1)
            c_tile(0, 0)
            act.wait_ge(ld_x, 32)
            for t in range(NT):
                s.activation(ln_rest[:, 0, t, :], x_in[:, t, :], ACT.Copy, accum_out=ln_sum[:, t:t + 1]).then_inc(ln_summed, 1)
            act.wait_ge(ln_summed, NT)
            s.activation(ln_neg[:, :], ln_sum[:, :], ACT.Copy, scale=-1.0 / D).then_inc(ln_centred, 1)
            act.wait_ge(ln_centred, 1)
            for t in range(NT):
                s.activation(ln_rest[:, 1, t, :], x_in[:, t, :], ACT.Square, bias=ln_neg[:, t:t + 1],
                             accum_out=ln_sq[:, t:t + 1]).then_inc(ln_squared, 1)
            c_tile(1, 1)
            c_cols(0)
            with act.Fori(0, NT // 2 - 1) as i:
                c_tile(i * 2 + 2, 0)
                c_cols(i * 2 + 1)
                c_tile(i * 2 + 3, 1)
                c_cols(i * 2 + 2)
            c_cols(NT - 1)
            act.wait_ge(crowd_ready, 1)
            is_crowded = act.value_load(crowded[0:1, 0:1], min_val=0, max_val=1)

            def round_counts(chunks):
                with act.If(is_crowded == 0):
                    for lo, w in chunks:
                        s.activation(CTr[:, 0:NT // 2, lo:lo + w], CT[:, 0:NT // 2, lo:lo + w], ACT.Copy).then_inc(ct_round[0], 1)

            round_counts(NCH[:1])
            for t in range(NT):
                act.wait_ge(xs_made, t + 1)
                s.activation(xs_r[:, t, :], xs_f[:, t % 3, :], ACT.Copy).then_inc(xs_round, 1)
            round_counts(NCH[1:])

            def round_w1(g):
                act.wait_ge(ld_w1, g * 16 + 16)
                act.wait_ge(z_ps, g * (NZ * HQ) + 1)
                s.activation(W1_r[:, :, :], raw1[:, :, :], ACT.Copy).then_inc(w1_round, 1)

            def round_w2(g):
                act.wait_ge(ld_w2, g * 16 + 16)
                act.wait_ge(y_ps, g * NT + 1)
                s.activation(W2_r[:, :, :], raw2[:, :, :], ACT.Copy).then_inc(w2_round, 1)

            act.wait_ge(xs_ready, NT)
            round_w1(0)
            round_w2(0)
            n = 0
            for lo, w in NCH:
                for m in range(KT):
                    act.wait_ge(agg_scaled, n + 1)
                    s.activation(agg_r[:, m, lo:lo + w], agg_f[:, n % 2, 0:w], ACT.Copy).then_inc(agg_round, 1)
                    n += 1

            def take_b1(g):
                s.activation(b1_now[:, :], b1c[:, bass.ds(g * HQ, HQ)], ACT.Copy).then_inc(b1_taken, 1)
                act.wait_ge(b1_taken, g + 1)

            def hidden(g, c):
                for h in range(HQ):
                    n = g * (NZ * HQ) + (c * HQ + h)
                    act.wait_ge(z_done, n + 1)
                    act.wait_ge(z_ps, n + 2)
                    s.activation(z_f[:, h, :], ps[:, (c * HQ + h) % 4, 0:ZC], ACT.Relu,
                                 bias=b1_now[:, h:h + 1]).then_inc(z_relu, 1)
                    act.wait_ge(z_relu, n + 1)
                    s.activation(z_r[:, c % 2, h, :], z_f[:, h, :], ACT.Copy).then_inc(z_round, 1)

            act.wait_ge(ld_small, 48)
            with act.Fori(0, HG - 1) as g:
                take_b1(g)
                for c in range(NZ):
                    hidden(g, c)
                round_w1(g + 1)
                round_w2(g + 1)
            take_b1(HG - 1)

            def round_y(c):
                for t in (2 * c, 2 * c + 1):
                    act.wait_ge(y_done, (HG - 1) * NT + t + 2)
                    s.activation(y_r[:, t, :], yacc[:, t, :], ACT.Copy, scale=dinv[:, t:t + 1]).then_inc(y_round, 1)

            hidden(HG - 1, 0)
            for c in range(1, NZ):
                hidden(HG - 1, c)
                round_y(c - 1)
            round_y(NZ - 1)
            for t in range(NT + 4):
                if t < NT:
                    act.wait_ge(o_read, t + 1)
                    s.activation(sq[:, t % 2, :], zn[:, t % 2, :], ACT.Square).then_inc(sq_out, 1)
                if t >= 4:
                    act.wait_ge(xnT_ps, t - 3)
                    s.activation(xnT[:, :], ps[:, 3 + t % 2, :], ACT.Copy).then_inc(xnT_done, 1)
            act.wait_ge(exp_in, 1)
            s.activation(tops[:, 3, :], tops[:, 2, :], ACT.Exp).then_inc(exp_out, 1)

            act.wait_ge(blocks_ready, 1)
            n_blocks = act.value_load(block_expert[0:1, 33:34], min_val=2, max_val=BMAX)

            def round_piece(piece, stream, b, free, part=None):
                m, half, _ = piece
                slot = stream % RAW_SLOTS
                if part in (None, 0):
                    act.wait_ge(ld_raw[slot], (b * (len(EACH) // RAW_SLOTS) + stream // RAW_SLOTS + 1) * 16)
                    free(act)
                lo, hi = (0, KT * 512) if part is None else (part * KT * 256, (part + 1) * KT * 256)
                ins = s.activation(w_r[:, m, half, lo:hi], raw[:, slot, lo:hi], ACT.Copy)
                if part in (None, 1):
                    ins.then_inc(prep_act, 1)

            def take_xT(b):
                act.wait_ge(g_trans, b + 2)
                s.activation(xT_r[:, :, 0:P], ps[:, 0, :].rearrange("p (k n) -> p k n", k=KT), ACT.Copy)
                s.activation(xT_r[:, :, P:SLOTS], ps[:, 1, 0:KT * SB].rearrange("p (k n) -> p k n", k=KT), ACT.Copy).then_inc(xT_round, 1)

            for i, piece in enumerate(FIRST):
                round_piece(piece, i, 0, lambda e: None)
            take_xT(0)
            with act.Fori(0, n_blocks) as b:
                for m in range(MT):
                    act.wait_ge(gu_ps, b * MT + m + 1)
                    s.activation(sil[:, m % 2, :], ps[:, 2 + m % 2, 0:SLOTS], ACT.Silu).then_inc(silu_done, 1)
                    round_piece(EACH[m // 2], len(FIRST) + m // 2, b, FREE[m // 2](b), m % 2)
                    act.wait_ge(h_done, b * MT + m + 3)
                    s.activation(hT_r[:, m, :], h_f[:, m % 2, :], ACT.Copy).then_inc(h_round, 1)
                take_xT(b + 1)
                for i in (4, 5):
                    round_piece(EACH[i], len(FIRST) + i, b, FREE[i](b))
                act.wait_ge(yb_ps, b + 2)
                act.wait_ge(st_ya, b * 16 + 16)
                s.activation(ysb[:, 0, :], ps[:, 6, :], ACT.Copy).then_inc(yb_done, 1)
                act.wait_ge(yb_done, b * 2 + 4)
                act.dma_start(y_rows[bass.ds(b * SLOTS, P), :], ysb[:, 0, :]).then_inc(st_ya, 16)
                act.dma_start(y_rows[bass.ds(b * SLOTS + P, SB), :], ysb[0:SB, 1, :]).then_inc(st_yb, 16)

        @block.vector
        def _(v):
            V = nc.vector
            steps = [0]

            def then(ins):
                steps[0] += 1
                ins.then_inc(dve, 1)
                v.wait_ge(dve, steps[0])

            V.memset(x_in[:, NT - 1, :], 0.0).then_inc(x_pad, 1)
            V.memset(crow[:, 0, N:NP], 0.0)
            V.memset(crow[:, 1, N:NP], 0.0).then_inc(crow_pad, 1)
            V.memset(zero_row[:, :], 0.0).then_inc(zero_set, 1)
            V.memset(st6[:, :, :], 0.0).then_inc(h_done, 2)
            V.memset(run_table[0:1, :, :], 0).then_inc(oh_free, 4)
            for j, (free, n) in enumerate(((c_row, 2), (ct_done, 1), (g_trans, 1), (yb_done, 2), (st_ya, 16), (st_yb, 16),
                                            (y_done, 1), (wo_used, 1), (yb_ps, 1), (prep_pool, 1), (z_ps, 1), (z_done, 2), (y_ps, 1))):
                V.memset(credit[:, j:j + 1], 0.0).then_inc(free, n)
            v.wait_ge(ld_edge, 16 * (6 if EREST else 4))
            V.tensor_copy(erowf[:, :, :], erow[:, :, :]).then_inc(edge_rows, 1)
            v.wait_ge(edge_rows, 1)
            for q in range(2):
                V.tensor_reduce(spans[:, 0, q:q + 1], erowf[:, 2 + q, :], AX_X, ALU.min)
                then(V.tensor_reduce(spans[:, 1, q:q + 1], erowf[:, 2 + q, :], AX_X, ALU.max))
            v.wait_ge(consts, CONSTS)
            for q in range(2):
                V.tensor_scalar(rel[:, q, :], tlo[:, 1, :], spans[:, 0, q:q + 1], None, ALU.is_ge)
                then(V.tensor_scalar(rel[:, 2 + q, :], tlo[:, 0, :], spans[:, 1, q:q + 1], None, ALU.is_le))
            V.tensor_tensor(rel[:, 0:2, :], rel[:, 0:2, :], rel[:, 2:4, :], ALU.mult).then_inc(rel_ready, 1)
            v.wait_ge(edge_cols_t, 1)
            V.tensor_copy(ecol[:, 0, 0:ET], ps[:, 0, 0:ET])
            then(V.tensor_copy(ecol[:, 1, 0:ET], ps[:, 0, 2 * P:2 * P + ET]))
            v.wait_ge(rel_t, 1)
            for q in range(2):
                then(V.tensor_tensor(jval[0:NT, q, 0:ET], ps[0:NT, 1, 0:ET], jidx[0:NT, q, 0:ET], ALU.mult))
                then(V.tensor_reduce(span_c[0:NT, q:q + 1], jval[0:NT, q, 0:ET], AX_X, ALU.max))
            then(V.tensor_scalar(span_c[0:NT, 1:2], span_c[0:NT, 1:2], -1.0, 256.0, ALU.mult, ALU.add))
            then(V.tensor_scalar(span_c[0:NT, 1:2], span_c[0:NT, 1:2], float(ET - 1), None, ALU.min))
            then(V.tensor_tensor(span_c[0:NT, 2:3], span_c[0:NT, 0:1], span_c[0:NT, 1:2], ALU.subtract))
            then(V.tensor_scalar(span_c[0:NT, 2:3], span_c[0:NT, 2:3], U + 1.0, U / 2 - 0.5, ALU.max, ALU.add))
            then(V.tensor_scalar(span_c[0:NT, 3:4], span_c[0:NT, 2:3], 1.0 / U, ROUND, ALU.mult, ALU.add))
            V.tensor_scalar(span_c[0:NT, 2:3], span_c[0:NT, 3:4], -ROUND, None, ALU.add).then_inc(span_ready, 1)
            v.wait_ge(table_t, 1)
            V.tensor_copy(run_table[0:1, :, 0:NT], ps[0:1, 1, 0:48].rearrange("p (a n) -> p a n", a=3)[:, :, 0:NT]).then_inc(table_ready, 1)
            v.wait_ge(table_ready, 1)

            then(V.tensor_copy(dst_h[:, :], ecol[:, 1, :]))
            with v.Fori(0, NT) as t:
                first, groups, base = read_run(v, t)
                with v.Fori(0, groups) as i:
                    g = base + i
                    for j in range(0, U, 2):
                        v.wait_ge(oh_free, g * 2 + (j // 2 + 1))
                        V.tensor_tensor(oh_dst[:, bass.ds(g % 2 * (U * P) + j * P, 2 * P)].rearrange("p (j n) -> p j n", j=2),
                                        iota_n[:, bass.ds(t * P, P)].unsqueeze(1).broadcast_to([P, 2, P]),
                                        dst_h[:, bass.ds(edge_column(first, i, j), 2)].unsqueeze(2).broadcast_to([P, 2, P]),
                                        ALU.is_equal)
                        for k in (j, j + 1):
                            last = V.tensor_scalar(oh_src[:, bass.ds(g % 2 * (U * NP) + k * NP, N)], iota_n[:, 0:N],
                                                   ecol[:, 0, bass.ds(edge_column(first, i, k), 1)], None, ALU.is_equal)
                        last.then_inc(oh_ready, 1)
            v.wait_ge(ln_squared, NT)
            V.tensor_scalar(small[:, 1, :], ln_sq[:, :], 1.0 / D, LN_EPS, ALU.mult, ALU.add).then_inc(rsqrt_in, 1)
            v.wait_ge(c_row, NT + 2)
            V.tensor_reduce(most[:, 0:1], deg[:, :], AX_X, ALU.max).then_inc(crowd_in, 1)
            V.tensor_scalar(small[:, 2, :], deg[:, :], 1.0, None, ALU.max).then_inc(rsqrt_in, 1)
            v.wait_ge(rsqrt_out, 2)
            for t in range(NT):
                V.tensor_scalar(diag[:, t * P:(t + 1) * P], ident[:, :], dinv[:, t:t + 1], None,
                                ALU.mult).then_inc(diag_ready, 1)
            V.tensor_tensor(scl[:, :], dinv[:, :], small[:, 0, :], ALU.mult).then_inc(scl_ready, 1)
            v.wait_ge(crowd_ps, 1)
            then(V.tensor_reduce(most[0:1, 1:2], ps[0:1, 0, 0:P], AX_X, ALU.max))
            then(V.tensor_scalar(most[0:1, 2:3], most[0:1, 1:2], float(COUNT_MAX), None, ALU.is_gt))
            V.tensor_copy(crowded[0:1, 0:1], most[0:1, 2:3]).then_inc(crowd_ready, 1)

            def make_xs(t):
                if t >= 3:
                    v.wait_ge(xs_ready, t - 2)
                V.tensor_scalar(xs_f[:, t % 3, :], x_in[:, t, :], ln_neg[:, t:t + 1], scl[:, t:t + 1], ALU.add,
                                ALU.mult).then_inc(xs_made, 1)

            def split_xs(t):
                v.wait_ge(xs_round, t + 1)
                V.tensor_tensor(xs_l[:, t, :], xs_f[:, t % 3, :], xs_r[:, t, :].bitcast(F32), ALU.subtract).then_inc(xs_ready, 1)

            v.wait_ge(scl_ready, 1)
            v.wait_ge(c_built, NT)
            make_xs(0)
            for t in range(NT):
                if t + 1 < NT:
                    make_xs(t + 1)
                split_xs(t)
                if t == 2:
                    v.wait_ge(ct_done, 3 * NT + 1)
                    v.wait_ge(crowd_ready, 1)
                    is_crowded = v.value_load(crowded[0:1, 0:1], min_val=0, max_val=1)
                    with v.If(is_crowded == 0):
                        V.tensor_copy(CTr[:, NT // 2:NT, 0:NCH[0][1]], CT[:, NT // 2:NT, 0:NCH[0][1]]).then_inc(ct_round[1], 1)
            with v.If(is_crowded == 0):
                for lo, w in NCH[1:]:
                    V.tensor_copy(CTr[:, NT // 2:NT, lo:lo + w], CT[:, NT // 2:NT, lo:lo + w]).then_inc(ct_round[1], 1)
            v.wait_ge(bcast_ready, 1)
            V.tensor_copy(dinv_row[:, :], ps[:, 4:7, :].rearrange("p a n -> p (a n)")[:, 0:NP]).then_inc(bcast_read, 1)

            def rest_w1(g):
                v.wait_ge(w1_round, g + 1)
                V.tensor_copy(W1_b[:, :, :], raw1[:, :, :])
                V.tensor_tensor(W1_l[:, :, :], raw1[:, :, :], W1_r[:, :, :].bitcast(F32), ALU.subtract).then_inc(w1_rest, 1)

            def rest_w2(g):
                v.wait_ge(w2_round, g + 1)
                V.tensor_tensor(W2_l[:, :, :], raw2[:, :, :], W2_r[:, :, :].bitcast(F32), ALU.subtract).then_inc(w2_rest, 1)

            v.wait_ge(y_zeroed, 16)
            rest_w1(0)
            rest_w2(0)
            v.wait_ge(bcast_read, 1)
            n = 0
            for lo, w in NCH:
                for m in range(KT):
                    v.wait_ge(agg_ps, n + 1)
                    V.tensor_tensor(agg_f[:, n % 2, 0:w], ps[:, n % 8, 0:w], dinv_row[:, lo:lo + w],
                                    ALU.mult).then_inc(agg_scaled, 1)
                    v.wait_ge(agg_scaled, n + 1)
                    V.tensor_copy(agg_b[:, m, lo:lo + w], agg_f[:, n % 2, 0:w])
                    v.wait_ge(agg_round, n + 1)
                    V.tensor_tensor(agg_l[:, m, lo:lo + w], agg_f[:, n % 2, 0:w], agg_r[:, m, lo:lo + w].bitcast(F32),
                                    ALU.subtract).then_inc(agg_done, 1)
                    n += 1

            def hidden(g, c):
                for h in range(HQ):
                    n = g * (NZ * HQ) + (c * HQ + h)
                    v.wait_ge(z_relu, n + 1)
                    V.tensor_copy(z_b[:, c % 2, h, :], z_f[:, h, :])
                    v.wait_ge(z_round, n + 1)
                    V.tensor_tensor(z_l[:, c % 2, h, :], z_f[:, h, :], z_r[:, c % 2, h, :].bitcast(F32),
                                    ALU.subtract).then_inc(z_done, 1)

            def add_up(g, c):
                for t in (2 * c, 2 * c + 1):
                    v.wait_ge(y_ps, g * NT + (t + 2))
                    V.tensor_tensor(yacc[:, t, :], ps[:, 4 + t % 4, :], yacc[:, t, :], ALU.add).then_inc(y_done, 1)
                    if isinstance(g, int):
                        v.wait_ge(y_round, t + 1)
                        V.scalar_tensor_tensor(y_l[:, t, :], yacc[:, t, :], dinv[:, t:t + 1], y_r[:, t, :].bitcast(F32),
                                               ALU.mult, ALU.subtract).then_inc(y_split, 1)

            v.wait_ge(yacc_zero, 1)
            with v.Fori(0, HG - 1) as g:
                hidden(g, 0)
                for c in range(1, NZ):
                    hidden(g, c)
                    add_up(g, c - 1)
                rest_w1(g + 1)
                add_up(g, NZ - 1)
                rest_w2(g + 1)
            hidden(HG - 1, 0)
            for c in range(1, NZ):
                hidden(HG - 1, c)
                add_up(HG - 1, c - 1)
            add_up(HG - 1, NZ - 1)
            v.wait_ge(ld_small, 48)

            def take_z(t):
                v.wait_ge(o_ps, t + 1)
                V.scalar_tensor_tensor(zn[:, t % 2, :], ps[:, t % 3, :], dinv[:, t:t + 1], b2b[:, :], ALU.mult,
                                       ALU.add).then_inc(o_read, 1)

            def make_xn(t):
                if t >= 2:
                    v.wait_ge(st_xn[t % 2], 16 * (t // 2))
                    v.wait_ge(xnT_ps, t - 1)
                V.tensor_scalar(xn2[:, t % 2, :], xt[:, t, :], mv[:, t, 0:1], pow_out[:, t % 2, G:G + 1], ALU.subtract,
                                ALU.mult).then_inc(xn_done, 1)

            def statistics(t):
                then(V.bn_stats(st6[:, t, :], xt[:, t, :]))
                then(V.bn_aggr(mv[:, t, :], st6[:, t, :]))
                return V.tensor_scalar(pow_in[:, t % 2, G:G + 1], mv[:, t, 1:2], LN_EPS, None, ALU.add)

            V.memset(pow_in[:, :, :], 1.0)
            take_z(0)
            for t in range(NT):
                z = zn[:, t % 2, :]
                groups = z.rearrange("p (g f) -> p g f", g=G)
                v.wait_ge(sq_out, t + 1)
                then(V.tensor_reduce(pow_in[:, t % 2, 0:G], sq[:, t % 2, :].rearrange("p (g f) -> p g f", g=G), AX_X, ALU.add))
                V.tensor_scalar(pow_in[:, t % 2, 0:G], pow_in[:, t % 2, 0:G], NORM_EPS ** 2, None, ALU.max).then_inc(rsqrt_in, 1)
                if t + 1 < NT:
                    take_z(t + 1)
                if t >= 1:
                    statistics(t - 1)
                v.wait_ge(rsqrt_out, t + 3)
                if t >= 2:
                    make_xn(t - 2)
                then(V.tensor_tensor(groups, groups, pow_out[:, t % 2, 0:G].unsqueeze(2).broadcast_to([P, G, GROUP]), ALU.mult))
                v.wait_ge(ld_xre[t % 4], 16 * (t // 4 + 1))
                then(V.tensor_tensor(xt[:, t, :], x_re[:, t % 4, :], z, ALU.add))
            statistics(NT - 1).then_inc(rsqrt_in, 1)
            v.wait_ge(rsqrt_out, NT + 3)
            make_xn(NT - 2)
            make_xn(NT - 1)

            v.wait_ge(gate_ps, NT)
            g3 = lambda j: gate[:, j, :].rearrange("p (t e) -> p t e", e=X)
            c3 = c16[:, :].rearrange("p (t e) -> p t e", e=X)
            over = lambda ap: ap.unsqueeze(2).broadcast_to([P, NT, X])
            then(V.tensor_copy(gate[:, 0, :], ps[:, 5, 0:LW]))
            for k in range(2):
                then(V.tensor_reduce(tops[:, k, :], g3(k), AX_X, ALU.max))
                then(V.tensor_tensor(g3(2), g3(k), over(tops[:, k, :]), ALU.is_equal))
                then(V.tensor_tensor(g3(3), g3(2), c3, ALU.mult))
                then(V.tensor_reduce(tops[:, 7, :], g3(3), AX_X, ALU.max))
                then(V.tensor_tensor(g3(4 + k), c3, over(tops[:, 7, :]), ALU.is_equal))
                if k == 0:
                    then(V.scalar_tensor_tensor(gate[:, 1, :], gate[:, 4, :], -3.0e38, gate[:, 0, :], ALU.mult, ALU.add))
            V.tensor_tensor(tops[:, 2, :], tops[:, 1, :], tops[:, 0, :], ALU.subtract).then_inc(exp_in, 1)
            then(V.tensor_tensor(gate[:, 6, :], gate[:, 4, :], gate[:, 5, :], ALU.add))
            V.tensor_tensor(routed[:, 0:LW].rearrange("p (t e) -> p t e", e=X), g3(6), over(valid[:, :]), ALU.mult).then_inc(routes, 1)
            v.wait_ge(exp_out, 1)
            then(V.tensor_scalar(tops[:, 4, :], tops[:, 3, :], 1.0, None, ALU.add))
            then(V.reciprocal(tops[:, 5, :], tops[:, 4, :]))
            then(V.tensor_tensor(tops[:, 6, :], tops[:, 5, :], tops[:, 3, :], ALU.mult))
            twice = lambda ap: ap.unsqueeze(1).broadcast_to([P, 2, LW])
            chosen = gate[:, 4:6, :]
            g4 = lambda ap: ap.rearrange("p k (t e) -> p k t e", e=X)
            v.wait_ge(rank_ps, 1)
            then(V.tensor_copy(rt[:, 0, :], ps[:, 6, LW:LW + X]))
            then(V.tensor_tensor(gate[:, 7:9, :], chosen, twice(ps[:, 6, 0:LW]), ALU.mult))
            then(V.tensor_reduce(rank[:, :, :], g4(gate[:, 7:9, :]), AX_X, ALU.add))

            def rounded(out, value, tmp):
                then(V.tensor_scalar(tmp, value, ROUND, None, ALU.add))
                then(V.tensor_scalar(out, tmp, -ROUND, None, ALU.add))

            then(V.tensor_scalar(rt[:, 1, :], rt[:, 0, :], 1.0 / SLOTS, 0.5 - 0.5 / SLOTS, ALU.mult, ALU.add))
            rounded(rt[:, 2, :], rt[:, 1, :], rt[:, 3, :])
            then(V.tensor_scalar(rt[:, 2, :], rt[:, 2, :], 1.0, None, ALU.max))
            then(V.tensor_tensor(etab[:, :, :], before[:, :, :], rt[:, 2, :].unsqueeze(1).broadcast_to([P, X, X]), ALU.mult))
            then(V.tensor_reduce(rt[:, 4, :], etab[:, :, :], AX_X, ALU.add))
            then(V.tensor_tensor(g4(gate[:, 7:9, :]), g4(chosen), rt[:, 4, :].unsqueeze(1).unsqueeze(1).broadcast_to([P, 2, NT, X]), ALU.mult))
            then(V.tensor_reduce(first_block[:, :, :], g4(gate[:, 7:9, :]), AX_X, ALU.add))
            then(V.tensor_scalar(part[:, 0, :, :], rank[:, :, :], 1.0 / SLOTS, 0.5 / SLOTS - 0.5, ALU.mult, ALU.add))
            rounded(part[:, 0, :, :], part[:, 0, :, :], part[:, 1, :, :])
            then(V.tensor_tensor(part[:, 1, :, :], first_block[:, :, :], part[:, 0, :, :], ALU.add))
            then(V.scalar_tensor_tensor(part[:, 2, :, :], part[:, 0, :, :], -float(SLOTS), rank[:, :, :], ALU.mult, ALU.add))
            for t in range(NT):
                for k in range(2):
                    j = 2 * t + k
                    V.tensor_scalar(oh_place[:, j, :], place[:, :], part[:, 2, k, t:t + 1], None, ALU.is_equal)
                    V.tensor_scalar(oh_block[:, j, :], bidx[:, :], part[:, 1, k, t:t + 1], tok[:, t:t + 1], ALU.is_equal,
                                    ALU.mult).then_inc(place_ready, 1)
            then(V.tensor_tensor(rt[:, 5, :], rt[:, 4, :], rt[:, 2, :], ALU.add))
            ends = rt[:, 5, :]
            bt = btab[:, :, :]
            then(V.tensor_tensor(bt, bidx[0:1, :].unsqueeze(2).broadcast_to([1, 32, X]),
                                 ends[0:1, :].unsqueeze(1).broadcast_to([1, 32, X]), ALU.is_ge))
            then(V.tensor_reduce(bef[0:1, 0:32], bt, AX_X, ALU.add))
            then(V.tensor_scalar(bef[0:1, 0:32], bef[0:1, 0:32], float(X - 1), None, ALU.min))
            then(V.tensor_copy(bef[0:1, 32:33], ends[0:1, X - 1:X]))
            then(V.tensor_copy(bef[0:1, 33:34], ends[0:1, X - 1:X]))
            V.tensor_copy(block_expert[0:1, :], bef[0:1, :]).then_inc(blocks_ready, 1)
            v.wait_ge(slots_ps, 1)
            V.tensor_copy(idx_all[:, 0, :], ps[:, 7, 0:NIDX])
            V.tensor_copy(idx_all[0:SB, 1, :], ps[0:SB, 1, 0:NIDX]).then_inc(slots_ready, 1)
            then(V.scalar_tensor_tensor(slotf[:, :, :], first_block[:, :, :], float(SLOTS), rank[:, :, :], ALU.mult, ALU.add))
            V.tensor_copy(sloti[:, :, :], slotf[:, :, :]).then_inc(rows_known, 1)
            v.wait_ge(blocks_ready, 1)
            n_blocks = v.value_load(block_expert[0:1, 33:34], min_val=2, max_val=BMAX)

            def rest_piece(piece, stream, b, free, part=None):
                m, half, _ = piece
                lo, hi = (0, KT * 512) if part is None else (part * KT * 256, (part + 1) * KT * 256)
                if part in (None, 0):
                    v.wait_ge(ld_raw[stream % RAW_SLOTS], (b * (len(EACH) // RAW_SLOTS) + stream // RAW_SLOTS + 1) * 16)
                    free(v)
                ins = V.tensor_copy(w_b[:, m, half, lo:hi], raw[:, stream % RAW_SLOTS, lo:hi])
                if piece not in BY_POOL:
                    if part in (None, 1):
                        v.wait_ge(prep_act, b * len(EACH) + stream + 1)
                    if part is None:
                        ins = V.tensor_tensor(w_l[:, m, half, :], raw[:, stream % RAW_SLOTS, :],
                                              w_r[:, m, half, :].bitcast(F32), ALU.subtract)
                    if part == 1:
                        ins = V.tensor_tensor(w_l[:, m, half, :], raw[:, stream % RAW_SLOTS, :],
                                              w_r[:, m, half, :].bitcast(F32), ALU.subtract)
                if part in (None, 1):
                    ins.then_inc(prep_dve, 1)

            def take_xT(b):
                v.wait_ge(xT_round, b + 1)
                V.tensor_copy(xT_b[:, :, :], xT_r[:, :, :].bitcast(F32))
                V.tensor_tensor(xT_l[:, :, 0:P], ps[:, 0, :].rearrange("p (k n) -> p k n", k=KT),
                                xT_r[:, :, 0:P].bitcast(F32), ALU.subtract)
                V.tensor_tensor(xT_l[:, :, P:SLOTS], ps[:, 1, 0:KT * SB].rearrange("p (k n) -> p k n", k=KT),
                                xT_r[:, :, P:SLOTS].bitcast(F32), ALU.subtract).then_inc(xT_done, 1)

            for i, piece in enumerate(FIRST):
                rest_piece(piece, i, 0, lambda e: None)
            take_xT(0)
            with v.Fori(0, n_blocks) as b:
                for m in range(MT):
                    v.wait_ge(silu_done, b * MT + m + 1)
                    V.tensor_tensor(h_f[:, m % 2, :], ps[:, 4 + m % 2, 0:SLOTS], sil[:, m % 2, :], ALU.mult).then_inc(h_done, 1)
                    if m >= 4:
                        rest_piece(EACH[m // 2], len(FIRST) + m // 2, b, FREE[m // 2](b), m % 2)
                    v.wait_ge(h_done, b * MT + m + 3)
                    V.tensor_copy(hT_b[:, m, :], h_f[:, m % 2, :])
                    v.wait_ge(h_round, b * MT + m + 1)
                    V.tensor_tensor(hT_l[:, m, :], h_f[:, m % 2, :], hT_r[:, m, :].bitcast(F32), ALU.subtract).then_inc(h_split, 1)
                take_xT(b + 1)
                for i in (4, 5):
                    rest_piece(EACH[i], len(FIRST) + i, b, FREE[i](b))
                v.wait_ge(yb_ps, b + 2)
                v.wait_ge(st_yb, b * 16 + 16)
                V.tensor_copy(ysb[0:SB, 1, :], ps[0:SB, 7, :]).then_inc(yb_done, 1)
            for t in range(NT):
                n = P if t < NT - 1 else LAST
                v.wait_ge(ygat[t % Y_RING], 32 * (t // Y_RING + 1))
                then(V.scalar_tensor_tensor(xt[0:n, t, :], ygath[0:n, t % Y_RING, 0, :], tops[0:n, 5, t:t + 1],
                                            xt[0:n, t, :], ALU.mult, ALU.add))
                V.scalar_tensor_tensor(xt[0:n, t, :], ygath[0:n, t % Y_RING, 1, :], tops[0:n, 6, t:t + 1],
                                       xt[0:n, t, :], ALU.mult, ALU.add).then_inc(comb, 1)

        @block.tensor
        def _(pe):
            T = nc.tensor
            pe.wait_ge(consts, CONSTS)
            pe.wait_ge(edge_rows, 1)
            for q in range(4):
                last = T.transpose(ps[:, 0, q * P:(q + 1) * P], erowf[:, q, :], ident[:, :])
            last.then_inc(edge_cols_t, 1)
            pe.wait_ge(rel_ready, 1)
            T.transpose(ps[0:NT, 1, 0:P], rel[:, 0, :], ident[:, :])
            T.transpose(ps[0:NT, 1, P:P + EB], rel[0:EB, 1, :], ident[0:EB, 0:EB]).then_inc(rel_t, 1)
            pe.wait_ge(span_ready, 1)
            for j, (c, rhs) in enumerate(((1, ident), (2, ident), (2, upper))):
                last = T.matmul(ps[0:1, 1, 16 * j:16 * j + NT], span_c[0:NT, c:c + 1], rhs[0:NT, 0:NT],
                                start=True, stop=True)
            last.then_inc(table_t, 1)
            pe.wait_ge(table_ready, 1)

            def count_edges(par, g, start):
                for j in range(U):
                    if j % 2 == 0:
                        pe.wait_ge(oh_ready, g * 2 + (j // 2 + 1))
                    for q, (lo, w) in enumerate(CCH):
                        last = T.matmul(ps[:, 3 * par + q, 0:w], oh_dst[:, bass.ds(g % 2 * (U * P) + j * P, P)],
                                        oh_src[:, bass.ds(g % 2 * (U * NP) + (j * NP + lo), w)],
                                        start=start and j == 0, stop=False)
                    if j % 2 == 1:
                        last.then_inc(oh_free, 1)

            def run_of(t):
                groups = pe.value_load(run_table[0:1, 1, bass.ds(t, 1)], min_val=2, max_val=-(-ET // U))
                base = pe.value_load(run_table[0:1, 2, bass.ds(t, 1)], min_val=0, max_val=(NT - 1) * -(-ET // U))
                return groups, base

            def build(t, par, run):
                groups, base = run
                pe.wait_ge(c_row, t + 1)
                count_edges(par, base, True)
                with pe.Fori(1, groups) as i:
                    count_edges(par, base + i, False)
                for q, (lo, w) in enumerate(CCH):
                    last = T.matmul(ps[:, 3 * par + q, 0:w], ident_h, loops[:, bass.ds(NP - P + lo - t * P, w)],
                                    start=False, stop=True)
                last.then_inc(c_built, 1)

            def turn(t, par):
                pe.wait_ge(c_row, t + 3)
                for q, n in enumerate((4, 4, 2)):
                    pe.wait_ge(ct_done, t * 3 + max(q, 1))
                    for a in range(n):
                        k = 4 * q + a
                        last = T.transpose(ps[:, 6 + q % 2, a * P:(a + 1) * P], crow[:, par, k * P:(k + 1) * P], ident[:, :])
                    last.then_inc(c_trans, 1)

            build(0, 0, run_of(0))
            build(1, 1, run_of(1))
            with pe.Fori(0, NT // 2 - 1) as i:
                for par in (0, 1):
                    run = run_of(i * 2 + par + 2)
                    turn(i * 2 + par, par)
                    build(i * 2 + par + 2, par, run)
            turn(NT - 2, 0)
            turn(NT - 1, 1)

            pe.wait_ge(crowd_in, 1)
            T.transpose(ps[0:1, 0, 0:P], most[:, 0:1], ident[:, :]).then_inc(crowd_ps, 1)
            pe.wait_ge(ct_done, 3 * NT + 1)
            pe.wait_ge(diag_ready, NT)
            for q, (lo, w) in enumerate(NCH):
                last = T.matmul(ps[:, 4 + q, 0:w], ones[:, :], diag[:, lo:lo + w], start=True, stop=True)
            last.then_inc(bcast_ready, 1)
            pe.wait_ge(crowd_ready, 1)
            is_crowded = pe.value_load(crowded[0:1, 0:1], min_val=0, max_val=1)

            def aggregate_in(parts, counts, as_type):
                for q, (lo, w) in enumerate(NCH):
                    if q == 1:
                        pe.wait_ge(bcast_read, 1)
                    if q >= 2:
                        pe.wait_ge(agg_done, (q - 1) * KT)
                    for k in range(NT):
                        if counts is CTr and k % (NT // 2) == 0:
                            pe.wait_ge(ct_round[k // (NT // 2)], q + 1)
                        if q == 0:
                            pe.wait_ge(xs_ready, k + 1)
                        for m in range(KT):
                            for part in parts:
                                last = T.matmul(ps[:, (q * KT + m) % 8, 0:w], as_type(part[:, k, m * P:(m + 1) * P]), counts[:, k, lo:lo + w],
                                                start=k == 0 and part is parts[0], stop=k == NT - 1 and part is parts[-1])
                            if k == NT - 1:
                                last.then_inc(agg_ps, 1)

            with pe.If(is_crowded == 0):
                aggregate_in((xs_r, xs_l), CTr, lambda part: part)
            with pe.Else():
                aggregate_in((xs_r, xs_l), CT, lambda part: part.bitcast(F32))

            def layer_1(g, c):
                nodes = slice(c * ZC, (c + 1) * ZC)
                for h in range(HQ):
                    cols = slice(h * P, (h + 1) * P)
                    for k in range(KT):
                        for w, a in ((W1_r, agg_r), (W1_b, agg_l), (W1_l, agg_b)):
                            last = T.matmul(ps[:, (c * HQ + h) % 4, 0:ZC], w[:, k, cols], a[:, k, nodes],
                                            start=k == 0 and w is W1_r, stop=k == KT - 1 and w is W1_l)
                    last.then_inc(z_ps, 1)

            def layer_2(g, c):
                pe.wait_ge(z_done, g * (NZ * HQ) + ((c + 1) * HQ + 2))
                for a in range(2):
                    t = 2 * c + a
                    pe.wait_ge(y_done, g * NT + max(t - 3, 0) + 1)
                    for h in range(HQ):
                        for z, w in ((z_r, W2_r), (z_l, W2_r), (z_b, W2_l)):
                            last = T.matmul(ps[:, 4 + t % 4, :], z[:, c % 2, h, a * P:(a + 1) * P], w[:, h, :],
                                            start=h == 0 and z is z_r, stop=h == HQ - 1 and z is z_b)
                    last.then_inc(y_ps, 1)

            def both_layers(g):
                pe.wait_ge(w1_rest, g + 1)
                layer_1(g, 0)
                for c in range(1, NZ):
                    layer_1(g, c)
                    if c == 1:
                        pe.wait_ge(w2_rest, g + 1)
                    layer_2(g, c - 1)
                layer_2(g, NZ - 1)

            pe.wait_ge(agg_done, KT * len(NCH))
            with pe.Fori(0, HG) as g:
                both_layers(g)

            def gate_step(t):
                if t >= 0:
                    pe.wait_ge(xnT_done, t + 1)
                    for k in range(KT):
                        last = T.matmul(ps[:, 5, t * X:(t + 1) * X], xnT[:, k * P:(k + 1) * P], wgs[:, k, :],
                                        start=k == 0, stop=k == KT - 1)
                    last.then_inc(gate_ps, 1)
                if t + 1 < NT:
                    pe.wait_ge(xn_done, t + 2)
                    for k in range(KT):
                        last = T.transpose(ps[:, 3 + (t + 1) % 2, k * P:(k + 1) * P], xn2[:, (t + 1) % 2, k * P:(k + 1) * P], ident[:, :])
                    last.then_inc(xnT_ps, 1)

            pe.wait_ge(ld_small, 48)

            def aggregate_out(parts, counts, as_type):
                for t in range(NT):
                    if t >= 3:
                        pe.wait_ge(o_read, t - 2)
                    for k in range(NT):
                        if t == 0:
                            pe.wait_ge(y_split, k + 1)
                        for part in parts:
                            last = T.matmul(ps[:, t % 3, :], counts[:, k, t * P:(t + 1) * P], as_type(part[:, k, :]),
                                            start=k == 0 and part is parts[0], stop=k == NT - 1 and part is parts[-1])
                    last.then_inc(o_ps, 1)
                    if t >= 4:
                        gate_step(t - 5)

            with pe.If(is_crowded == 0):
                aggregate_out((y_r, y_l), CTr, lambda part: part)
            with pe.Else():
                aggregate_out((y_r, y_l), CT, lambda part: part.bitcast(F32))
            for t in range(NT - 5, NT):
                gate_step(t)
            pe.wait_ge(routes, 1)
            T.matmul(ps[:, 6, 0:LW + X], upper_h[:, :], routed[:, :], start=True, stop=False)
            for t in range(NT):
                T.matmul(ps[:, 6, (t + 1) * X:(NT + 1) * X].rearrange("p (t e) -> p t e", e=X), ones_h[:, :],
                         routed[:, t * X:(t + 1) * X].unsqueeze(1).broadcast_to([P, NT - t, X]), start=False, stop=False)
            T.matmul(ps[:, 6, 0:(NT + 1) * X].rearrange("p (t e) -> p t e", e=X), ones_h[:, :],
                     routed[:, LW:LW + X].unsqueeze(1).broadcast_to([P, NT + 1, X]), start=False, stop=True).then_inc(rank_ps, 1)
            for j in range(2 * NT):
                pe.wait_ge(place_ready, j + 1)
                T.matmul(ps[:, 7, 0:32], oh_place[:, j, 0:P], oh_block[:, j, :], start=j == 0, stop=j == 2 * NT - 1)
                last = T.matmul(ps[0:SB, 1, 0:32], oh_place[:, j, P:SLOTS], oh_block[:, j, :], start=j == 0, stop=j == 2 * NT - 1)
            last.then_inc(slots_ps, 1)

            def turn_rows(b):
                pe.wait_ge(gath_a, b * 16 + 16)
                pe.wait_ge(gath_b, b * 16 + 16)
                for k in range(KT):
                    T.transpose(ps[:, 0, k * P:(k + 1) * P], grow[:, 0, k * P:(k + 1) * P], ident[:, :])
                for k in range(KT):
                    last = T.transpose(ps[:, 1, k * SB:(k + 1) * SB], grow[0:SB, 1, k * P:(k + 1) * P], ident[0:SB, 0:SB])
                last.then_inc(g_trans, 1)

            pe.wait_ge(blocks_ready, 1)
            n_blocks = pe.value_load(block_expert[0:1, 33:34], min_val=2, max_val=BMAX)
            turn_rows(0)
            with pe.Fori(0, n_blocks) as b:
                pe.wait_ge(xT_done, b + 1)
                for m in range(MT):
                    half, col = divmod(m * P, HM)
                    if col == 0:
                        done = FIRST[:2 * half + 2]
                        pe.wait_ge(prep_act, b * len(EACH) + len(done))
                        pe.wait_ge(prep_dve, b * count(EACH, BY_DVE) + len(done))
                        pe.wait_ge(prep_pool, b * count(EACH, BY_POOL) + count(done, BY_POOL) + 1)
                    pe.wait_ge(h_done, b * MT + m + 1)
                    for mat, bank in ((0, 2), (1, 4)):
                        for k in range(KT):
                            cols = slice(k * HM + col, k * HM + col + P)
                            for w, a in ((w_r, xT_r), (w_b, xT_l), (w_l, xT_b)):
                                last = T.matmul(ps[:, bank + m % 2, 0:SLOTS], w[:, mat, half, cols], a[:, k, :],
                                                start=k == 0 and w is w_r, stop=k == KT - 1 and w is w_l)
                    last.then_inc(gu_ps, 1)
                turn_rows(b + 1)
                pe.wait_ge(yb_done, b * 2 + 2)
                for m in range(MT):
                    half, j = divmod(m, MT // 2)
                    if j == 0:
                        done = FIRST + EACH[:half + 1]
                        pe.wait_ge(prep_act, b * len(EACH) + len(done))
                        pe.wait_ge(prep_pool, b * count(EACH, BY_POOL) + count(done, BY_POOL) + 1)
                    pe.wait_ge(h_split, b * MT + m + 1)
                    for bank, lo, n in ((6, 0, P), (7, P, SB)):
                        for h, w in ((hT_r, w_r), (hT_l, w_r), (hT_b, w_l)):
                            last = T.matmul(ps[0:n, bank, :], h[:, m, lo:lo + n], w[:, 2, half, j * D:(j + 1) * D],
                                            start=m == 0 and h is hT_r, stop=m == MT - 1 and h is hT_b)
                    if m == MT // 2 - 1:
                        last.then_inc(wo_used, 1)
                last.then_inc(yb_ps, 1)


INPUTS = ["x", "src", "dst", "L0_gnn_W1", "L0_gnn_b1", "L0_gnn_W2", "L0_gnn_b2",
          "L0_ffn_wg", "L0_ffn_w0", "L0_ffn_w1", "L0_ffn_wo"]


def kernel(**inputs):
    import numpy as np
    import concourse.bacc as bacc
    from concourse.bass_utils import run_bass_kernel_spmd

    nc = bacc.Bacc("TRN2", target_bir_lowering=False, num_devices=1)
    arrays, args = {}, []
    for name in INPUTS:
        a = np.ascontiguousarray(inputs[name])
        arrays[f"in_{name}"] = a
        args.append(nc.dram_tensor(f"in_{name}", a.shape, mybir.dt.from_np(a.dtype), kind="ExternalInput").ap())
    out = nc.dram_tensor("out", arrays["in_x"].shape, F32, kind="ExternalOutput").ap()
    gnn_moe_kernel(nc, *args, out)
    result = run_bass_kernel_spmd(nc, [arrays], core_ids=[0])
    return result.results[0]["out"]
```

```python
from contextlib import ExitStack

import concourse.bass as bass
from concourse import mybir

F32 = mybir.dt.float32
F32R = mybir.dt.float32r
F16 = mybir.dt.float16
BF16 = mybir.dt.bfloat16
I32 = mybir.dt.int32
ALU = mybir.AluOpType
ACT = mybir.ActivationFunctionType
AX_X = mybir.AxisListType.X

P = 128
GROUP = 64
LN_EPS = 1e-5
NORM_EPS = 1e-12
SLOTS = 224
SB = SLOTS - P
NO_NODE = 1300


def gnn_moe_kernel(nc, x, src, dst, W1, b1, W2, b2, wg, w0, w1, wo, out):
    N, D = x.shape
    H = W1.shape[1]
    NE = src.shape[0]
    X, _, M = w0.shape
    NT = -(-N // P)
    NP = NT * P
    LAST = N - (NT - 1) * P
    KT, HT, MT = D // P, H // P, M // P
    G = D // GROUP
    ET = -(-NE // P)
    EB = ET - P
    EFULL = NE // P - P
    EREST = NE - (NE // P) * P
    U = 4
    OH_RING = 2
    MAXG = -(-ET // U)
    FIRSTS, GROUPS = ET, MAXG + 1
    EC = ET + 2 * U
    BMAX = (2 * N + X * SLOTS) // SLOTS
    NIDX = BMAX + 1
    NCH = [(0, 512), (512, 512), (1024, NP - 1024)]
    CCH = [(0, 512), (512, 512), (1024, N - 1024)]
    ZC = 256
    NZ = NP // ZC
    HQ = 2
    HG = HT // HQ
    ROUND = 1.5 * 2 ** 23
    COUNT_MAX = 4095
    assert NT == 10 and KT == 4 and MT == 8 and 0 < EB <= P and NE > 3 * P
    assert NT * MAXG * GROUPS * FIRSTS < 1 << 24

    xn_rows = nc.dram_tensor("xn_rows", [N, D], F32).ap()
    y_rows = nc.dram_tensor("y_rows", [BMAX * SLOTS, D], F32).ap()

    with ExitStack() as ctx:
        def sb(name, shape, dt=F32):
            return ctx.enter_context(nc.sbuf_tensor(name, shape, dt))

        def sem(name):
            return ctx.enter_context(nc.semaphore(name))

        ARENA = 192512
        arena = ctx.enter_context(nc.sbuf_tensor("arena", [P, ARENA], mybir.dt.uint8))
        arena_base = nc.sbuf_base - ARENA

        def at(name, offset, shape, dt=F32):
            return nc.alloc_sbuf_tensor_at(name, shape, dt, offset=arena_base + offset)

        CT = at("CT", 0, [P, NT, NP])
        CTr = at("CTr", 0, [P, NT, NP], F32R)
        erow = at("erow", 0, [P, 4, P], I32)
        erowf = at("erowf", 2048, [P, 4, P])
        jidx = at("jidx", 4096, [P, 2, 256])
        jval = at("jval", 6144, [P, 2, 256])
        crow = at("crow", 51200, [P, 2, NP])
        oh_src = at("oh_src", 171008, [P, OH_RING * U * NP], F16)
        oh_dst = at("oh_dst", 61440, [P, OH_RING * U * P], F16)
        iota_n = at("iota_n", 72704, [P, NP], F16)
        ecol = at("ecol", 75264, [P, 2, EC])
        loops = at("loops", 146432, [P, 2 * NP - P], F16)
        ident_h = loops[:, NP - P:NP]
        dst_h = at("dst_h", 77824, [P, EC], F16)
        x_in = at("x_in", 84992, [P, NT, D])
        xs_r = at("xs_r", 105472, [P, NT, D], F32R)
        xs_l = at("xs_l", 125952, [P, NT, D], F32R)
        xs_f = at("xs_f", 146432, [P, 3, D])
        ln_rest = at("ln_rest", 105472, [P, 2, NT, D])
        zero_row = at("zero_row", 158720, [P, D])
        agg_r = at("agg_r", 51200, [P, KT, NP], F32R)
        agg_b = at("agg_b", 71680, [P, KT, NP], BF16)
        agg_l = at("agg_l", 81920, [P, KT, NP], BF16)
        dinv_row = at("dinv_row", 176128, [P, NP])
        diag = at("diag", 171008, [P, NP])
        agg_f = at("agg_f", 92160, [P, 2, 512])
        yacc = at("yacc", 105472, [P, NT, D])
        raw1 = at("raw1", 97280, [P, KT, HQ * P])
        raw2 = at("raw2", 101376, [P, HQ, D])
        y_l = at("y_l", 125952, [P, NT, D], F32R)
        W1_r = at("W1_r", 146432, [P, KT, HQ * P], F32R)
        W1_b = at("W1_b", 150528, [P, KT, HQ * P], BF16)
        W1_l = at("W1_l", 152576, [P, KT, HQ * P], BF16)
        W2_r = at("W2_r", 154624, [P, HQ, D], F32R)
        W2_l = at("W2_l", 158720, [P, HQ, D], BF16)
        z_r = at("z_r", 162816, [P, 2, HQ, ZC], F32R)
        z_l = at("z_l", 166912, [P, 2, HQ, ZC], F32R)
        y_r = at("y_r", 171008, [P, NT, D], F32R)
        xt = at("xt", 51200, [P, NT, D])
        zn = at("zn", 71680, [P, 2, D])
        sq = at("sq", 75776, [P, 2, D])
        x_re = at("x_re", 90112, [P, 4, D])
        xn2 = at("xn2", 83968, [P, 2, D])
        xnT = at("xnT", 79872, [P, 2, D])
        LW = NT * X
        gate = at("gate", 71680, [P, 9, LW])
        btab = at("btab", 79360, [1, 32, X])
        btab2 = at("btab2", 101376, [1, 32, X])
        etab = at("etab", 81408, [P, X, X])
        oh_place = at("oh_place", 90112, [P, 2 * NT, SLOTS], F16)
        oh_block = at("oh_block", 99072, [P, 2 * NT, 32], F16)
        w_r = at("w_r", 0, [P, 3, 2, KT * 512], F32R)
        w_l = at("w_l", 105472, [P, 3, 2, KT * 512], BF16)
        w_b = at("w_b", 130048, [P, 2, 2, KT * 512], BF16)
        raw = at("raw", 146432, [P, 3, KT * 512])
        xT_r = at("xT_r", 171008, [P, KT, SLOTS], F32R)
        hT_r = at("hT_r", 174592, [P, MT, SLOTS], F32R)
        hT_l = at("hT_l", 181760, [P, MT, SLOTS], F32R)
        hT_b = at("hT_b", 188928, [P, MT, SLOTS], BF16)
        sil = at("sil", 92160, [P, 2, SLOTS])
        h_f = at("h_f", 93952, [P, 2, SLOTS])
        grow = at("grow", 95744, [P, 2, D])
        ysb = at("ysb", 99840, [P, 2, D])
        xT_b = at("xT_b", 83968, [P, KT, SLOTS], BF16)
        xT_l = at("xT_l", 85760, [P, KT, SLOTS], BF16)
        low_a = at("low_a", 71680, [P, 6, D])
        low_b = at("low_b", 87552, [P, 2, D])
        ygath = at("ygath", 0, [P, NT, D])
        z_b = sb("z_b", [P, 2, HQ, ZC], BF16)
        z_f = sb("z_f", [P, 2, ZC])
        assert NZ * ZC == NP and MT * P == 2 * 512 and KT * 512 == (MT // 2) * D

        ident = sb("ident", [P, P])
        minus_half = sb("minus_half", [P, 16])
        ln_sum = sb("ln_sum", [P, NT])
        ln_neg = sb("ln_neg", [P, NT])
        ln_sq = sb("ln_sq", [P, NT])
        ones = sb("ones", [P, P])
        upper = sb("upper", [P, P])
        spans = sb("spans", [P, 2, 2])
        rel = sb("rel", [P, 4, NT])
        tlo = sb("tlo", [P, 2, NT])
        span_c = sb("span_c", [P, 4])
        runs = sb("runs", [1, 2, NT])
        run_table = sb("run_table", [1, 16], I32)
        mv = sb("mv", [P, NT, 2])
        st6 = sb("st6", [P, NT, 6])
        deg = sb("deg", [P, NT])
        most = sb("most", [P, 4])
        crowded = sb("crowded", [1, 2], I32)
        small = sb("small", [P, 3, NT])
        dinv = sb("dinv", [P, NT])
        scl = sb("scl", [P, NT])
        b1c = sb("b1c", [P, HT])
        b1_now = sb("b1_now", [P, HQ])
        b2b = sb("b2b", [P, D])
        wgs = sb("wgs", [P, KT, X])
        pow_in = sb("pow_in", [P, 2, G + 1])
        pow_out = sb("pow_out", [P, 2, G + 1])
        c16 = sb("c16", [P, LW])
        valid = sb("valid", [P, NT])
        tok = sb("tok", [P, NT])
        routed = sb("routed", [P, (NT + 1) * X], F16)
        upper_h = sb("upper_h", [P, P], F16)
        ones_h = sb("ones_h", [P, P], F16)
        before = sb("before", [P, X, X])
        place = sb("place", [P, SLOTS], F16)
        part = sb("part", [P, 3, 2, NT])
        weight = sb("weight", [P, 2, NT])
        low_c = sb("low_c", [P, 2, D])
        rt = sb("rt", [P, 10, X])
        slotf = sb("slotf", [P, 2, NT])
        sloti = sb("sloti", [P, 2, NT], I32)
        tops = sb("tops", [P, 8, NT])
        bidx = sb("bidx", [P, 32])
        block_expert = sb("block_expert", [1, 34], I32)
        bef = sb("bef", [1, 34])
        block_tokens = sb("block_tokens", [1, 32], I32)
        tokens_f = sb("tokens_f", [1, 32])
        idx_all = sb("idx_all", [P, 2, NIDX], I32)
        credit = sb("credit", [P, 16])
        table_load = sb("table_load", [P, 1])
        held = sb("held", [P, 3])
        idx_now = sb("idx_now", [P, 2], I32)
        ps = ctx.enter_context(nc.psum_tensor("ps", [P, 8, 512], F32))

        consts = sem("consts")
        zero_set = sem("zero_set")
        y_zeroed = sem("y_zeroed")
        edge_pad, x_pad, crow_pad = sem("edge_pad"), sem("x_pad"), sem("crow_pad")
        ld_edge, ld_x, ld_w1, ld_w2, ld_small = (sem(n) for n in ("ld_edge", "ld_x", "ld_w1", "ld_w2", "ld_small"))
        ld_xre = [sem(f"ld_xre{i}") for i in range(4)]
        dve = sem("dve")
        edge_rows = sem("edge_rows")
        edge_cols_t = sem("edge_cols_t")
        rel_ready = sem("rel_ready")
        rel_t = sem("rel_t")
        span_ready = sem("span_ready")
        table_t = sem("table_t")
        table_ready = sem("table_ready")
        oh_ready = sem("oh_ready")
        oh_free = sem("oh_free")
        ln_summed, ln_centred, ln_squared = sem("ln_summed"), sem("ln_centred"), sem("ln_squared")
        c_built = sem("c_built")
        c_row = sem("c_row")
        c_trans = sem("c_trans")
        ct_done = sem("ct_done")
        rsqrt_in, rsqrt_out = sem("rsqrt_in"), sem("rsqrt_out")
        scl_ready = sem("scl_ready")
        diag_ready = sem("diag_ready")
        bcast_ready, bcast_read = sem("bcast_ready"), sem("bcast_read")
        xs_made = sem("xs_made")
        xs_round = sem("xs_round")
        xs_ready = sem("xs_ready")
        agg_ps = sem("agg_ps")
        agg_done = sem("agg_done")
        agg_scaled = sem("agg_scaled")
        agg_round = sem("agg_round")
        crowd_in = sem("crowd_in")
        crowd_ps = sem("crowd_ps")
        crowd_ready = sem("crowd_ready")
        ct_round = [sem("ct_round0"), sem("ct_round1")]
        yacc_zero = sem("yacc_zero")
        w1_round, w1_rest = sem("w1_round"), sem("w1_rest")
        w2_round, w2_rest = sem("w2_round"), sem("w2_rest")
        b1_taken = sem("b1_taken")
        z_ps = sem("z_ps")
        z_relu = sem("z_relu")
        z_round = sem("z_round")
        z_done = sem("z_done")
        y_ps = sem("y_ps")
        y_done = sem("y_done")
        y_round = sem("y_round")
        y_split = sem("y_split")
        o_ps = sem("o_ps")
        o_read = sem("o_read")
        sq_out = sem("sq_out")
        xn_done = sem("xn_done")
        xnT_ps = sem("xnT_ps")
        xnT_done = sem("xnT_done")
        gate_ps = sem("gate_ps")
        st_xn = [sem("st_xn0"), sem("st_xn1")]
        exp_in = sem("exp_in")
        exp_out = sem("exp_out")
        routes = sem("routes")
        rank_ps = sem("rank_ps")
        slots_ready = sem("slots_ready")
        blocks_ready, tokens_known = sem("blocks_ready"), sem("tokens_known")
        place_ready, slots_ps, rows_known = sem("place_ready"), sem("slots_ps"), sem("rows_known")
        idx_ready = sem("idx_ready")
        gath_a, gath_b = sem("gath_a"), sem("gath_b")
        g_trans = sem("g_trans")
        xT_done = sem("xT_done")
        ld_raw = [sem(f"ld_raw{i}") for i in range(3)]
        first_made = sem("first_made")
        prep_act, prep_dve, prep_pool = sem("prep_act"), sem("prep_dve"), sem("prep_pool")
        xT_round = sem("xT_round")
        wo_used = sem("wo_used")
        gu_ps = sem("gu_ps")
        silu_done = sem("silu_done")
        h_done = sem("h_done")
        h_round = sem("h_round")
        h_split = sem("h_split")
        yb_ps = sem("yb_ps")
        yb_done = sem("yb_done")
        st_ya, st_yb = sem("st_ya"), sem("st_yb")
        low_got, low_added = sem("low_got"), sem("low_added")
        high_got = [sem(f"high_got{t}") for t in range(NT)]
        comb = sem("comb")
        st_out = sem("st_out")

        HM = M // 2

        def columns(w, half):
            return lambda e: w[bass.ds(e, 1), :, half * HM:(half + 1) * HM].rearrange("o (k p) m -> p (o k) m", p=P)

        def rows(w, half):
            return lambda e: w[bass.ds(e, 1), half * HM:(half + 1) * HM, :].rearrange("o (j p) d -> p (o j) d", p=P)

        W0A, W1A, W0B, W1B = ((m, half, columns(w, half)) for half in (0, 1) for m, w in ((0, w0), (1, w1)))
        WOA, WOB = ((2, half, rows(wo, half)) for half in (0, 1))
        FIRST = [W0A, W1A, W0B, W1B]
        EACH = [WOA, WOB, W0A, W1A, W0B, W1B]
        RAW_SLOTS = 3
        BY_POOL = (WOA, WOB, W1B)
        BY_DVE = (W0A, W1A, W0B, W1B)

        def low(t):
            return low_a[:, t, :] if t < 6 else low_b[:, t - 6, :] if t < 8 else low_c[:, t - 8, :]

        def count(pieces, kinds):
            return sum(p in kinds for p in pieces)

        FREE = [
            lambda b: lambda e: e.wait_ge(wo_used, b + 1),
            lambda b: lambda e: e.wait_ge(yb_ps, b + 1),
            lambda b: lambda e: e.wait_ge(gu_ps, b * MT + MT // 2),
            lambda b: lambda e: e.wait_ge(gu_ps, b * MT + MT // 2),
            lambda b: lambda e: e.wait_ge(gu_ps, b * MT + MT),
            lambda b: lambda e: e.wait_ge(gu_ps, b * MT + MT),
        ]

        TABLE_CONSTS, ONE_HOT_CONSTS, CONSTS = 8, 12, 18

        def read_run(engine, t):
            word = engine.value_load(run_table[0:1, bass.ds(t, 1)], min_val=2 * FIRSTS,
                                     max_val=(NT - 1) * MAXG * GROUPS * FIRSTS + MAXG * FIRSTS + ET - 1)
            return word % FIRSTS, word // FIRSTS % GROUPS, word // (FIRSTS * GROUPS)

        def edge_column(first, i, j, n=1):
            return nc.s_assert_within(first + i * U + j, 0, EC - n,
                                      skip_runtime_bounds_check_because="the last group ends at EC or before")

        block = ctx.enter_context(nc.Block())

        @block.sync
        def _(sp):
            sp.wait_ge(edge_pad, 1)
            for q, e in ((2, dst), (0, src)):
                sp.dma_start(erow[:, q, :], e[0:P * P].rearrange("(j p) -> j p", p=P)).then_inc(ld_edge, 16)
                sp.dma_start(erow[0:EFULL, q + 1, :],
                             e[P * P:(P + EFULL) * P].rearrange("(j p) -> j p", p=P)).then_inc(ld_edge, 16)
                if EREST:
                    sp.dma_start(erow[EFULL:EFULL + 1, q + 1, 0:EREST],
                                 e[(P + EFULL) * P:NE].rearrange("(a p) -> a p", a=1)).then_inc(ld_edge, 16)
            sp.wait_ge(x_pad, 1)
            sp.dma_start(x_in[:, 0:NT - 1, :], x[0:(NT - 1) * P, :].rearrange("(t p) d -> p t d", p=P)).then_inc(ld_x, 16)
            sp.dma_start(x_in[0:LAST, NT - 1, :], x[(NT - 1) * P:N, :]).then_inc(ld_x, 16)
            sp.dma_start(b1c[:, :], b1.rearrange("(h p) -> p h", p=P), allow_slow_non_contiguous=True).then_inc(ld_small, 16)
            sp.dma_start(b2b[:, :], b2.rearrange("(a d) -> a d", a=1).broadcast_to([P, D])).then_inc(ld_small, 16)
            sp.dma_start(wgs[:, :, :], wg.rearrange("(k p) e -> p k e", p=P)).then_inc(ld_small, 16)
            sp.wait_ge(zero_set, 1)
            sp.dma_start(y_rows[(X - 1) * SLOTS:BMAX * SLOTS, :].rearrange("(p j) d -> p j d", p=SLOTS // 2),
                         zero_row[0:SLOTS // 2, :].unsqueeze(1).broadcast_to([SLOTS // 2, 2 * (BMAX - X + 1), D])).then_inc(y_zeroed, 16)
            def load_group(g):
                sp.dma_start(raw1[:, :, :], W1[:, bass.ds(g * (HQ * P), HQ * P)].rearrange("(k p) h -> p k h", p=P)).then_inc(ld_w1, 16)
                sp.dma_start(raw2[:, :, :], W2[bass.ds(g * (HQ * P), HQ * P), :].rearrange("(h p) d -> p h d", p=P)).then_inc(ld_w2, 16)

            sp.wait_ge(xs_made, NT)
            load_group(0)
            with sp.Fori(0, HG - 1) as g:
                sp.wait_ge(w1_rest, g + 1)
                sp.wait_ge(w2_rest, g + 1)
                load_group(g + 1)

            def reload(t):
                n = P if t < NT - 1 else LAST
                sp.dma_start(x_re[0:n, t % 4, :], x[t * P:t * P + n, :]).then_inc(ld_xre[t % 4], 16)

            sp.wait_ge(y_split, NT)
            for t in range(4):
                reload(t)
            sp.wait_ge(y_ps, HG * NT + 1)
            for i in range(RAW_SLOTS):
                sp.dma_start(raw[:, i, :].rearrange("p (k m) -> p k m", m=512), FIRST[i][2](0)).then_inc(ld_raw[i], 16)
            for t in range(NT):
                sp.wait_ge(xn_done, t + 1)
                n = P if t < NT - 1 else LAST
                sp.dma_start(xn_rows[t * P:t * P + n, :], xn2[0:n, t % 2, :]).then_inc(st_xn[t % 2], 16)
                if t + 4 < NT:
                    reload(t + 4)
            for i in range(RAW_SLOTS, len(FIRST)):
                sp.wait_ge(prep_act, i - RAW_SLOTS + 1)
                sp.wait_ge(prep_dve, i - RAW_SLOTS + 1)
                sp.dma_start(raw[:, i % RAW_SLOTS, :].rearrange("p (k m) -> p k m", m=512),
                             FIRST[i][2](0)).then_inc(ld_raw[i % RAW_SLOTS], 16)
            sp.wait_ge(blocks_ready, 1)
            n_blocks = sp.value_load(block_expert[0:1, 33:34], min_val=X, max_val=BMAX)
            with sp.Fori(0, n_blocks) as b:
                own = sp.value_load(block_expert[0:1, bass.ds(b, 1)], min_val=0, max_val=X - 1)
                nxt = sp.value_load(block_expert[0:1, bass.ds(b + 1, 1)], min_val=0, max_val=X - 1)
                for i, piece in enumerate(EACH):
                    slot = (len(FIRST) + i) % RAW_SLOTS
                    before = (FIRST + EACH)[:len(FIRST) + i - RAW_SLOTS + 1]
                    if before[-1] in BY_DVE:
                        sp.wait_ge(prep_dve, b * count(EACH, BY_DVE) + count(before, BY_DVE))
                    if before[-1] in BY_POOL:
                        sp.wait_ge(prep_pool, b * count(EACH, BY_POOL) + count(before, BY_POOL) + 1)
                    sp.dma_start(raw[:, slot, :].rearrange("p (k m) -> p k m", m=512),
                                 piece[2](own if i < 2 else nxt)).then_inc(ld_raw[slot], 16)
            for t in range(NT):
                sp.wait_ge(comb, t + 1)
                n = P if t < NT - 1 else LAST
                sp.dma_start(out[t * P:t * P + n, :], xt[0:n, t, :]).then_inc(st_out, 16)
            sp.wait_ge(st_out, 16 * NT)

        @block.gpsimd
        def _(pool):
            g = nc.gpsimd
            g.memset(erow[:, :, :], NO_NODE).then_inc(edge_pad, 1)
            g.memset(ident[:, :], 0.0).then_inc(consts, 1)
            g.memset(upper[:, :], 1.0).then_inc(consts, 1)
            pool.wait_ge(consts, 2)
            g.affine_select(out=ident[:, :], in_=ident[:, :], compare_op=ALU.not_equal, fill=1.0, base=0,
                            pattern=[[-1, P]], channel_multiplier=1).then_inc(consts, 1)
            g.affine_select(out=upper[:, :], in_=upper[:, :], compare_op=ALU.is_ge, fill=0.0, base=-1,
                            pattern=[[1, P]], channel_multiplier=-1).then_inc(consts, 1)
            for q in range(2):
                g.iota(tlo[:, q, :], pattern=[[P, NT]], base=q * (P - 1), channel_multiplier=0,
                       allow_small_or_imprecise_dtypes=True).then_inc(consts, 1)
                g.iota(jidx[:, q, :], pattern=[[1 - 2 * q, 256]], base=1 if q == 0 else 256, channel_multiplier=0,
                       allow_small_or_imprecise_dtypes=True).then_inc(consts, 1)
            g.memset(ecol[:, :, ET:EC], NO_NODE).then_inc(consts, 1)
            g.iota(iota_n[:, :], pattern=[[1, NP]], base=0, channel_multiplier=0,
                   allow_small_or_imprecise_dtypes=True).then_inc(consts, 1)
            g.memset(loops[:, :], 0.0).then_inc(consts, 1)
            pool.wait_ge(consts, 11)
            g.tensor_copy(ident_h, ident[:, :]).then_inc(consts, 1)
            g.memset(ones[:, :], 1.0).then_inc(consts, 1)
            g.memset(valid[:, :], 1.0).then_inc(consts, 1)
            g.memset(minus_half[:, :], -0.5).then_inc(consts, 1)
            g.iota(c16[:, :], pattern=[[0, NT], [-1, X]], base=X, channel_multiplier=0,
                   allow_small_or_imprecise_dtypes=True).then_inc(consts, 1)
            g.iota(bidx[:, :], pattern=[[1, 32]], base=0, channel_multiplier=0,
                   allow_small_or_imprecise_dtypes=True).then_inc(consts, 1)
            pool.wait_ge(consts, 17)
            g.affine_select(out=valid[:, :], in_=valid[:, :], compare_op=ALU.is_ge, fill=0.0, base=N - 1,
                            pattern=[[-P, NT]], channel_multiplier=-1).then_inc(consts, 1)
            pool.wait_ge(consts, CONSTS)

            def rsqrt(n, where, value, width):
                pool.wait_ge(rsqrt_in, n)
                g.tensor_tensor(where, value, minus_half[:, 0:width], ALU.pow).then_inc(rsqrt_out, 1)

            g.iota(tok[:, :], pattern=[[P, NT]], base=0, channel_multiplier=1,
                   allow_small_or_imprecise_dtypes=True).then_inc(consts, 1)
            g.iota(place[:, :], pattern=[[1, SLOTS]], base=0, channel_multiplier=0,
                   allow_small_or_imprecise_dtypes=True).then_inc(consts, 1)
            g.memset(before[:, :, :], 1.0).then_inc(consts, 1)
            g.memset(routed[:, :], 0.0).then_inc(consts, 1)
            g.tensor_copy(upper_h[:, :], upper[:, :]).then_inc(consts, 1)
            g.tensor_copy(ones_h[:, :], ones[:, :]).then_inc(consts, 1)
            pool.wait_ge(consts, CONSTS + 6)
            g.tensor_tensor(tok[:, :], tok[:, :], valid[:, :], ALU.mult).then_inc(consts, 1)
            g.affine_select(out=before[:, :, :], in_=before[:, :, :], compare_op=ALU.is_ge, fill=0.0, base=-1,
                            pattern=[[1, X], [-1, X]], channel_multiplier=0).then_inc(consts, 1)

            rsqrt(1, small[:, 0, :], small[:, 1, :], NT)
            rsqrt(2, dinv[:, :], small[:, 2, :], NT)
            pool.wait_ge(agg_ps, KT * len(NCH))
            g.memset(yacc[:, :, :], 0.0).then_inc(yacc_zero, 1)

            for t in range(NT):
                rsqrt(t + 3, pow_out[:, t % 2, :], pow_in[:, t % 2, :], G + 1)
            rsqrt(NT + 3, pow_out[:, :, G], pow_in[:, :, G], 2)

            def hold(c):
                g.tensor_tensor(held[:, c:c + 1], ones[:, 0:1], ones[:, 0:1], ALU.mult)

            def fetch(b):
                pool.wait_ge(g_trans, b + 1)
                g.tensor_copy(idx_now[:, 0:1], idx_all[:, 0, bass.ds(b, 1)]).then_inc(idx_ready, 1)
                g.tensor_copy(idx_now[0:SB, 1:2], idx_all[0:SB, 1, bass.ds(b, 1)]).then_inc(idx_ready, 1)
                pool.wait_ge(idx_ready, b * 2 + 2)
                hold(0)
                g.indirect_dma_start(out=grow[:, 0, :], out_offset=None, in_=xn_rows,
                                     in_offset=bass.IndirectOffsetOnAxis(ap=idx_now[:, 0:1], axis=0)).then_inc(gath_a, 16)
                g.indirect_dma_start(out=grow[0:SB, 1, :], out_offset=None, in_=xn_rows,
                                     in_offset=bass.IndirectOffsetOnAxis(ap=idx_now[0:SB, 1:2], axis=0)).then_inc(gath_b, 16)

            def first_rest(piece, i):
                m, half, _ = piece
                pool.wait_ge(first_made, i + 1)
                if piece not in BY_POOL:
                    g.tensor_tensor(w_l[:, m, half, :], raw[:, i % RAW_SLOTS, :], w_r[:, m, half, :].bitcast(F32),
                                    ALU.subtract).then_inc(prep_dve, 1)
                else:
                    for lo, done in ((0, prep_dve), (KT * 256, prep_pool)):
                        g.tensor_tensor(w_l[:, m, half, lo:lo + KT * 256], raw[:, i % RAW_SLOTS, lo:lo + KT * 256],
                                        w_r[:, m, half, lo:lo + KT * 256].bitcast(F32), ALU.subtract).then_inc(done, 1)

            def rest(piece, stream, b):
                m, half, _ = piece
                pool.wait_ge(prep_act, b * len(EACH) + stream + 1)
                g.tensor_tensor(w_l[:, m, half, :], raw[:, stream % RAW_SLOTS, :],
                                w_r[:, m, half, :].bitcast(F32), ALU.subtract).then_inc(prep_pool, 1)

            for i, piece in enumerate(FIRST[:2]):
                first_rest(piece, i)
            pool.wait_ge(slots_ready, 1)
            pool.wait_ge(st_xn[0], 16 * (NT // 2))
            pool.wait_ge(st_xn[1], 16 * (NT // 2))
            fetch(0)
            for i, piece in enumerate(FIRST[2:]):
                first_rest(piece, i + 2)
            pool.wait_ge(blocks_ready, 1)
            last_block = pool.value_load(block_expert[0:1, 32:33], min_val=X - 1, max_val=BMAX - 1)
            with pool.Fori(0, last_block) as b:
                fetch(b + 1)
                for i, piece in enumerate(EACH):
                    if piece in BY_POOL:
                        rest(piece, len(FIRST) + i, b)
            fetch(last_block + 1)
            rest(WOA, len(FIRST), last_block)
            rest(WOB, len(FIRST) + 1, last_block)
            pool.wait_ge(rows_known, 1)
            pool.wait_ge(st_ya, last_block * 16 + 16)
            pool.wait_ge(st_yb, last_block * 16 + 16)
            hold(1)
            for t in range(NT):
                n = P if t < NT - 1 else LAST
                g.indirect_dma_start(out=low(t)[0:n, :], out_offset=None, in_=y_rows,
                                     in_offset=bass.IndirectOffsetOnAxis(ap=sloti[0:n, 0, t:t + 1], axis=0)).then_inc(low_got, 16)
            rest(W1B, len(FIRST) + 5, last_block)
            pool.wait_ge(gu_ps, last_block * MT + MT)
            pool.wait_ge(st_ya, last_block * 16 + 32)
            pool.wait_ge(st_yb, last_block * 16 + 32)
            pool.wait_ge(prep_act, last_block * len(EACH) + len(FIRST + EACH))
            hold(2)
            for t in range(NT):
                n = P if t < NT - 1 else LAST
                g.indirect_dma_start(out=ygath[0:n, t, :], out_offset=None, in_=y_rows,
                                     in_offset=bass.IndirectOffsetOnAxis(ap=sloti[0:n, 1, t:t + 1], axis=0)).then_inc(high_got[t], 16)

        @block.scalar
        def _(act):
            s = nc.scalar

            def c_tile(t, par):
                act.wait_ge(c_built, t + 1)
                if not isinstance(t, int) or t >= 2:
                    act.wait_ge(c_trans, t * 3 - 3)
                s.activation(crow[:, par, 0:N], ps[:, 3 * par:3 * par + 3, :].rearrange("p a n -> p (a n)")[:, 0:N],
                             ACT.Copy, accum_out=deg[:, bass.ds(t, 1)]).then_inc(c_row, 1)

            def c_cols(t):
                for q, n in enumerate((4, 4, 2)):
                    act.wait_ge(c_trans, t * 3 + q + 1)
                    s.activation(CT[:, 4 * q:4 * q + n, bass.ds(t * P, P)],
                                 ps[:, 6 + q % 2, 0:n * P].rearrange("p (a n) -> p a n", a=n), ACT.Copy).then_inc(ct_done, 1)

            act.wait_ge(crow_pad, 1)
            c_tile(0, 0)
            act.wait_ge(ld_x, 32)
            for t in range(NT):
                s.activation(ln_rest[:, 0, t, :], x_in[:, t, :], ACT.Copy, accum_out=ln_sum[:, t:t + 1]).then_inc(ln_summed, 1)
            act.wait_ge(ln_summed, NT)
            s.activation(ln_neg[:, :], ln_sum[:, :], ACT.Copy, scale=-1.0 / D).then_inc(ln_centred, 1)
            act.wait_ge(ln_centred, 1)
            for t in range(NT):
                s.activation(ln_rest[:, 1, t, :], x_in[:, t, :], ACT.Square, bias=ln_neg[:, t:t + 1],
                             accum_out=ln_sq[:, t:t + 1]).then_inc(ln_squared, 1)
            c_tile(1, 1)
            c_cols(0)
            with act.Fori(0, NT // 2 - 1) as i:
                c_tile(i * 2 + 2, 0)
                c_cols(i * 2 + 1)
                c_tile(i * 2 + 3, 1)
                c_cols(i * 2 + 2)
            c_cols(NT - 1)
            def round_counts(chunks):
                with act.If(is_crowded == 0):
                    for lo, w in chunks:
                        s.activation(CTr[:, 0:NT // 2, lo:lo + w], CT[:, 0:NT // 2, lo:lo + w], ACT.Copy).then_inc(ct_round[0], 1)

            for t in range(NT):
                if t == 2:
                    act.wait_ge(crowd_ready, 1)
                    is_crowded = act.value_load(crowded[0:1, 0:1], min_val=0, max_val=1)
                    round_counts(NCH[:1])
                act.wait_ge(xs_made, t + 1)
                s.activation(xs_r[:, t, :], xs_f[:, t % 3, :], ACT.Copy).then_inc(xs_round, 1)
            round_counts(NCH[1:])

            def round_w1(g):
                act.wait_ge(ld_w1, g * 16 + 16)
                act.wait_ge(z_ps, g * (NZ * HQ) + 1)
                s.activation(W1_r[:, :, :], raw1[:, :, :], ACT.Copy).then_inc(w1_round, 1)

            def round_w2(g):
                act.wait_ge(ld_w2, g * 16 + 16)
                act.wait_ge(y_ps, g * NT + 1)
                s.activation(W2_r[:, :, :], raw2[:, :, :], ACT.Copy).then_inc(w2_round, 1)

            act.wait_ge(xs_ready, NT)
            round_w1(0)
            round_w2(0)
            n = 0
            for lo, w in NCH:
                for m in range(KT):
                    act.wait_ge(agg_scaled, n + 1)
                    s.activation(agg_r[:, m, lo:lo + w], agg_f[:, n % 2, 0:w], ACT.Copy).then_inc(agg_round, 1)
                    n += 1

            def take_b1(g):
                s.activation(b1_now[:, :], b1c[:, bass.ds(g * HQ, HQ)], ACT.Copy).then_inc(b1_taken, 1)
                act.wait_ge(b1_taken, g + 1)

            def hidden(g, c):
                for h in range(HQ):
                    n = g * (NZ * HQ) + (c * HQ + h)
                    act.wait_ge(z_done, n + 1)
                    act.wait_ge(z_ps, n + 2)
                    s.activation(z_f[:, h, :], ps[:, 4 + (c * HQ + h) % 4, 0:ZC], ACT.Relu,
                                 bias=b1_now[:, h:h + 1]).then_inc(z_relu, 1)
                    act.wait_ge(z_relu, n + 1)
                    s.activation(z_r[:, c % 2, h, :], z_f[:, h, :], ACT.Copy).then_inc(z_round, 1)

            act.wait_ge(ld_small, 48)
            with act.Fori(0, HG - 1) as g:
                take_b1(g)
                for c in range(NZ):
                    hidden(g, c)
                round_w1(g + 1)
                round_w2(g + 1)
            take_b1(HG - 1)

            def make_first(i):
                m, half, _ = FIRST[i]
                act.wait_ge(ld_raw[i % RAW_SLOTS], (i // RAW_SLOTS + 1) * 16)
                s.activation(w_r[:, m, half, :], raw[:, i % RAW_SLOTS, :], ACT.Copy).then_inc(prep_act, 1)
                s.activation(w_b[:, m, half, :], raw[:, i % RAW_SLOTS, :], ACT.Copy).then_inc(first_made, 1)

            def round_y(c):
                for t in (2 * c, 2 * c + 1):
                    act.wait_ge(y_done, (HG - 1) * NT + t + 2)
                    s.activation(y_r[:, t, :], yacc[:, t, :], ACT.Copy, scale=dinv[:, t:t + 1]).then_inc(y_round, 1)

            hidden(HG - 1, 0)
            for c in range(1, NZ):
                hidden(HG - 1, c)
                round_y(c - 1)
            round_y(NZ - 1)
            for t in range(NT + 4):
                if t < NT:
                    act.wait_ge(o_read, t + 1)
                    s.activation(sq[:, t % 2, :], zn[:, t % 2, :], ACT.Square).then_inc(sq_out, 1)
                if t >= 4:
                    act.wait_ge(xnT_ps, t - 3)
                    s.activation(xnT[:, t % 2, :], ps[:, 2 + t % 2, :], ACT.Copy).then_inc(xnT_done, 1)
            act.wait_ge(o_ps, NT)
            make_first(0)
            act.wait_ge(exp_in, 1)
            s.activation(tops[:, 3, :], tops[:, 2, :], ACT.Exp).then_inc(exp_out, 1)

            for i in range(1, len(FIRST)):
                make_first(i)
            act.wait_ge(blocks_ready, 1)
            n_blocks = act.value_load(block_expert[0:1, 33:34], min_val=X, max_val=BMAX)

            def round_piece(piece, stream, b, free, part=None):
                m, half, _ = piece
                slot = stream % RAW_SLOTS
                if part in (None, 0):
                    act.wait_ge(ld_raw[slot], (b * (len(EACH) // RAW_SLOTS) + stream // RAW_SLOTS + 1) * 16)
                    free(act)
                lo, hi = (0, KT * 512) if part is None else (part * KT * 256, (part + 1) * KT * 256)
                ins = s.activation(w_r[:, m, half, lo:hi], raw[:, slot, lo:hi], ACT.Copy)
                if part in (None, 1):
                    ins.then_inc(prep_act, 1)

            def take_xT(b):
                act.wait_ge(g_trans, b + 2)
                s.activation(xT_r[:, :, 0:P], ps[:, 0, :].rearrange("p (k n) -> p k n", k=KT), ACT.Copy)
                s.activation(xT_r[:, :, P:SLOTS], ps[:, 1, 0:KT * SB].rearrange("p (k n) -> p k n", k=KT), ACT.Copy).then_inc(xT_round, 1)

            take_xT(0)
            s.activation(table_load[:, 0:1], dinv[:, 0:1], ACT.Silu)
            with act.Fori(0, n_blocks) as b:
                for m in range(MT):
                    act.wait_ge(gu_ps, b * MT + m + 1)
                    s.activation(sil[:, m % 2, :], ps[:, 2 + m % 2, 0:SLOTS], ACT.Silu).then_inc(silu_done, 1)
                    round_piece(EACH[m // 2], len(FIRST) + m // 2, b, FREE[m // 2](b), m % 2)
                    act.wait_ge(h_done, b * MT + m + 3)
                    s.activation(hT_r[:, m, :], h_f[:, m % 2, :], ACT.Copy).then_inc(h_round, 1)
                take_xT(b + 1)
                for i in (4, 5):
                    round_piece(EACH[i], len(FIRST) + i, b, FREE[i](b))
                act.wait_ge(yb_ps, b + 2)
                act.wait_ge(st_ya, b * 16 + 16)
                s.activation(ysb[:, 0, :], ps[:, 6, :], ACT.Copy).then_inc(yb_done, 1)
                act.wait_ge(yb_done, b * 2 + 4)
                act.dma_start(y_rows[bass.ds(b * SLOTS, P), :], ysb[:, 0, :]).then_inc(st_ya, 16)
                act.dma_start(y_rows[bass.ds(b * SLOTS + P, SB), :], ysb[0:SB, 1, :]).then_inc(st_yb, 16)

        @block.vector
        def _(v):
            V = nc.vector
            steps = [0]

            def then(ins):
                steps[0] += 1
                ins.then_inc(dve, 1)
                v.wait_ge(dve, steps[0])

            V.memset(x_in[:, NT - 1, :], 0.0).then_inc(x_pad, 1)
            V.memset(crow[:, 0, N:NP], 0.0)
            V.memset(crow[:, 1, N:NP], 0.0).then_inc(crow_pad, 1)
            V.memset(zero_row[:, :], 0.0).then_inc(zero_set, 1)
            V.memset(st6[:, :, :], 0.0).then_inc(h_done, 2)
            V.memset(run_table[0:1, :], 0).then_inc(oh_free, OH_RING * U // 2)
            for j, (free, n) in enumerate(((c_row, 2), (ct_done, 1), (g_trans, 1), (yb_done, 2), (st_ya, 16), (st_yb, 16),
                                            (y_done, 1), (wo_used, 1), (yb_ps, 1), (prep_pool, 1), (z_ps, 1), (z_done, 2), (y_ps, 1))):
                V.memset(credit[:, j:j + 1], 0.0).then_inc(free, n)
            v.wait_ge(ld_edge, 16 * (6 if EREST else 4))
            V.tensor_copy(erowf[:, :, :], erow[:, :, :]).then_inc(edge_rows, 1)
            v.wait_ge(edge_rows, 1)
            for q in range(2):
                V.tensor_reduce(spans[:, 0, q:q + 1], erowf[:, 2 + q, :], AX_X, ALU.min)
                then(V.tensor_reduce(spans[:, 1, q:q + 1], erowf[:, 2 + q, :], AX_X, ALU.max))
            v.wait_ge(consts, TABLE_CONSTS)
            for q in range(2):
                V.tensor_scalar(rel[:, q, :], tlo[:, 1, :], spans[:, 0, q:q + 1], None, ALU.is_ge)
                then(V.tensor_scalar(rel[:, 2 + q, :], tlo[:, 0, :], spans[:, 1, q:q + 1], None, ALU.is_le))
            V.tensor_tensor(rel[:, 0:2, :], rel[:, 0:2, :], rel[:, 2:4, :], ALU.mult).then_inc(rel_ready, 1)
            v.wait_ge(rel_t, 1)
            for q in range(2):
                then(V.tensor_tensor(jval[0:NT, q, 0:ET], ps[0:NT, 1, 0:ET], jidx[0:NT, q, 0:ET], ALU.mult))
                then(V.tensor_reduce(span_c[0:NT, q:q + 1], jval[0:NT, q, 0:ET], AX_X, ALU.max))
            then(V.tensor_scalar(span_c[0:NT, 1:2], span_c[0:NT, 1:2], -1.0, 256.0, ALU.mult, ALU.add))
            then(V.tensor_scalar(span_c[0:NT, 1:2], span_c[0:NT, 1:2], float(ET - 1), None, ALU.min))
            then(V.tensor_tensor(span_c[0:NT, 2:3], span_c[0:NT, 0:1], span_c[0:NT, 1:2], ALU.subtract))
            then(V.tensor_scalar(span_c[0:NT, 2:3], span_c[0:NT, 2:3], U + 1.0, U / 2 - 0.5, ALU.max, ALU.add))
            then(V.tensor_scalar(span_c[0:NT, 3:4], span_c[0:NT, 2:3], 1.0 / U, ROUND, ALU.mult, ALU.add))
            V.tensor_scalar(span_c[0:NT, 2:3], span_c[0:NT, 3:4], -ROUND, None, ALU.add).then_inc(span_ready, 1)
            v.wait_ge(consts, ONE_HOT_CONSTS)
            v.wait_ge(edge_cols_t, 1)
            V.tensor_copy(ecol[:, 0, 0:ET], ps[:, 0, 0:ET])
            V.tensor_copy(ecol[:, 1, 0:ET], ps[:, 0, 2 * P:2 * P + ET])
            then(V.tensor_copy(dst_h[:, 0:ET], ps[:, 0, 2 * P:2 * P + ET]))
            then(V.tensor_copy(dst_h[:, ET:EC], ecol[:, 1, ET:EC]))
            v.wait_ge(table_t, 1)
            row = lambda a: ps[0:1, 1, 16 * a:16 * a + NT]
            then(V.tensor_copy(runs[0:1, 0, :], row(0)))
            then(V.scalar_tensor_tensor(runs[0:1, 1, :], row(1), float(FIRSTS), runs[0:1, 0, :], ALU.mult, ALU.add))
            then(V.scalar_tensor_tensor(runs[0:1, 0, :], row(2), float(FIRSTS * GROUPS), runs[0:1, 1, :], ALU.mult, ALU.add))
            V.tensor_copy(run_table[0:1, 0:NT], runs[0:1, 0, :]).then_inc(table_ready, 1)
            v.wait_ge(table_ready, 1)

            with v.Fori(0, NT) as t:
                first, groups, base = read_run(v, t)
                with v.Fori(0, groups) as i:
                    g = base + i
                    for j in range(0, U, 2):
                        v.wait_ge(oh_free, g * 2 + (j // 2 + 1))
                        V.tensor_tensor(oh_dst[:, bass.ds(g % OH_RING * (U * P) + j * P, 2 * P)].rearrange("p (j n) -> p j n", j=2),
                                        iota_n[:, bass.ds(t * P, P)].unsqueeze(1).broadcast_to([P, 2, P]),
                                        dst_h[:, bass.ds(edge_column(first, i, j, 2), 2)].unsqueeze(2).broadcast_to([P, 2, P]),
                                        ALU.is_equal)
                        for k in (j, j + 1):
                            last = V.tensor_scalar(oh_src[:, bass.ds(g % OH_RING * (U * NP) + k * NP, N)], iota_n[:, 0:N],
                                                   ecol[:, 0, bass.ds(edge_column(first, i, k), 1)], None, ALU.is_equal)
                        last.then_inc(oh_ready, 1)
            v.wait_ge(ln_squared, NT)
            V.tensor_scalar(small[:, 1, :], ln_sq[:, :], 1.0 / D, LN_EPS, ALU.mult, ALU.add).then_inc(rsqrt_in, 1)
            v.wait_ge(c_row, NT + 2)
            V.tensor_reduce(most[:, 0:1], deg[:, :], AX_X, ALU.max).then_inc(crowd_in, 1)
            V.tensor_scalar(small[:, 2, :], deg[:, :], 1.0, None, ALU.max).then_inc(rsqrt_in, 1)
            v.wait_ge(rsqrt_out, 2)
            V.tensor_tensor(scl[:, :], dinv[:, :], small[:, 0, :], ALU.mult).then_inc(scl_ready, 1)

            def make_xs(t):
                if t >= 3:
                    v.wait_ge(xs_ready, t - 2)
                V.tensor_scalar(xs_f[:, t % 3, :], x_in[:, t, :], ln_neg[:, t:t + 1], scl[:, t:t + 1], ALU.add,
                                ALU.mult).then_inc(xs_made, 1)

            def split_xs(t):
                v.wait_ge(xs_round, t + 1)
                V.tensor_tensor(xs_l[:, t, :], xs_f[:, t % 3, :], xs_r[:, t, :].bitcast(F32), ALU.subtract).then_inc(xs_ready, 1)

            v.wait_ge(scl_ready, 1)
            v.wait_ge(c_built, NT)
            make_xs(0)
            make_xs(1)
            v.wait_ge(crowd_ps, 1)
            then(V.tensor_reduce(most[0:1, 1:2], ps[0:1, 0, 0:P], AX_X, ALU.max))
            then(V.tensor_scalar(most[0:1, 2:3], most[0:1, 1:2], float(COUNT_MAX), None, ALU.is_gt))
            V.tensor_copy(crowded[0:1, 0:1], most[0:1, 2:3]).then_inc(crowd_ready, 1)
            for t in range(NT):
                split_xs(t)
                if t + 2 < NT:
                    make_xs(t + 2)
                if t == NT // 2 - 1:
                    for j in range(NT):
                        V.tensor_scalar(diag[:, j * P:(j + 1) * P], ident[:, :], dinv[:, j:j + 1], None,
                                        ALU.mult).then_inc(diag_ready, 1)
                if t == 2:
                    v.wait_ge(ct_done, 3 * NT + 1)
                    v.wait_ge(crowd_ready, 1)
                    is_crowded = v.value_load(crowded[0:1, 0:1], min_val=0, max_val=1)
                    with v.If(is_crowded == 0):
                        V.tensor_copy(CTr[:, NT // 2:NT, 0:NCH[0][1]], CT[:, NT // 2:NT, 0:NCH[0][1]]).then_inc(ct_round[1], 1)
            with v.If(is_crowded == 0):
                for lo, w in NCH[1:]:
                    V.tensor_copy(CTr[:, NT // 2:NT, lo:lo + w], CT[:, NT // 2:NT, lo:lo + w]).then_inc(ct_round[1], 1)
            v.wait_ge(bcast_ready, 1)
            V.tensor_copy(dinv_row[:, :], ps[:, 4:7, :].rearrange("p a n -> p (a n)")[:, 0:NP]).then_inc(bcast_read, 1)

            def rest_w1(g):
                v.wait_ge(w1_round, g + 1)
                V.tensor_copy(W1_b[:, :, :], raw1[:, :, :])
                V.tensor_tensor(W1_l[:, :, :], raw1[:, :, :], W1_r[:, :, :].bitcast(F32), ALU.subtract).then_inc(w1_rest, 1)

            def rest_w2(g):
                v.wait_ge(w2_round, g + 1)
                V.tensor_tensor(W2_l[:, :, :], raw2[:, :, :], W2_r[:, :, :].bitcast(F32), ALU.subtract).then_inc(w2_rest, 1)

            v.wait_ge(y_zeroed, 16)
            rest_w1(0)
            rest_w2(0)
            v.wait_ge(bcast_read, 1)
            places = [(m, lo, w) for lo, w in NCH for m in range(KT)]

            def scale(n):
                m, lo, w = places[n]
                v.wait_ge(agg_ps, n + 1)
                if n >= 2:
                    v.wait_ge(agg_done, n - 1)
                V.tensor_tensor(agg_f[:, n % 2, 0:w], ps[:, n % 8, 0:w], dinv_row[:, lo:lo + w],
                                ALU.mult).then_inc(agg_scaled, 1)

            scale(0)
            for n, (m, lo, w) in enumerate(places):
                if n + 1 < len(places):
                    scale(n + 1)
                v.wait_ge(agg_scaled, n + 1)
                V.tensor_copy(agg_b[:, m, lo:lo + w], agg_f[:, n % 2, 0:w])
                v.wait_ge(agg_round, n + 1)
                V.tensor_tensor(agg_l[:, m, lo:lo + w], agg_f[:, n % 2, 0:w], agg_r[:, m, lo:lo + w].bitcast(F32),
                                ALU.subtract).then_inc(agg_done, 1)

            def hidden(g, c):
                for h in range(HQ):
                    n = g * (NZ * HQ) + (c * HQ + h)
                    v.wait_ge(z_relu, n + 1)
                    V.tensor_copy(z_b[:, c % 2, h, :], z_f[:, h, :])
                    v.wait_ge(z_round, n + 1)
                    V.tensor_tensor(z_l[:, c % 2, h, :], z_f[:, h, :], z_r[:, c % 2, h, :].bitcast(F32),
                                    ALU.subtract).then_inc(z_done, 1)

            def add_up(g, c):
                if c == 0:
                    v.wait_ge(yacc_zero, 1)
                for t in (2 * c, 2 * c + 1):
                    v.wait_ge(y_ps, g * NT + (t + 2))
                    V.tensor_tensor(yacc[:, t, :], ps[:, t % 4, :], yacc[:, t, :], ALU.add).then_inc(y_done, 1)
                    if isinstance(g, int):
                        v.wait_ge(y_round, t + 1)
                        V.scalar_tensor_tensor(y_l[:, t, :], yacc[:, t, :], dinv[:, t:t + 1], y_r[:, t, :].bitcast(F32),
                                               ALU.mult, ALU.subtract).then_inc(y_split, 1)

            with v.Fori(0, HG - 1) as g:
                hidden(g, 0)
                for c in range(1, NZ):
                    hidden(g, c)
                    add_up(g, c - 1)
                rest_w1(g + 1)
                add_up(g, NZ - 1)
                rest_w2(g + 1)
            hidden(HG - 1, 0)
            for c in range(1, NZ):
                hidden(HG - 1, c)
                add_up(HG - 1, c - 1)
            add_up(HG - 1, NZ - 1)
            v.wait_ge(ld_small, 48)

            def take_z(t):
                v.wait_ge(o_ps, t + 1)
                V.scalar_tensor_tensor(zn[:, t % 2, :], ps[:, 4 + t % 3, :], dinv[:, t:t + 1], b2b[:, :], ALU.mult,
                                       ALU.add).then_inc(o_read, 1)

            def make_xn(t):
                if t >= 2:
                    v.wait_ge(st_xn[t % 2], 16 * (t // 2))
                    v.wait_ge(xnT_ps, t - 1)
                V.tensor_scalar(xn2[:, t % 2, :], xt[:, t, :], mv[:, t, 0:1], pow_out[:, t % 2, G:G + 1], ALU.subtract,
                                ALU.mult).then_inc(xn_done, 1)

            def statistics(t):
                then(V.bn_stats(st6[:, t, :], xt[:, t, :]))
                then(V.bn_aggr(mv[:, t, :], st6[:, t, :]))
                return V.tensor_scalar(pow_in[:, t % 2, G:G + 1], mv[:, t, 1:2], LN_EPS, None, ALU.add)

            V.memset(pow_in[:, :, :], 1.0)
            take_z(0)
            for t in range(NT):
                z = zn[:, t % 2, :]
                groups = z.rearrange("p (g f) -> p g f", g=G)
                v.wait_ge(sq_out, t + 1)
                then(V.tensor_reduce(pow_in[:, t % 2, 0:G], sq[:, t % 2, :].rearrange("p (g f) -> p g f", g=G), AX_X, ALU.add))
                V.tensor_scalar(pow_in[:, t % 2, 0:G], pow_in[:, t % 2, 0:G], NORM_EPS ** 2, None, ALU.max).then_inc(rsqrt_in, 1)
                if t + 1 < NT:
                    take_z(t + 1)
                if t >= 1:
                    statistics(t - 1)
                v.wait_ge(rsqrt_out, t + 3)
                if t >= 2:
                    make_xn(t - 2)
                then(V.tensor_tensor(groups, groups, pow_out[:, t % 2, 0:G].unsqueeze(2).broadcast_to([P, G, GROUP]), ALU.mult))
                v.wait_ge(ld_xre[t % 4], 16 * (t // 4 + 1))
                then(V.tensor_tensor(xt[:, t, :], x_re[:, t % 4, :], z, ALU.add))
            statistics(NT - 1).then_inc(rsqrt_in, 1)
            v.wait_ge(rsqrt_out, NT + 3)
            make_xn(NT - 2)
            make_xn(NT - 1)

            v.wait_ge(gate_ps, NT)
            g3 = lambda j: gate[:, j, :].rearrange("p (t e) -> p t e", e=X)
            c3 = c16[:, :].rearrange("p (t e) -> p t e", e=X)
            over = lambda ap: ap.unsqueeze(2).broadcast_to([P, NT, X])
            logits = ps[:, 7, 0:LW]
            for k in range(2):
                values = logits.rearrange("p (t e) -> p t e", e=X) if k == 0 else g3(1)
                then(V.tensor_reduce(tops[:, k, :], values, AX_X, ALU.max))
                then(V.tensor_tensor(g3(2), values, over(tops[:, k, :]), ALU.is_equal))
                then(V.tensor_tensor(g3(3), g3(2), c3, ALU.mult))
                then(V.tensor_reduce(tops[:, 7, :], g3(3), AX_X, ALU.max))
                then(V.tensor_tensor(g3(4 + k), c3, over(tops[:, 7, :]), ALU.is_equal))
                if k == 0:
                    then(V.scalar_tensor_tensor(gate[:, 1, :], gate[:, 4, :], -3.0e38, logits, ALU.mult, ALU.add))
            V.tensor_tensor(tops[:, 2, :], tops[:, 1, :], tops[:, 0, :], ALU.subtract).then_inc(exp_in, 1)
            then(V.tensor_tensor(gate[:, 6, :], gate[:, 4, :], gate[:, 5, :], ALU.add))
            V.tensor_tensor(routed[:, 0:LW].rearrange("p (t e) -> p t e", e=X), g3(6), over(valid[:, :]), ALU.mult).then_inc(routes, 1)
            v.wait_ge(exp_out, 1)
            then(V.tensor_scalar(tops[:, 4, :], tops[:, 3, :], 1.0, None, ALU.add))
            then(V.reciprocal(tops[:, 5, :], tops[:, 4, :]))
            then(V.tensor_tensor(tops[:, 6, :], tops[:, 5, :], tops[:, 3, :], ALU.mult))
            chosen = gate[:, 4:6, :]
            v.wait_ge(rank_ps, 1)
            then(V.tensor_copy(rt[:, 0, :], ps[:, 6, LW:LW + X]))
            def rounded(out, value, tmp):
                then(V.tensor_scalar(tmp, value, ROUND, None, ALU.add))
                then(V.tensor_scalar(out, tmp, -ROUND, None, ALU.add))

            then(V.tensor_scalar(rt[:, 1, :], rt[:, 0, :], 1.0 / SLOTS, 0.5 - 0.5 / SLOTS, ALU.mult, ALU.add))
            rounded(rt[:, 2, :], rt[:, 1, :], rt[:, 3, :])
            then(V.tensor_scalar(rt[:, 2, :], rt[:, 2, :], 1.0, None, ALU.max))
            then(V.tensor_tensor(etab[:, :, :], before[:, :, :], rt[:, 2, :].unsqueeze(1).broadcast_to([P, X, X]), ALU.mult))
            then(V.tensor_reduce(rt[:, 4, :], etab[:, :, :], AX_X, ALU.add))
            then(V.scalar_tensor_tensor(g3(0), rt[:, 4, :].unsqueeze(1).broadcast_to([P, NT, X]), float(SLOTS),
                                        ps[:, 6, 0:LW].rearrange("p (t e) -> p t e", e=X), ALU.mult, ALU.add))
            then(V.tensor_tensor(gate[:, 7:9, :], chosen, gate[:, 0, :].unsqueeze(1).broadcast_to([P, 2, LW]), ALU.mult))
            then(V.tensor_reduce(slotf[:, :, :], gate[:, 7:9, :].rearrange("p k (t e) -> p k t e", e=X), AX_X, ALU.add))
            then(V.tensor_scalar(part[:, 0, :, :], slotf[:, :, :], 1.0 / SLOTS, 0.5 / SLOTS - 0.5, ALU.mult, ALU.add))
            rounded(part[:, 1, :, :], part[:, 0, :, :], part[:, 2, :, :])
            then(V.scalar_tensor_tensor(part[:, 2, :, :], part[:, 1, :, :], -float(SLOTS), slotf[:, :, :], ALU.mult, ALU.add))
            blocks_of = oh_block[:, :, :].rearrange("p (k t) b -> p k t b", k=2)
            then(V.tensor_tensor(blocks_of, bidx[:, :].unsqueeze(1).unsqueeze(1).broadcast_to([P, 2, NT, 32]),
                                 part[:, 1, :, :].unsqueeze(3).broadcast_to([P, 2, NT, 32]), ALU.is_equal))
            V.tensor_tensor(blocks_of, blocks_of, tok[:, :].unsqueeze(1).unsqueeze(3).broadcast_to([P, 2, NT, 32]), ALU.mult)
            for k in range(2):
                for t in range(NT):
                    V.tensor_scalar(oh_place[:, k * NT + t, :], place[:, :], part[:, 2, k, t:t + 1], None,
                                    ALU.is_equal).then_inc(place_ready, 1)
            v.wait_ge(slots_ps, 1)
            V.tensor_copy(idx_all[:, 0, :], ps[:, 7, 0:NIDX])
            V.tensor_copy(idx_all[0:SB, 1, :], ps[0:SB, 1, 0:NIDX]).then_inc(slots_ready, 1)
            then(V.tensor_tensor(rt[:, 5, :], rt[:, 4, :], rt[:, 2, :], ALU.add))
            ends = rt[:, 5, :]
            bt = btab[:, :, :]
            then(V.tensor_tensor(bt, bidx[0:1, :].unsqueeze(2).broadcast_to([1, 32, X]),
                                 ends[0:1, :].unsqueeze(1).broadcast_to([1, 32, X]), ALU.is_ge))
            then(V.tensor_reduce(bef[0:1, 0:32], bt, AX_X, ALU.add))
            then(V.tensor_scalar(bef[0:1, 0:32], bef[0:1, 0:32], float(X - 1), None, ALU.min))
            then(V.tensor_scalar(bef[0:1, 32:33], ends[0:1, X - 1:X], -1.0, None, ALU.add))
            then(V.tensor_copy(bef[0:1, 33:34], ends[0:1, X - 1:X]))
            V.tensor_copy(block_expert[0:1, :], bef[0:1, :]).then_inc(blocks_ready, 1)
            then(V.tensor_tensor(btab2[:, :, :], bidx[0:1, :].unsqueeze(2).broadcast_to([1, 32, X]),
                                 rt[0:1, 4, :].unsqueeze(1).broadcast_to([1, 32, X]), ALU.is_ge))
            then(V.tensor_tensor(btab2[:, :, :], btab2[:, :, :], bt, ALU.subtract))
            then(V.scalar_tensor_tensor(rt[0:1, 6, :], rt[0:1, 4, :], float(SLOTS), rt[0:1, 0, :], ALU.mult, ALU.add))
            then(V.tensor_tensor(btab2[:, :, :], btab2[:, :, :], rt[0:1, 6, :].unsqueeze(1).broadcast_to([1, 32, X]), ALU.mult))
            then(V.tensor_reduce(tokens_f[0:1, :], btab2[:, :, :], AX_X, ALU.add))
            then(V.scalar_tensor_tensor(tokens_f[0:1, :], bidx[0:1, :], -float(SLOTS), tokens_f[0:1, :], ALU.mult, ALU.add))
            then(V.tensor_scalar(tokens_f[0:1, :], tokens_f[0:1, :], 0.0, float(SLOTS), ALU.max, ALU.min))
            V.tensor_copy(block_tokens[0:1, :], tokens_f[0:1, :]).then_inc(tokens_known, 1)
            then(V.tensor_tensor(part[:, 0, 0, :], slotf[:, 0, :], slotf[:, 1, :], ALU.is_lt))
            then(V.tensor_scalar(part[:, 0, 1, :], part[:, 0, 0, :], -1.0, 1.0, ALU.mult, ALU.add))
            V.tensor_tensor(part[:, 1, 0, :], slotf[:, 0, :], slotf[:, 1, :], ALU.min)
            V.tensor_tensor(part[:, 1, 1, :], slotf[:, 0, :], slotf[:, 1, :], ALU.max)
            for k in range(2):
                V.tensor_tensor(part[:, 2, 0, :], tops[:, 5, :], part[:, 0, k, :], ALU.mult)
                then(V.tensor_tensor(part[:, 2, 1, :], tops[:, 6, :], part[:, 0, 1 - k, :], ALU.mult))
                then(V.tensor_tensor(weight[:, k, :], part[:, 2, 0, :], part[:, 2, 1, :], ALU.add))
            V.tensor_copy(sloti[:, :, :], part[:, 1, :, :]).then_inc(rows_known, 1)
            v.wait_ge(blocks_ready, 1)
            n_blocks = v.value_load(block_expert[0:1, 33:34], min_val=X, max_val=BMAX)

            def rest_piece(piece, stream, b, free, part=None):
                m, half, _ = piece
                lo, hi = (0, KT * 512) if part is None else (part * KT * 256, (part + 1) * KT * 256)
                if part in (None, 0):
                    v.wait_ge(ld_raw[stream % RAW_SLOTS], (b * (len(EACH) // RAW_SLOTS) + stream // RAW_SLOTS + 1) * 16)
                    free(v)
                ins = V.tensor_copy(w_b[:, m, half, lo:hi], raw[:, stream % RAW_SLOTS, lo:hi])
                if piece not in BY_POOL:
                    if part in (None, 1):
                        v.wait_ge(prep_act, b * len(EACH) + stream + 1)
                    if part is None:
                        ins = V.tensor_tensor(w_l[:, m, half, :], raw[:, stream % RAW_SLOTS, :],
                                              w_r[:, m, half, :].bitcast(F32), ALU.subtract)
                    if part == 1:
                        ins = V.tensor_tensor(w_l[:, m, half, :], raw[:, stream % RAW_SLOTS, :],
                                              w_r[:, m, half, :].bitcast(F32), ALU.subtract)
                if part in (None, 1):
                    ins.then_inc(prep_dve, 1)

            def take_xT(b):
                v.wait_ge(xT_round, b + 1)
                V.tensor_copy(xT_b[:, :, :], xT_r[:, :, :].bitcast(F32))
                V.tensor_tensor(xT_l[:, :, 0:P], ps[:, 0, :].rearrange("p (k n) -> p k n", k=KT),
                                xT_r[:, :, 0:P].bitcast(F32), ALU.subtract)
                V.tensor_tensor(xT_l[:, :, P:SLOTS], ps[:, 1, 0:KT * SB].rearrange("p (k n) -> p k n", k=KT),
                                xT_r[:, :, P:SLOTS].bitcast(F32), ALU.subtract).then_inc(xT_done, 1)

            take_xT(0)
            with v.Fori(0, n_blocks) as b:
                for m in range(MT):
                    v.wait_ge(silu_done, b * MT + m + 1)
                    V.tensor_tensor(h_f[:, m % 2, :], ps[:, 4 + m % 2, 0:SLOTS], sil[:, m % 2, :], ALU.mult).then_inc(h_done, 1)
                    if m >= 4:
                        rest_piece(EACH[m // 2], len(FIRST) + m // 2, b, FREE[m // 2](b), m % 2)
                    v.wait_ge(h_done, b * MT + m + 3)
                    V.tensor_copy(hT_b[:, m, :], h_f[:, m % 2, :])
                    v.wait_ge(h_round, b * MT + m + 1)
                    V.tensor_tensor(hT_l[:, m, :], h_f[:, m % 2, :], hT_r[:, m, :].bitcast(F32), ALU.subtract).then_inc(h_split, 1)
                take_xT(b + 1)
                for i in (4, 5):
                    rest_piece(EACH[i], len(FIRST) + i, b, FREE[i](b))
                v.wait_ge(yb_ps, b + 2)
                v.wait_ge(st_yb, b * 16 + 16)
                V.tensor_copy(ysb[0:SB, 1, :], ps[0:SB, 7, :]).then_inc(yb_done, 1)
            for t in range(NT):
                n = P if t < NT - 1 else LAST
                v.wait_ge(low_got, 16 * NT)
                V.scalar_tensor_tensor(xt[0:n, t, :], low(t)[0:n, :], weight[0:n, 0, t:t + 1], xt[0:n, t, :], ALU.mult,
                                       ALU.add).then_inc(low_added, 1)
            for t in range(NT):
                n = P if t < NT - 1 else LAST
                v.wait_ge(low_added, t + 1)
                v.wait_ge(high_got[t], 16)
                V.scalar_tensor_tensor(xt[0:n, t, :], ygath[0:n, t, :], weight[0:n, 1, t:t + 1], xt[0:n, t, :], ALU.mult,
                                       ALU.add).then_inc(comb, 1)

        @block.tensor
        def _(pe):
            T = nc.tensor
            pe.wait_ge(consts, TABLE_CONSTS)
            pe.wait_ge(edge_rows, 1)
            for q in range(4):
                last = T.transpose(ps[:, 0, q * P:(q + 1) * P], erowf[:, q, :], ident[:, :])
            last.then_inc(edge_cols_t, 1)
            pe.wait_ge(rel_ready, 1)
            T.transpose(ps[0:NT, 1, 0:P], rel[:, 0, :], ident[:, :])
            T.transpose(ps[0:NT, 1, P:P + EB], rel[0:EB, 1, :], ident[0:EB, 0:EB]).then_inc(rel_t, 1)
            pe.wait_ge(span_ready, 1)
            for j, (c, rhs) in enumerate(((1, ident), (2, ident), (2, upper))):
                last = T.matmul(ps[0:1, 1, 16 * j:16 * j + NT], span_c[0:NT, c:c + 1], rhs[0:NT, 0:NT],
                                start=True, stop=True)
            last.then_inc(table_t, 1)
            pe.wait_ge(table_ready, 1)

            def count_edges(par, g, start):
                for j in range(U):
                    if j % 2 == 0:
                        pe.wait_ge(oh_ready, g * 2 + (j // 2 + 1))
                    for q, (lo, w) in enumerate(CCH):
                        last = T.matmul(ps[:, 3 * par + q, 0:w], oh_dst[:, bass.ds(g % OH_RING * (U * P) + j * P, P)],
                                        oh_src[:, bass.ds(g % OH_RING * (U * NP) + (j * NP + lo), w)],
                                        start=start and j == 0, stop=False)
                    if j % 2 == 1:
                        last.then_inc(oh_free, 1)

            def build(t, par, run):
                _, groups, base = run
                pe.wait_ge(c_row, t + 1)
                count_edges(par, base, True)
                with pe.Fori(1, groups) as i:
                    count_edges(par, base + i, False)
                for q, (lo, w) in enumerate(CCH):
                    last = T.matmul(ps[:, 3 * par + q, 0:w], ident_h, loops[:, bass.ds(NP - P + lo - t * P, w)],
                                    start=False, stop=True)
                last.then_inc(c_built, 1)

            def turn(t, par):
                pe.wait_ge(c_row, t + 3)
                for q, n in enumerate((4, 4, 2)):
                    pe.wait_ge(ct_done, t * 3 + max(q, 1))
                    for a in range(n):
                        k = 4 * q + a
                        last = T.transpose(ps[:, 6 + q % 2, a * P:(a + 1) * P], crow[:, par, k * P:(k + 1) * P], ident[:, :])
                    last.then_inc(c_trans, 1)

            build(0, 0, read_run(pe, 0))
            build(1, 1, read_run(pe, 1))
            with pe.Fori(0, NT // 2 - 1) as i:
                for par in (0, 1):
                    run = read_run(pe, i * 2 + par + 2)
                    turn(i * 2 + par, par)
                    build(i * 2 + par + 2, par, run)
            turn(NT - 2, 0)
            turn(NT - 1, 1)

            pe.wait_ge(crowd_in, 1)
            T.transpose(ps[0:1, 0, 0:P], most[:, 0:1], ident[:, :]).then_inc(crowd_ps, 1)
            pe.wait_ge(ct_done, 3 * NT + 1)

            def broadcast_dinv():
                pe.wait_ge(diag_ready, NT)
                for q, (lo, w) in enumerate(NCH):
                    last = T.matmul(ps[:, 4 + q, 0:w], ones[:, :], diag[:, lo:lo + w], start=True, stop=True)
                last.then_inc(bcast_ready, 1)

            pe.wait_ge(crowd_ready, 1)
            is_crowded = pe.value_load(crowded[0:1, 0:1], min_val=0, max_val=1)

            def aggregate_in(parts, counts, as_type):
                for q, (lo, w) in enumerate(NCH):
                    if q == 1:
                        pe.wait_ge(bcast_read, 1)
                    if q >= 2:
                        pe.wait_ge(agg_done, (q - 1) * KT)
                    for k in range(NT):
                        if counts is CTr and k % (NT // 2) == 0:
                            pe.wait_ge(ct_round[k // (NT // 2)], q + 1)
                        if q == 0:
                            pe.wait_ge(xs_ready, k + 1)
                            if k == NT - 2:
                                broadcast_dinv()
                        for m in range(KT):
                            for part in parts:
                                last = T.matmul(ps[:, (q * KT + m) % 8, 0:w], as_type(part[:, k, m * P:(m + 1) * P]), counts[:, k, lo:lo + w],
                                                start=k == 0 and part is parts[0], stop=k == NT - 1 and part is parts[-1])
                            if k == NT - 1:
                                last.then_inc(agg_ps, 1)

            with pe.If(is_crowded == 0):
                aggregate_in((xs_r, xs_l), CTr, lambda part: part)
            with pe.Else():
                aggregate_in((xs_r, xs_l), CT, lambda part: part.bitcast(F32))

            def layer_1(g, c):
                nodes = slice(c * ZC, (c + 1) * ZC)
                for h in range(HQ):
                    cols = slice(h * P, (h + 1) * P)
                    for k in range(KT):
                        for w, a in ((W1_r, agg_r), (W1_b, agg_l), (W1_l, agg_b)):
                            last = T.matmul(ps[:, 4 + (c * HQ + h) % 4, 0:ZC], w[:, k, cols], a[:, k, nodes],
                                            start=k == 0 and w is W1_r, stop=k == KT - 1 and w is W1_l)
                    last.then_inc(z_ps, 1)

            def layer_2(g, c):
                pe.wait_ge(z_done, g * (NZ * HQ) + ((c + 1) * HQ + 2))
                for a in range(2):
                    t = 2 * c + a
                    pe.wait_ge(y_done, g * NT + max(t - 3, 0) + 1)
                    for h in range(HQ):
                        for z, w in ((z_r, W2_r), (z_l, W2_r), (z_b, W2_l)):
                            last = T.matmul(ps[:, t % 4, :], z[:, c % 2, h, a * P:(a + 1) * P], w[:, h, :],
                                            start=h == 0 and z is z_r, stop=h == HQ - 1 and z is z_b)
                    last.then_inc(y_ps, 1)

            def both_layers(g):
                pe.wait_ge(w1_rest, g + 1)
                layer_1(g, 0)
                for c in range(1, NZ):
                    layer_1(g, c)
                    if c == 1:
                        pe.wait_ge(w2_rest, g + 1)
                        pe.wait_ge(agg_done, len(NCH) * KT)
                    layer_2(g, c - 1)
                layer_2(g, NZ - 1)

            pe.wait_ge(agg_done, 2 * KT)
            with pe.Fori(0, HG) as g:
                both_layers(g)

            def turn_xn(t):
                pe.wait_ge(xn_done, t + 1)
                for k in range(KT):
                    last = T.transpose(ps[:, 2 + t % 2, k * P:(k + 1) * P], xn2[:, t % 2, k * P:(k + 1) * P], ident[:, :])
                last.then_inc(xnT_ps, 1)

            def logits(t):
                pe.wait_ge(xnT_done, t + 1)
                for k in range(KT):
                    last = T.matmul(ps[:, 7, t * X:(t + 1) * X], xnT[:, t % 2, k * P:(k + 1) * P], wgs[:, k, :],
                                    start=k == 0, stop=k == KT - 1)
                last.then_inc(gate_ps, 1)

            pe.wait_ge(ld_small, 48)

            def aggregate_out(parts, counts, as_type):
                for t in range(NT):
                    if t >= 3:
                        pe.wait_ge(o_read, t - 2)
                    for k in range(NT):
                        if t == 0:
                            pe.wait_ge(y_split, k + 1)
                        for part in parts:
                            last = T.matmul(ps[:, 4 + t % 3, :], counts[:, k, t * P:(t + 1) * P], as_type(part[:, k, :]),
                                            start=k == 0 and part is parts[0], stop=k == NT - 1 and part is parts[-1])
                    last.then_inc(o_ps, 1)
                    if t >= 4:
                        turn_xn(t - 4)
                    if t >= 5:
                        logits(t - 5)

            with pe.If(is_crowded == 0):
                aggregate_out((y_r, y_l), CTr, lambda part: part)
            with pe.Else():
                aggregate_out((y_r, y_l), CT, lambda part: part.bitcast(F32))
            turn_xn(NT - 4)
            logits(NT - 5)
            turn_xn(NT - 3)
            logits(NT - 4)
            logits(NT - 3)
            turn_xn(NT - 2)
            turn_xn(NT - 1)
            logits(NT - 2)
            logits(NT - 1)
            pe.wait_ge(routes, 1)
            T.matmul(ps[:, 6, 0:LW + X], upper_h[:, :], routed[:, :], start=True, stop=False)
            for t in range(NT):
                T.matmul(ps[:, 6, (t + 1) * X:(NT + 1) * X].rearrange("p (t e) -> p t e", e=X), ones_h[:, :],
                         routed[:, t * X:(t + 1) * X].unsqueeze(1).broadcast_to([P, NT - t, X]), start=False, stop=False)
            T.matmul(ps[:, 6, 0:(NT + 1) * X].rearrange("p (t e) -> p t e", e=X), ones_h[:, :],
                     routed[:, LW:LW + X].unsqueeze(1).broadcast_to([P, NT + 1, X]), start=False, stop=True).then_inc(rank_ps, 1)
            for j in range(2 * NT):
                pe.wait_ge(place_ready, j + 1)
                T.matmul(ps[:, 7, 0:32], oh_place[:, j, 0:P], oh_block[:, j, :], start=j == 0, stop=j == 2 * NT - 1)
                last = T.matmul(ps[0:SB, 1, 0:32], oh_place[:, j, P:SLOTS], oh_block[:, j, :], start=j == 0, stop=j == 2 * NT - 1)
            last.then_inc(slots_ps, 1)

            def turn_rows(b):
                pe.wait_ge(gath_a, b * 16 + 16)
                for k in range(KT):
                    T.transpose(ps[:, 0, k * P:(k + 1) * P], grow[:, 0, k * P:(k + 1) * P], ident[:, :])
                pe.wait_ge(gath_b, b * 16 + 16)
                for k in range(KT):
                    last = T.transpose(ps[:, 1, k * SB:(k + 1) * SB], grow[0:SB, 1, k * P:(k + 1) * P], ident[0:SB, 0:SB])
                last.then_inc(g_trans, 1)

            pe.wait_ge(blocks_ready, 1)
            n_blocks = pe.value_load(block_expert[0:1, 33:34], min_val=X, max_val=BMAX)
            turn_rows(0)
            def expert(b, width):
                parts = [(6, 0, P), (7, P, width - P)][:1 + (width > P)]
                pe.wait_ge(xT_done, b + 1)
                for m in range(MT):
                    half, col = divmod(m * P, HM)
                    if col == 0:
                        done = FIRST[:2 * half + 2]
                        pe.wait_ge(prep_act, b * len(EACH) + len(done))
                        pe.wait_ge(prep_dve, b * count(EACH, BY_DVE) + len(done))
                        pe.wait_ge(prep_pool, b * count(EACH, BY_POOL) + count(done, BY_POOL) + 1)
                    pe.wait_ge(h_done, b * MT + m + 1)
                    for mat, bank in ((0, 2), (1, 4)):
                        for k in range(KT):
                            cols = slice(k * HM + col, k * HM + col + P)
                            for w, a in ((w_r, xT_r), (w_b, xT_l), (w_l, xT_b)):
                                last = T.matmul(ps[:, bank + m % 2, 0:width], w[:, mat, half, cols], a[:, k, 0:width],
                                                start=k == 0 and w is w_r, stop=k == KT - 1 and w is w_l)
                    last.then_inc(gu_ps, 1)
                turn_rows(b + 1)
                pe.wait_ge(yb_done, b * 2 + 2)
                for m in range(MT):
                    half, j = divmod(m, MT // 2)
                    if j == 0:
                        done = FIRST + EACH[:half + 1]
                        pe.wait_ge(prep_act, b * len(EACH) + len(done))
                        pe.wait_ge(prep_pool, b * count(EACH, BY_POOL) + count(done, BY_POOL) + 1)
                    pe.wait_ge(h_split, b * MT + m + 1)
                    for bank, lo, n in parts:
                        for h, w in ((hT_r, w_r), (hT_l, w_r), (hT_b, w_l)):
                            last = T.matmul(ps[0:n, bank, :], h[:, m, lo:lo + n], w[:, 2, half, j * D:(j + 1) * D],
                                            start=m == 0 and h is hT_r, stop=m == MT - 1 and h is hT_b)
                    if m == MT // 2 - 1:
                        last.then_inc(wo_used, 1)
                last.then_inc(yb_ps, 1)

            pe.wait_ge(tokens_known, 1)
            with pe.Fori(0, n_blocks) as b:
                tokens = pe.value_load(block_tokens[0:1, bass.ds(b, 1)], min_val=0, max_val=SLOTS)
                with pe.If(tokens > 160):
                    with pe.If(tokens > 192):
                        expert(b, SLOTS)
                    with pe.Else():
                        expert(b, 192)
                with pe.Else():
                    with pe.If(tokens > P):
                        expert(b, 160)
                    with pe.Else():
                        expert(b, P)


INPUTS = ["x", "src", "dst", "L0_gnn_W1", "L0_gnn_b1", "L0_gnn_W2", "L0_gnn_b2",
          "L0_ffn_wg", "L0_ffn_w0", "L0_ffn_w1", "L0_ffn_wo"]


def kernel(**inputs):
    import numpy as np
    import concourse.bacc as bacc
    from concourse.bass_utils import run_bass_kernel_spmd

    nc = bacc.Bacc("TRN2", target_bir_lowering=False, num_devices=1)
    arrays, args = {}, []
    for name in INPUTS:
        a = np.ascontiguousarray(inputs[name])
        arrays[f"in_{name}"] = a
        args.append(nc.dram_tensor(f"in_{name}", a.shape, mybir.dt.from_np(a.dtype), kind="ExternalInput").ap())
    out = nc.dram_tensor("out", arrays["in_x"].shape, F32, kind="ExternalOutput").ap()
    gnn_moe_kernel(nc, *args, out)
    result = run_bass_kernel_spmd(nc, [arrays], core_ids=[0])
    return result.results[0]["out"]
```
